# Optimizing a Trainium2 kernel written in Bass

```python
import numpy as np
import jax
import jax.numpy as jnp

def _softmax(x, axis=-1):
    return jax.nn.softmax(x, axis=axis)

def _gelu(x):
    return jax.nn.gelu(x, approximate=True)

def _silu(x):
    return jax.nn.silu(x)

def _sigmoid(x):
    return jax.nn.sigmoid(x)

def _layernorm(x, axis=-1, eps=1e-05):
    m = jnp.mean(x, axis=axis, keepdims=True)
    v = jnp.var(x, axis=axis, keepdims=True)
    return (x - m) / jnp.sqrt(v + eps)

def _scatter_add(tgt, idx, src, axis=0):
    return tgt.at[idx].add(src)

def _segment_sum(src, seg, n):
    return jax.ops.segment_sum(src, seg, n)
kernel_name = 'mk_seq_postln_d4_jaxref_r8_f677e8'

def setup_inputs(seed: int=0):
    np.random.seed(seed)
    _w = jnp.asarray

    def _L0_attn_setup():
        import jax, jax.numpy as jnp
        import numpy as np
        H, HD, D = (16, 64, 128)
        SCALE = HD ** (-0.5)
        TEMP = 1.0
        EPS = 1e-05
        key = jax.random.key(seed)
        ks = jax.random.split(key, 10)
        B, N = (2, 256)
        lim = 1.0 / np.sqrt(D)

        def lin(k, out_d, in_d):
            k1, k2 = jax.random.split(k)
            W = jax.random.uniform(k1, (out_d, in_d), jnp.float32, -lim, lim)
            b = jax.random.uniform(k2, (out_d,), jnp.float32, -lim, lim)
            return (W, b)
        Wq, bq = lin(ks[0], H * HD, D)
        Wk, bk = lin(ks[1], H * HD, D)
        Wv, bv = lin(ks[2], H * HD, D)
        Wo, bo = lin(ks[3], D, H * HD)
        return {'x': jax.random.normal(ks[4], (B, N, D), jnp.float32), 'adaptive_scale': jnp.ones((H,), jnp.float32), 'Wq': Wq, 'bq': bq, 'Wk': Wk, 'bk': bk, 'Wv': Wv, 'bv': bv, 'Wo': Wo, 'bo': bo, 'gamma': jnp.ones((D,), jnp.float32), 'beta': jnp.zeros((D,), jnp.float32)}
    _L0_attn_in = _L0_attn_setup()

    def _L0_ffn_setup():
        import jax, jax.numpy as jnp
        import numpy as np
        B, S, D = (4, 256, 128)
        E = 8
        DFF = 512
        CAP_FACTOR = 1.25
        key = jax.random.key(seed)
        ks = jax.random.split(key, 4)
        std_gate = float(np.sqrt(0.1 / D))
        inputs = jax.random.normal(ks[0], (B, S, D), dtype=jnp.float32)
        gate_w = jax.random.normal(ks[1], (E, D), dtype=jnp.float32) * std_gate
        w1 = jax.random.normal(ks[2], (E, D, DFF), dtype=jnp.float32) * (1.0 / np.sqrt(D))
        b1 = jnp.zeros((E, DFF), dtype=jnp.float32)
        w2 = jax.random.normal(ks[3], (E, DFF, D), dtype=jnp.float32) * (1.0 / np.sqrt(DFF))
        b2 = jnp.zeros((E, D), dtype=jnp.float32)
        return {'inputs': inputs, 'gate_w': gate_w, 'w1': w1, 'b1': b1, 'w2': w2, 'b2': b2}
    _L0_ffn_in = _L0_ffn_setup()

    def _L1_attn_setup():
        import jax, jax.numpy as jnp
        import numpy as np
        NUM_HEADS = 16

        def _heads(t, B, N, H, hd):
            return t.reshape(B, N, H, hd).transpose(0, 2, 1, 3)
        key = jax.random.key(seed)
        ks = jax.random.split(key, 9)
        B, N, D = (2, 256, 128)
        w = 0.02
        return {'x': jax.random.normal(ks[0], (B, N, D), dtype=jnp.float32), 'wq': jax.random.normal(ks[1], (D, D), dtype=jnp.float32) * w, 'bq': jax.random.normal(ks[2], (D,), dtype=jnp.float32) * w, 'wk': jax.random.normal(ks[3], (D, D), dtype=jnp.float32) * w, 'bk': jax.random.normal(ks[4], (D,), dtype=jnp.float32) * w, 'wv': jax.random.normal(ks[5], (D, D), dtype=jnp.float32) * w, 'bv': jax.random.normal(ks[6], (D,), dtype=jnp.float32) * w, 'wo': jax.random.normal(ks[7], (D, D), dtype=jnp.float32) * w, 'bo': jax.random.normal(ks[8], (D,), dtype=jnp.float32) * w}
    _L1_attn_in = _L1_attn_setup()

    def _L1_ffn_setup():
        import jax, jax.numpy as jnp
        import numpy as np
        TOP_K = 2
        key = jax.random.key(seed)
        ks = jax.random.split(key, 5)
        B, S, H, I, E = (4, 256, 128, 512, 8)
        scale_hi = (2.0 / (H + I)) ** 0.5
        scale_he = (2.0 / (H + E)) ** 0.5
        return {'x': jax.random.normal(ks[0], (B, S, H), dtype=jnp.float32), 'router_w': jax.random.normal(ks[1], (E, H), dtype=jnp.float32) * scale_he, 'gate_w': jax.random.normal(ks[2], (E, I, H), dtype=jnp.float32) * scale_hi, 'up_w': jax.random.normal(ks[3], (E, I, H), dtype=jnp.float32) * scale_hi, 'down_w': jax.random.normal(ks[4], (E, H, I), dtype=jnp.float32) * scale_hi}
    _L1_ffn_in = _L1_ffn_setup()

    def _L2_attn_setup():
        import jax, jax.numpy as jnp
        import numpy as np
        DIM = 128
        NUM_HEADS = 16
        NUM_GROUPS = 8

        def grouped_linear(x, w, b):
            B, N, Cin = x.shape
            G = w.shape[0]
            xg = x.reshape(B, N, G, Cin // G)
            out = jnp.einsum('bngi,gio->bngo', xg, w)
            out = out.reshape(B, N, -1)
            if b is not None:
                out = out + b
            return out
        key = jax.random.key(seed)
        k1, k2, k3, k4 = jax.random.split(key, 4)
        G = NUM_GROUPS
        x = jax.random.normal(k1, (2, 256, DIM), dtype=jnp.float32)
        w_qkv = jax.random.normal(k2, (G, DIM // G, 3 * DIM // G), dtype=jnp.float32) * (DIM // G) ** (-0.5)
        w_proj = jax.random.normal(k3, (G, DIM // G, DIM // G), dtype=jnp.float32) * (DIM // G) ** (-0.5)
        b_proj = jax.random.normal(k4, (DIM,), dtype=jnp.float32) * 0.02
        return {'x': x, 'w_qkv': w_qkv, 'w_proj': w_proj, 'b_proj': b_proj}
    _L2_attn_in = _L2_attn_setup()

    def _L2_ffn_setup():
        import jax, jax.numpy as jnp
        import numpy as np
        import math
        D_IN = 128
        FEATURES = (512, 512, 128)
        BATCH, SEQ = (8, 256)

        def _conn_dense(kernel_bool, x):
            w = jnp.where(kernel_bool, jnp.float32(1.0), jnp.float32(-1.0))
            return x @ w
        key = jax.random.key(seed)
        kx, kk0, kk1, kk2 = jax.random.split(key, 4)
        x = jax.random.normal(kx, (BATCH, SEQ, D_IN), dtype=jnp.float32)
        k0 = jax.random.randint(kk0, (2 * D_IN, FEATURES[0]), 0, 2).astype(jnp.bool_)
        k1 = jax.random.randint(kk1, (FEATURES[0], FEATURES[1]), 0, 2).astype(jnp.bool_)
        k2 = jax.random.randint(kk2, (FEATURES[1], FEATURES[2]), 0, 2).astype(jnp.bool_)
        s0 = jnp.asarray(1.0 / math.sqrt(2 * D_IN), dtype=jnp.float32)
        s1 = jnp.asarray(1.0 / math.sqrt(FEATURES[0]), dtype=jnp.float32)
        s2 = jnp.asarray(1.0 / math.sqrt(FEATURES[1]), dtype=jnp.float32)
        return {'x': x, 'k0': k0, 'k1': k1, 'k2': k2, 's0': s0, 's1': s1, 's2': s2}
    _L2_ffn_in = _L2_ffn_setup()

    def _L3_attn_setup():
        import jax, jax.numpy as jnp
        import numpy as np
        N_EMBD = 128
        N_HEAD = 16
        SEQ = 256
        BATCH = 2
        NEG = -1000000000.0
        key = jax.random.key(seed)
        k0, k1, k2 = jax.random.split(key, 3)
        return {'hidden_states': jax.random.normal(k0, (BATCH, SEQ, N_EMBD), dtype=jnp.float32), 'w_attn': jax.random.normal(k1, (3 * N_EMBD, N_EMBD), dtype=jnp.float32) * 0.02, 'b_attn': jnp.zeros((3 * N_EMBD,), dtype=jnp.float32), 'w_proj': jax.random.normal(k2, (N_EMBD, N_EMBD), dtype=jnp.float32) * 0.02, 'b_proj': jnp.zeros((N_EMBD,), dtype=jnp.float32)}
    _L3_attn_in = _L3_attn_setup()

    def _L3_ffn_setup():
        import jax, jax.numpy as jnp
        import numpy as np
        import math
        B, T, C = (4, 256, 128)
        E, K = (8, 2)
        EH, SH = (256, 512)
        CAP_FACTOR = 1.25
        SCALING = 1.0
        FC_MULT = 1.0

        def _capacity(N, k):
            avg = math.ceil(N * k / E)
            return max(int(math.ceil(avg * CAP_FACTOR)), 1)
        key = jax.random.key(seed)
        ks = jax.random.split(key, 6)
        sd = 0.02
        return {'x': jax.random.normal(ks[0], (B, T, C), jnp.float32), 'proj_w': jax.random.normal(ks[1], (E, C), jnp.float32) * sd, 'proj_b': jnp.zeros((E,), jnp.float32), 'expert_bias': jnp.zeros((E,), jnp.float32), 'fc1_w': jax.random.normal(ks[2], (E, EH, C), jnp.float32) * sd, 'fc1_b': jnp.zeros((E, EH), jnp.float32), 'fc2_w': jax.random.normal(ks[3], (E, C, EH), jnp.float32) * sd, 'fc2_b': jnp.zeros((E, C), jnp.float32), 'sh1_w': jax.random.normal(ks[4], (SH, C), jnp.float32) * sd, 'sh1_b': jnp.zeros((SH,), jnp.float32), 'sh2_w': jax.random.normal(ks[5], (C, SH), jnp.float32) * sd, 'sh2_b': jnp.zeros((C,), jnp.float32)}
    _L3_ffn_in = _L3_ffn_setup()
    _d = {'L0_attn_x': _L0_attn_in['x'], 'L0_attn_adaptive_scale': _L0_attn_in['adaptive_scale'], 'L0_attn_Wq': _L0_attn_in['Wq'], 'L0_attn_bq': _L0_attn_in['bq'], 'L0_attn_Wk': _L0_attn_in['Wk'], 'L0_attn_bk': _L0_attn_in['bk'], 'L0_attn_Wv': _L0_attn_in['Wv'], 'L0_attn_bv': _L0_attn_in['bv'], 'L0_attn_Wo': _L0_attn_in['Wo'], 'L0_attn_bo': _L0_attn_in['bo'], 'L0_attn_gamma': _L0_attn_in['gamma'], 'L0_attn_beta': _L0_attn_in['beta'], 'L0_ffn_gate_w': _L0_ffn_in['gate_w'], 'L0_ffn_w1': _L0_ffn_in['w1'], 'L0_ffn_b1': _L0_ffn_in['b1'], 'L0_ffn_w2': _L0_ffn_in['w2'], 'L0_ffn_b2': _L0_ffn_in['b2'], 'L1_attn_wq': _L1_attn_in['wq'], 'L1_attn_bq': _L1_attn_in['bq'], 'L1_attn_wk': _L1_attn_in['wk'], 'L1_attn_bk': _L1_attn_in['bk'], 'L1_attn_wv': _L1_attn_in['wv'], 'L1_attn_bv': _L1_attn_in['bv'], 'L1_attn_wo': _L1_attn_in['wo'], 'L1_attn_bo': _L1_attn_in['bo'], 'L1_ffn_router_w': _L1_ffn_in['router_w'], 'L1_ffn_gate_w': _L1_ffn_in['gate_w'], 'L1_ffn_up_w': _L1_ffn_in['up_w'], 'L1_ffn_down_w': _L1_ffn_in['down_w'], 'L2_attn_w_qkv': _L2_attn_in['w_qkv'], 'L2_attn_w_proj': _L2_attn_in['w_proj'], 'L2_attn_b_proj': _L2_attn_in['b_proj'], 'L2_ffn_k0': _L2_ffn_in['k0'], 'L2_ffn_k1': _L2_ffn_in['k1'], 'L2_ffn_k2': _L2_ffn_in['k2'], 'L2_ffn_s0': _L2_ffn_in['s0'], 'L2_ffn_s1': _L2_ffn_in['s1'], 'L2_ffn_s2': _L2_ffn_in['s2'], 'L3_attn_w_attn': _L3_attn_in['w_attn'], 'L3_attn_b_attn': _L3_attn_in['b_attn'], 'L3_attn_w_proj': _L3_attn_in['w_proj'], 'L3_attn_b_proj': _L3_attn_in['b_proj'], 'L3_ffn_proj_w': _L3_ffn_in['proj_w'], 'L3_ffn_proj_b': _L3_ffn_in['proj_b'], 'L3_ffn_expert_bias': _L3_ffn_in['expert_bias'], 'L3_ffn_fc1_w': _L3_ffn_in['fc1_w'], 'L3_ffn_fc1_b': _L3_ffn_in['fc1_b'], 'L3_ffn_fc2_w': _L3_ffn_in['fc2_w'], 'L3_ffn_fc2_b': _L3_ffn_in['fc2_b'], 'L3_ffn_sh1_w': _L3_ffn_in['sh1_w'], 'L3_ffn_sh1_b': _L3_ffn_in['sh1_b'], 'L3_ffn_sh2_w': _L3_ffn_in['sh2_w'], 'L3_ffn_sh2_b': _L3_ffn_in['sh2_b']}
    _x0 = _d['L0_attn_x']
    _d['L0_attn_x'] = jax.random.normal(jax.random.fold_in(jax.random.key(seed), 1), (16, 256, 128), dtype=_x0.dtype)
    del _x0
    return _d

def reference(L0_attn_x, L0_attn_adaptive_scale, L0_attn_Wq, L0_attn_bq, L0_attn_Wk, L0_attn_bk, L0_attn_Wv, L0_attn_bv, L0_attn_Wo, L0_attn_bo, L0_attn_gamma, L0_attn_beta, L0_ffn_gate_w, L0_ffn_w1, L0_ffn_b1, L0_ffn_w2, L0_ffn_b2, L1_attn_wq, L1_attn_bq, L1_attn_wk, L1_attn_bk, L1_attn_wv, L1_attn_bv, L1_attn_wo, L1_attn_bo, L1_ffn_router_w, L1_ffn_gate_w, L1_ffn_up_w, L1_ffn_down_w, L2_attn_w_qkv, L2_attn_w_proj, L2_attn_b_proj, L2_ffn_k0, L2_ffn_k1, L2_ffn_k2, L2_ffn_s0, L2_ffn_s1, L2_ffn_s2, L3_attn_w_attn, L3_attn_b_attn, L3_attn_w_proj, L3_attn_b_proj, L3_ffn_proj_w, L3_ffn_proj_b, L3_ffn_expert_bias, L3_ffn_fc1_w, L3_ffn_fc1_b, L3_ffn_fc2_w, L3_ffn_fc2_b, L3_ffn_sh1_w, L3_ffn_sh1_b, L3_ffn_sh2_w, L3_ffn_sh2_b):

    def _L0_attn_ref(x, adaptive_scale, Wq, bq, Wk, bk, Wv, bv, Wo, bo, gamma, beta):
        import jax, jax.numpy as jnp
        import numpy as np
        H, HD, D = (16, 64, 128)
        SCALE = HD ** (-0.5)
        TEMP = 1.0
        EPS = 1e-05
        B, N, _ = x.shape
        Q = (x @ Wq.T + bq).reshape(B, N, H, HD)
        K = (x @ Wk.T + bk).reshape(B, N, H, HD)
        V = (x @ Wv.T + bv).reshape(B, N, H, HD)
        scores = jnp.einsum('bnhd,bmhd->bhnm', Q, K)
        scores = scores * (SCALE * adaptive_scale)[None, :, None, None] / TEMP
        w = jax.nn.softmax(scores, axis=-1)
        attn = jnp.einsum('bhnm,bmhd->bnhd', w, V).reshape(B, N, H * HD)
        y = x + (attn @ Wo.T + bo)
        mu = jnp.mean(y, axis=-1, keepdims=True)
        var = jnp.var(y, axis=-1, keepdims=True)
        return (y - mu) / jnp.sqrt(var + EPS) * gamma + beta

    def _L0_ffn_ref(inputs, gate_w, w1, b1, w2, b2):
        import jax, jax.numpy as jnp
        import numpy as np
        B, S, D = (4, 256, 128)
        E = 8
        DFF = 512
        CAP_FACTOR = 1.25
        d_model = inputs.shape[-1]
        tokens = inputs.reshape(-1, d_model)
        T = tokens.shape[0]
        num_experts = gate_w.shape[0]
        capacity = int(np.ceil(CAP_FACTOR * T / num_experts))
        logits = jnp.einsum('td,ed->te', tokens.astype(jnp.float32), gate_w)
        probs = jax.nn.softmax(logits, axis=-1)
        expert_idx = jnp.argmax(probs, axis=-1)
        mask = jax.nn.one_hot(expert_idx, num_experts, dtype=jnp.float32)
        ranks = jnp.cumsum(mask, axis=0) - 1.0
        keep = (ranks < capacity) * mask
        pos = ranks.astype(jnp.int32)
        sec_mask = jax.nn.one_hot(pos, capacity, dtype=jnp.float32) * keep[:, :, None]
        combine_weights = probs[:, :, None] * sec_mask
        dispatch = jnp.einsum('tec,td->ecd', sec_mask, tokens)
        h = jax.nn.relu(jnp.einsum('ecd,edh->ech', dispatch, w1) + b1[:, None, :])
        expert_out = jnp.einsum('ech,ehd->ecd', h, w2) + b2[:, None, :]
        ans = jnp.einsum('tec,ecd->td', combine_weights, expert_out)
        return ans.reshape(inputs.shape)

    def _L1_attn_ref(x, wq, bq, wk, bk, wv, bv, wo, bo):
        import jax, jax.numpy as jnp
        import numpy as np
        NUM_HEADS = 16

        def _heads(t, B, N, H, hd):
            return t.reshape(B, N, H, hd).transpose(0, 2, 1, 3)
        B, N, D = x.shape
        H = NUM_HEADS
        hd = D // H
        q = _heads(x @ wq.T + bq, B, N, H, hd)
        k = _heads(x @ wk.T + bk, B, N, H, hd)
        v = _heads(x @ wv.T + bv, B, N, H, hd)
        q2 = jnp.sum(q * q, axis=-1)
        k2 = jnp.sum(k * k, axis=-1)
        qk = jnp.einsum('bhid,bhjd->bhij', q, k)
        d2 = jnp.maximum(q2[..., :, None] + k2[..., None, :] - 2.0 * qk, 1e-12)
        attn = jax.nn.softmax(-jnp.sqrt(d2), axis=-1)
        out = jnp.einsum('bhij,bhjd->bhid', attn, v)
        out = out.transpose(0, 2, 1, 3).reshape(B, N, D)
        return out @ wo.T + bo

    def _L1_ffn_ref(x, router_w, gate_w, up_w, down_w):
        import jax, jax.numpy as jnp
        import numpy as np
        TOP_K = 2
        B, S, H = x.shape
        E = router_w.shape[0]
        xf = x.reshape(-1, H)
        logits = xf @ router_w.T
        probs = jax.nn.softmax(logits, axis=-1)
        topk_p, topk_i = jax.lax.top_k(probs, TOP_K)
        topk_p = topk_p / topk_p.sum(axis=-1, keepdims=True)

        def body(out, inputs):
            e, gw, uw, dw = inputs
            sel = topk_i == e
            mask = sel.any(axis=-1)
            w_tok = (topk_p * sel).sum(axis=-1)
            cnt = mask.sum().astype(xf.dtype)
            mean_w = jnp.where(cnt > 0, w_tok.sum() / jnp.maximum(cnt, 1.0), 0.0)
            h = jax.nn.silu(xf @ gw.T) * (xf @ uw.T)
            eo = h @ dw.T
            out = out + mask[:, None].astype(xf.dtype) * eo * mean_w
            return (out, None)
        out0 = jnp.zeros_like(xf)
        out, _ = jax.lax.scan(body, out0, (jnp.arange(E), gate_w, up_w, down_w))
        return out.reshape(B, S, H)

    def _L2_attn_ref(x, w_qkv, w_proj, b_proj):
        import jax, jax.numpy as jnp
        import numpy as np
        DIM = 128
        NUM_HEADS = 16
        NUM_GROUPS = 8

        def grouped_linear(x, w, b):
            B, N, Cin = x.shape
            G = w.shape[0]
            xg = x.reshape(B, N, G, Cin // G)
            out = jnp.einsum('bngi,gio->bngo', xg, w)
            out = out.reshape(B, N, -1)
            if b is not None:
                out = out + b
            return out
        B, N, C = x.shape
        H = NUM_HEADS
        D = C // H
        scale = D ** (-0.5)
        qkv = grouped_linear(x, w_qkv, None)
        qkv = qkv.reshape(B, N, 3, H, D)
        qkv = jnp.transpose(qkv, (2, 0, 3, 1, 4))
        q, k, v = (qkv[0] * scale, qkv[1], qkv[2])
        attn = jnp.einsum('bhnd,bhmd->bhnm', q, k)
        attn = jax.nn.softmax(attn, axis=-1)
        out = jnp.einsum('bhnm,bhmd->bhnd', attn, v)
        out = jnp.transpose(out, (0, 2, 1, 3)).reshape(B, N, C)
        out = grouped_linear(out, w_proj, b_proj)
        return out

    def _L2_ffn_ref(x, k0, k1, k2, s0, s1, s2):
        import jax, jax.numpy as jnp
        import numpy as np
        import math
        D_IN = 128
        FEATURES = (512, 512, 128)
        BATCH, SEQ = (8, 256)

        def _conn_dense(kernel_bool, x):
            w = jnp.where(kernel_bool, jnp.float32(1.0), jnp.float32(-1.0))
            return x @ w
        h = jnp.concatenate([x, -x], axis=-1)
        h = s0 * _conn_dense(k0, h)
        h = jax.nn.relu(h) * 2
        h = s1 * _conn_dense(k1, h)
        h = jax.nn.relu(h) * 2
        h = s2 * _conn_dense(k2, h)
        return h

    def _L3_attn_ref(hidden_states, w_attn, b_attn, w_proj, b_proj):
        import jax, jax.numpy as jnp
        import numpy as np
        N_EMBD = 128
        N_HEAD = 16
        SEQ = 256
        BATCH = 2
        NEG = -1000000000.0
        B, S, E = hidden_states.shape
        H = N_HEAD
        D = E // H
        qkv = hidden_states @ w_attn.T + b_attn
        q, k, v = jnp.split(qkv, 3, axis=-1)
        split = lambda t: t.reshape(B, S, H, D).transpose(0, 2, 1, 3)
        q, k, v = (split(q), split(k), split(v))
        w = jnp.einsum('bhnd,bhmd->bhnm', q, k) * jax.lax.rsqrt(float(D))
        mask = jnp.tril(jnp.ones((S, S), dtype=jnp.float32))
        w = jnp.where(mask > 0, w, NEG)
        w = jax.nn.softmax(w, axis=-1)
        attn = jnp.einsum('bhnm,bhmd->bhnd', w, v)
        attn = attn.transpose(0, 2, 1, 3).reshape(B, S, E)
        return attn @ w_proj.T + b_proj

    def _L3_ffn_ref(x, proj_w, proj_b, expert_bias, fc1_w, fc1_b, fc2_w, fc2_b, sh1_w, sh1_b, sh2_w, sh2_b):
        import jax, jax.numpy as jnp
        import numpy as np
        import math
        B, T, C = (4, 256, 128)
        E, K = (8, 2)
        EH, SH = (256, 512)
        CAP_FACTOR = 1.25
        SCALING = 1.0
        FC_MULT = 1.0

        def _capacity(N, k):
            avg = math.ceil(N * k / E)
            return max(int(math.ceil(avg * CAP_FACTOR)), 1)
        Bx, Tx, Cx = x.shape
        N = Bx * Tx
        xf = x.reshape(N, Cx)
        z = xf @ proj_w.T + proj_b
        s = jax.nn.sigmoid(z) + expert_bias
        logits = jnp.log(jnp.clip(s, 1e-12)) * SCALING
        probs = jax.nn.softmax(logits, axis=-1)
        topk_w, topk_idx = jax.lax.top_k(probs, K)
        topk_w = topk_w / jnp.clip(topk_w.sum(-1, keepdims=True), 1e-12)
        pair_e = topk_idx.reshape(-1)
        pair_w = topk_w.reshape(-1)
        pair_tok = jnp.repeat(jnp.arange(N), K)
        cap = _capacity(N, K)
        assigned = pair_e[None, :] == jnp.arange(E)[:, None]
        wmat = jnp.where(assigned, pair_w[None, :], -jnp.inf)
        kept_w, kept_pair = jax.lax.top_k(wmat, cap)
        valid = kept_w > -jnp.inf
        kept_w = jnp.where(valid, kept_w, 0.0)
        kept_tok = pair_tok[kept_pair]
        xe = xf[kept_tok]
        h = jax.nn.gelu(jnp.einsum('ecd,ehd->ech', xe, fc1_w) + fc1_b[:, None, :], approximate=False)
        oe = jnp.einsum('ech,edh->ecd', h, fc2_w) + fc2_b[:, None, :]
        contrib = oe * kept_w[..., None]
        y = jnp.zeros((N, Cx), x.dtype).at[kept_tok.reshape(-1)].add(contrib.reshape(-1, Cx))
        sh = jax.nn.gelu(xf @ sh1_w.T + sh1_b, approximate=False) @ sh2_w.T + sh2_b
        return ((sh + y) * FC_MULT).reshape(Bx, Tx, Cx)
    x = L0_attn_x
    x = _layernorm(x + _L0_attn_ref(x, L0_attn_adaptive_scale, L0_attn_Wq, L0_attn_bq, L0_attn_Wk, L0_attn_bk, L0_attn_Wv, L0_attn_bv, L0_attn_Wo, L0_attn_bo, L0_attn_gamma, L0_attn_beta), axis=-1)
    x = _layernorm(x + _L0_ffn_ref(x, L0_ffn_gate_w, L0_ffn_w1, L0_ffn_b1, L0_ffn_w2, L0_ffn_b2), axis=-1)
    x = _layernorm(x + _L1_attn_ref(x, L1_attn_wq, L1_attn_bq, L1_attn_wk, L1_attn_bk, L1_attn_wv, L1_attn_bv, L1_attn_wo, L1_attn_bo), axis=-1)
    x = _layernorm(x + _L1_ffn_ref(x, L1_ffn_router_w, L1_ffn_gate_w, L1_ffn_up_w, L1_ffn_down_w), axis=-1)
    x = _layernorm(x + _L2_attn_ref(x, L2_attn_w_qkv, L2_attn_w_proj, L2_attn_b_proj), axis=-1)
    x = _layernorm(x + _L2_ffn_ref(x, L2_ffn_k0, L2_ffn_k1, L2_ffn_k2, L2_ffn_s0, L2_ffn_s1, L2_ffn_s2), axis=-1)
    x = _layernorm(x + _L3_attn_ref(x, L3_attn_w_attn, L3_attn_b_attn, L3_attn_w_proj, L3_attn_b_proj), axis=-1)
    x = _layernorm(x + _L3_ffn_ref(x, L3_ffn_proj_w, L3_ffn_proj_b, L3_ffn_expert_bias, L3_ffn_fc1_w, L3_ffn_fc1_b, L3_ffn_fc2_w, L3_ffn_fc2_b, L3_ffn_sh1_w, L3_ffn_sh1_b, L3_ffn_sh2_w, L3_ffn_sh2_b), axis=-1)
    return x

_drawn_inputs = setup_inputs


def setup_inputs(seed=0):
    import zlib

    import numpy as np

    out = dict(_drawn_inputs(seed))
    spreads = {'L0_attn_adaptive_scale': (1.0, 0.6),
     'L0_attn_gamma': (1.0, 0.2),
     'L0_attn_beta': (0.0, 0.1),
     'L0_ffn_b1': (0.0, 0.271),
     'L0_ffn_b2': (0.0, 0.1),
     'L3_attn_b_attn': (0.0, 0.315),
     'L3_attn_b_proj': (0.0, 0.1),
     'L3_ffn_proj_b': (0.0, 0.575),
     'L3_ffn_expert_bias': (0.0, 0.1),
     'L3_ffn_fc1_b': (0.0, 0.8),
     'L3_ffn_fc2_b': (0.0, 0.1),
     'L3_ffn_sh1_b': (0.0, 0.322),
     'L3_ffn_sh2_b': (0.0, 0.1)}
    factors = {'L0_attn_bq': 4.92,
     'L0_attn_bk': 8.0,
     'L1_attn_wq': 8.0,
     'L1_attn_bq': 8.0,
     'L1_attn_wk': 8.0,
     'L1_attn_bk': 8.0,
     'L1_attn_wv': 4.008,
     'L1_attn_bv': 4.664,
     'L1_attn_wo': 3.891,
     'L2_attn_b_proj': 2.721,
     'L3_ffn_fc1_w': 3.577,
     'L3_ffn_fc2_w': 3.342}
    for name, (base, spread) in spreads.items():
        noise = np.random.default_rng([zlib.crc32(name.encode()), seed]).standard_normal(out[name].shape)
        drawn = base * np.exp(spread * noise) if base else spread * noise
        out[name] = jnp.asarray(drawn.astype(out[name].dtype))
    for name, factor in factors.items():
        out[name] = (out[name] * factor).astype(out[name].dtype)
    return out
```

```python
from contextlib import ExitStack
import concourse.bass as bass
from concourse import mybir

F32 = mybir.dt.float32
BF16 = mybir.dt.bfloat16
U8 = mybir.dt.uint8
I32 = mybir.dt.int32
ALU = mybir.AluOpType
ACT = mybir.ActivationFunctionType
AX = mybir.AxisListType
P = 128
H = 16
NB, SEQ = 16, 256
TB = SEQ // P
NT = NB * TB
PARTS = 3
EPS = 1e-5
E = 8
AHEAD = 3
CAPACITY = {0: -(-5 * NT * P // (4 * E)), 3: -(-5 * (-(-NT * P * 2 // E)) // 4)}


class Signal:

    def __init__(self, nc, name, per, ahead=AHEAD):
        self.sem, self.per, self.ahead = nc.alloc_semaphore(name), per, ahead

    def open(self, engine):
        engine.sem_inc(self.sem, self.ahead * self.per)

    def at(self, batch, k=None):
        return (batch + self.ahead) * self.per + (self.per if k is None else k + 1)


SIX = [1, 4, 7, 10, 12, 15]
PLANS = {
    "wide": dict(ring=4, lags=(0, 0, 0, 1, 3, 3, 5, 6, 8, 4), slots=(0, 1, 4), by_scalar=SIX),
    "dist": dict(ring=8, lags=(0, 1, 2, 4, 6, 6, 8, 9, 12, 2), slots=(0, 2, 9), by_scalar=[]),
    "plain": dict(ring=8, lags=(0, 0, 0, 3, 5, 5, 7, 8, 11, 2), slots=(0, 2, 8), by_scalar=SIX),
    "causal": dict(ring=8, lags=(0, 0, 0, 3, 5, 5, 7, 8, 11, 2), slots=(0, 2, 8), by_scalar=SIX),
}
BODY = 2


def attention(nc, name, kind, x_state, consts, w, scratch=None, scale=None):
    dist, causal = kind == "dist", kind == "causal"
    wide = kind == "wide"
    HD = 64 if wide else P // H
    NG = H * HD // P if wide else 4
    HG = H // NG
    CROSS = PARTS * PARTS * HD
    KR = CROSS + (2 * PARTS if dist else 0)
    plan = PLANS[kind]
    RING = plan["ring"]
    LAG_M, LAG_R, LAG_E, LAG_N, LAG_T, LAG_K, LAG_PV, LAG_O, LAG_OUT, LAG_W = plan["lags"]
    SLOT_XT, SLOT_QK, SLOT_V = plan["slots"]
    per_e = {"v": [h for h in range(H) if h not in plan["by_scalar"]], "a": plan["by_scalar"]}
    bank = [h % 2 for h in range(H)] if wide else [h % 3 for h in range(H - 1)] + [1]
    bank_last = {h: next(d for d in range(1, H) if bank[(h - d) % H] == bank[h]) for h in range(H)}
    evac_by = {h: e for e in per_e for h in per_e[e]}

    with ExitStack() as ctx:
        def sb(n, shape, dt=F32):
            return ctx.enter_context(nc.sbuf_tensor(f"{name}_{n}", shape, dt))

        def ps(n, shape, dt=F32):
            return ctx.enter_context(nc.psum_tensor(f"{name}_{n}", shape, dt))

        def sig(n, per):
            return Signal(nc, f"{name}_{n}", per)

        NQ = NG if wide else 1
        wqk, wv, wo = sb("wqk", [P, 2, NQ, P]), sb("wv", [P, NQ * P]), sb("wo", [P, NG, P])
        bqk = sb("bqk", [P, 2, NQ])
        bv, bo = sb("bv", [P, NQ * P]), sb("bo", [P, P])
        xs, xb, xT = sb("xs", [P, TB, P]), sb("xb", [P, TB, P]), sb("xT", [P, SEQ])
        if wide:
            QT, KT = sb("QT", [P, 2, NG, SEQ]), sb("KT", [P, 2, H, SEQ])
            V = sb("V", [P, 2, TB, H * HD])
            hscale, bqs = sb("hscale", [P, NG]), sb("bqs", [P, NG])
            gamma, beta = sb("gamma", [P, P]), sb("beta", [P, P])
            xbeta, z = sb("xbeta", [P, TB, P]), sb("z", [P, TB, P])
        else:
            qk, rest = sb("qk", [P, 2 * SEQ]), sb("rest", [P, 2 * SEQ])
            parts = sb("parts", [P, PARTS, 2 * SEQ], BF16)
            QS, KS = sb("QS", [P, 2, H, SEQ], BF16), sb("KS", [P, 2, H, SEQ], BF16)
            v32 = sb("v32", [P, 2, TB, H, 32])
        prob, probT = sb("prob", [P, RING, TB, SEQ]), sb("probT", [P, RING, TB, SEQ])
        nmax, rsum, rinv = sb("nmax", [P, RING, TB]), sb("rsum", [P, RING, TB]), sb("rinv", [P, RING, TB])
        OT = sb("OT", [P, NG, SEQ])
        y, stats, mv = sb("y", [P, TB, P]), sb("stats", [P, TB, 6]), sb("mv", [P, TB, 2])
        veps, rstd, mhalf = sb("veps", [P, TB]), sb("rstd", [P, TB]), sb("mhalf", [P, TB])
        if dist:
            D = sb("D", [P, RING, TB * SEQ + TB])
            sq, hsum = sb("sq", [P, 2 * SEQ]), sb("hsum", [P, 2, H])
            n2, n2r = sb("n2", [H, 2 * SEQ]), sb("n2r", [H, 2 * SEQ])
            n2p = sb("n2p", [H, PARTS, 2 * SEQ], BF16)
        psS = [ps(f"S{i}", [P, TB, SEQ]) for i in range(max(bank) + 1)]
        psT = [ps(f"T{i}", [P, TB, SEQ]) for i in range(2)]
        psO, psM = [ps(f"O{i}", [P, SEQ]) for i in range(2)], ps("M", [P, 2, SEQ])
        psY = ps("Y", [P, SEQ])[:] if wide else psM[:, 1, :]

        n_stack = 2 * PARTS * PARTS + (2 if dist else 0)
        loaded = nc.alloc_semaphore(f"{name}_loaded")
        zeroed, filled = nc.alloc_semaphore(f"{name}_zeroed"), nc.alloc_semaphore(f"{name}_filled")
        passed = nc.alloc_semaphore(f"{name}_passed")
        xb_ready = sig("xb_ready", 1 + wide)
        xs_ready, xT_psum, xT_ready = sig("xs_ready", 1), sig("xT_psum", 1), sig("xT_ready", 1)
        qk_psum, qk_ready, v_psum, v_ready = sig("qk_psum", 1), sig("qk_ready", 2), sig("v_psum", 1), sig("v_ready", 1)
        split, stored, stacked = sig("split", 4), sig("stored", 16 * (2 if dist else 1)), sig("stacked", 16 * n_stack)
        scores, maxed, expd, sums_inv, normed = sig("scores", H), sig("maxed", H), sig("expd", H * TB), sig("sums_inv", H), sig("normed", H * TB)
        turned = sig("turned", H)
        turned_out = {e: sig(f"turned_{e}", max(len(per_e[e]), 1)) for e in per_e}
        weighed, o_out = sig("weighed", H), sig("o_out", NG)
        y_psum, y_steps, rstd_ready, x_done = sig("y_psum", 1), sig("y_steps", 6), sig("rstd_ready", 1), sig("x_done", TB)
        if wide:
            vw_psum, vw_out = sig("vw_psum", 2 * TB), sig("vw_out", 2 * TB)
            qk_out = {"a": sig("qk_out_a", NG // 2), "v": sig("qk_out_v", NG // 2)}
            qkw_psum = sig("qkw_psum", NG)
            z_steps, a_scaled = sig("z_steps", 8), sig("a_scaled", 1)
            rstd2_ready = sig("rstd2_ready", 1)
        if dist:
            squared, n2_psum, n2_split, logged, rooted = sig("squared", 1), sig("n2_psum", 1), sig("n2_split", 5), sig("logged", H), sig("rooted", H)
            clamped = sig("clamped", H * TB)

        with nc.Block() as block:
            loads = [(wqk[:], w["wqk"]), (wv[:], w["wv"]), (wo[:], w["wo"]), (bo[:], w["bo"].partition_broadcast(P))]
            if "bqk" in w:
                loads += [(bqk[:], w["bqk"]), (bv[:], w["bv"].partition_broadcast(P))]
            if dist:
                loads += [(hsum[:], w["hsum"])]
            if wide:
                loads += [(hscale[:], w["adaptive"]), (gamma[:], w["gamma"].partition_broadcast(P)),
                          (beta[:], w["beta"].partition_broadcast(P))]

            @block.sync
            def _(sp):
                for dst, src in loads:
                    sp.dma_start(dst, src).then_inc(loaded, 16)
                sp.wait_ge(loaded, 16 * len(loads))

            @block.gpsimd
            def _(pool):
                nc.gpsimd.memset(KT[:] if wide else v32[:], 0.0).then_inc(zeroed, 1)
                nc.gpsimd.memset(mhalf[:], -0.5).then_inc(zeroed, 1)
                if "bqk" not in w:
                    nc.gpsimd.memset(bqk[:], 0.0).then_inc(zeroed, 1)
                    nc.gpsimd.memset(bv[:], 0.0).then_inc(zeroed, 1)

            @block.vector
            def _(dve):
                if wide:
                    dve.wait_ge(loaded, 16 * len(loads))
                    nc.vector.tensor_scalar(hscale[:], hscale[:], float(HD) ** -0.5, None, ALU.mult).then_inc(filled, 1)
                    dve.wait_ge(filled, 1)
                    nc.vector.tensor_tensor(bqs[:], bqk[:, 0, :], hscale[:], ALU.mult).then_inc(filled, 1)
                if dist:
                    nc.vector.memset(QS[:], 1.0).then_inc(filled, 1)
                    nc.vector.memset(KS[:], 1.0).then_inc(filled, 1)

        def body(b0, first, last):
            slots = H * BODY + (LAG_OUT + LAG_W if last else 0)

            def head_at(s, lag):
                s -= lag
                if s >= H * BODY or (first and s < 0):
                    return None
                bl, h = divmod(s, H)
                return b0 + bl, bl % 2, h

            def misc_at(s, slot):
                bl, j = divmod(s, H)
                if j == slot and bl < BODY and not (last and bl == BODY - 1):
                    return b0 + bl + 1, (bl + 1) % 2
                return None

            def out_at(s, lag=0):
                s -= lag + LAG_OUT
                if (s + 1) % H == 0 and s < H * BODY and not (first and s < 0):
                    bl = (s + 1) // H - 1
                    return b0 + bl, bl % 2
                return None

            return slots, head_at, misc_at, out_at

        def back(b, h, d):
            return (b, h - d) if h >= d else (b - 1, h - d + H)

        def stage_x(pool, b):
            pool.wait_ge(xT_psum.sem, xT_psum.at(b - 1))
            nc.gpsimd.tensor_copy(xs[:], x_state[:, bass.ds(b * TB, TB), :]).then_inc(xs_ready.sem, 1)

        def add_out_bias(pool, b):
            pool.wait_ge(y_steps.sem, y_steps.at(b - 1, 0))
            if wide:
                pool.wait_ge(z_steps.sem, z_steps.at(b - 1, 2))
            pool.sem_inc(passed, 1)
            nc.gpsimd.tensor_tensor(xb[:], x_state[:, bass.ds(b * TB, TB), :],
                                    bo[:].unsqueeze(1).to_broadcast([P, TB, P]), ALU.add).then_inc(xb_ready.sem, 1)
            if wide:
                nc.gpsimd.tensor_tensor(xbeta[:], x_state[:, bass.ds(b * TB, TB), :],
                                        beta[:].unsqueeze(1).to_broadcast([P, TB, P]), ALU.add).then_inc(xb_ready.sem, 1)

        def turn_x(pe, b):
            pe.wait_ge(xs_ready.sem, xs_ready.at(b, 0))
            if wide:
                pe.wait_ge(vw_out.sem, vw_out.at(b - 1))
            else:
                pe.wait_ge(v_ready.sem, v_ready.at(b - 1))
                pe.wait_ge(y_steps.sem, y_steps.at(b - 3, 0))
            for t in range(TB):
                i = nc.tensor.transpose(psM[:, 0, t * P:(t + 1) * P], xs[:, t, :], consts["ident"][:])
            i.then_inc(xT_psum.sem, 1)

        def take_xT(act, b):
            act.wait_ge(xT_psum.sem, xT_psum.at(b))
            v = vw_psum if wide else v_psum
            act.wait_ge(v.sem, v.at(b - 1))
            nc.scalar.activation(xT[:], psM[:, 0, :], ACT.Copy).then_inc(xT_ready.sem, 1)

        def project_qk(pe, b):
            pe.wait_ge(xT_ready.sem, xT_ready.at(b))
            for j in range(2):
                i = nc.tensor.matmul(psM[:, j, :], wqk[:, j, 0, :], xT[:], start=True, stop=True)
            i.then_inc(qk_psum.sem, 1)

        def take_qk(dve, b):
            dve.wait_ge(qk_psum.sem, qk_psum.at(b))
            dve.wait_ge(split.sem, split.at(b - 1))
            if dist:
                dve.wait_ge(squared.sem, squared.at(b - 1))
            nc.vector.tensor_scalar(qk[:, 0:SEQ], psM[:, 0, :], bqk[:, 0, :], scale, ALU.add, ALU.mult).then_inc(qk_ready.sem, 1)
            nc.vector.tensor_scalar(qk[:, SEQ:], psM[:, 1, :], bqk[:, 1, :], None, ALU.add).then_inc(qk_ready.sem, 1)

        def split_qk(dve, b, step):
            if step == 0:
                dve.wait_ge(qk_ready.sem, qk_ready.at(b))
                dve.wait_ge(stored.sem, stored.at(b - 1))
                nc.vector.tensor_copy(parts[:, 0, :], qk[:]).then_inc(split.sem, 1)
                return
            dve.wait_ge(split.sem, split.at(b, step - 1))
            if step == 1:
                nc.vector.tensor_tensor(rest[:], qk[:], parts[:, 0, :], ALU.subtract).then_inc(split.sem, 1)
            elif step == 2:
                nc.vector.tensor_copy(parts[:, 1, :], rest[:]).then_inc(split.sem, 1)
            else:
                nc.vector.tensor_tensor(parts[:, 2, :], rest[:], parts[:, 1, :], ALU.subtract).then_inc(split.sem, 1)

        def square_qk(pool, b):
            pool.wait_ge(qk_ready.sem, qk_ready.at(b))
            pool.wait_ge(n2_psum.sem, n2_psum.at(b - 1))
            nc.gpsimd.tensor_tensor(sq[:], qk[:], qk[:], ALU.mult).then_inc(squared.sem, 1)

        def sum_squares(pe, b):
            pe.wait_ge(squared.sem, squared.at(b))
            pe.wait_ge(qk_ready.sem, qk_ready.at(b))
            for j in range(2):
                i = nc.tensor.matmul(psM[0:H, j, :], hsum[:, j, :], sq[:, j * SEQ:(j + 1) * SEQ], start=True, stop=True)
            i.then_inc(n2_psum.sem, 1)

        def split_squares(dve, b):
            dve.wait_ge(n2_psum.sem, n2_psum.at(b))
            dve.wait_ge(stored.sem, stored.at(b - 1))
            nc.vector.tensor_copy(n2[:], psM[0:H, :, :].rearrange("p a b -> p (a b)")).then_inc(n2_split.sem, 1)
            dve.wait_ge(n2_split.sem, n2_split.at(b, 0))
            nc.vector.tensor_copy(n2p[:, 0, :], n2[:]).then_inc(n2_split.sem, 1)
            dve.wait_ge(n2_split.sem, n2_split.at(b, 1))
            nc.vector.tensor_tensor(n2r[:], n2[:], n2p[:, 0, :], ALU.subtract).then_inc(n2_split.sem, 1)
            dve.wait_ge(n2_split.sem, n2_split.at(b, 2))
            nc.vector.tensor_copy(n2p[:, 1, :], n2r[:]).then_inc(n2_split.sem, 1)
            dve.wait_ge(n2_split.sem, n2_split.at(b, 3))
            nc.vector.tensor_tensor(n2p[:, 2, :], n2r[:], n2p[:, 1, :], ALU.subtract).then_inc(n2_split.sem, 1)

        def project_v(pe, b):
            if dist:
                pe.wait_ge(n2_split.sem, n2_split.at(b, 0))
            pe.wait_ge(qk_ready.sem, qk_ready.at(b))
            for t in range(TB):
                i = nc.tensor.matmul(psM[:, 0, t * P:(t + 1) * P], xT[:, t * P:(t + 1) * P], wv[:], start=True, stop=True)
            i.then_inc(v_psum.sem, 1)

        def take_v(dve, b, par):
            dve.wait_ge(v_psum.sem, v_psum.at(b))
            dve.wait_ge(weighed.sem, weighed.at(b - 2))
            src = psM[:, 0, :].rearrange("p (t c) -> p t c", t=TB)
            for t in range(TB):
                i = nc.vector.tensor_tensor(v32[:, par, t, :, 0:HD], src[:, t, :].rearrange("p (h c) -> p h c", h=H),
                                            bv[:].rearrange("p (h c) -> p h c", h=H), ALU.add)
            i.then_inc(v_ready.sem, 1)

        def stack(sp, b, par):
            sp.wait_ge(split.sem, split.at(b))
            sp.wait_ge(stacked.sem, stacked.at(b - 1))
            sp.dma_start(scratch["parts"], parts[:]).then_inc(stored.sem, 16)
            if dist:
                sp.wait_ge(n2_split.sem, n2_split.at(b))
                sp.dma_start(scratch["n2"], n2p[:]).then_inc(stored.sem, 16)
            sp.wait_ge(stored.sem, stored.at(b))
            sp.wait_ge(scores.sem, scores.at(b - 2))
            src = scratch["parts"].rearrange("(h c) a n -> a c h n", h=H)
            for a in range(PARTS):
                for a2 in range(PARTS):
                    rows = slice((a * PARTS + a2) * HD, (a * PARTS + a2 + 1) * HD)
                    sp.dma_start(QS[rows, par, :, :], src[a, :, :, 0:SEQ]).then_inc(stacked.sem, 16)
                    sp.dma_start(KS[rows, par, :, :], src[a2, :, :, SEQ:]).then_inc(stacked.sem, 16)
            if dist:
                n2v = scratch["n2"].rearrange("h a n -> a h n")
                sp.dma_start(QS[CROSS:CROSS + PARTS, par, :, :], n2v[:, :, 0:SEQ]).then_inc(stacked.sem, 16)
                sp.dma_start(KS[CROSS + PARTS:KR, par, :, :], n2v[:, :, SEQ:]).then_inc(stacked.sem, 16)

        def project_qk_wide(pe, b, g):
            if g == 0:
                pe.wait_ge(xT_ready.sem, xT_ready.at(b))
            else:
                e = "av"[(g - 1) % 2]
                pe.wait_ge(qk_out[e].sem, qk_out[e].at(b, (g - 1) // 2))
            for j in range(2):
                i = nc.tensor.matmul(psM[:, j, :], wqk[:, j, g, :], xT[:], start=True, stop=True)
            i.then_inc(qkw_psum.sem, 1)

        def take_qk_wide(eng, e, b, par, g):
            eng.wait_ge(qkw_psum.sem, qkw_psum.at(b, g))
            if g < 2:
                eng.wait_ge(scores.sem, scores.at(b - 2))
            halves = [(slice(HD * j, HD * (j + 1)), HG * g + j) for j in range(HG)]
            if e == "a":
                nc.scalar.activation(QT[:, par, g, :], psM[:, 0, :], ACT.Identity, bias=bqs[:, g:g + 1], scale=hscale[:, g:g + 1])
                for rows, h in halves:
                    i = nc.scalar.activation(KT[rows, par, h, :], psM[rows, 1, :], ACT.Identity, bias=bqk[rows, 1, g:g + 1])
            else:
                nc.vector.tensor_scalar(QT[:, par, g, :], psM[:, 0, :], hscale[:, g:g + 1], bqs[:, g:g + 1], ALU.mult, ALU.add)
                for rows, h in halves:
                    i = nc.vector.tensor_scalar(KT[rows, par, h, :], psM[rows, 1, :], bqk[rows, 1, g:g + 1], None, ALU.add)
            i.then_inc(qk_out[e].sem, 1)

        def project_v_wide(pe, b, n):
            t, half = divmod(n, 2)
            if n == 0:
                pe.wait_ge(qk_out["v"].sem, qk_out["v"].at(b))
            else:
                pe.wait_ge(vw_out.sem, vw_out.at(b, n - 1))
            nc.tensor.matmul(psM[:].rearrange("p a b -> p (a b)"), xT[:, t * P:(t + 1) * P], wv[:, 512 * half:512 * (half + 1)],
                             start=True, stop=True).then_inc(vw_psum.sem, 1)

        def take_v_wide(dve, b, par, n):
            t, half = divmod(n, 2)
            dve.wait_ge(vw_psum.sem, vw_psum.at(b, n))
            if n == 0:
                dve.wait_ge(weighed.sem, weighed.at(b - 2))
            cols = slice(512 * half, 512 * (half + 1))
            nc.vector.tensor_tensor(V[:, par, t, cols], psM[:].rearrange("p a b -> p (a b)"), bv[:, cols], ALU.add).then_inc(vw_out.sem, 1)

        def score(pe, b, par, h):
            if h == 0 and not wide:
                pe.wait_ge(stacked.sem, stacked.at(b))
            if wide and h == 0:
                for o in qk_out.values():
                    pe.wait_ge(o.sem, o.at(b))
            pb, ph = back(b, h, bank_last[h])
            if dist:
                pe.wait_ge(clamped.sem, clamped.at(pb, ph * TB + 1))
            else:
                pe.wait_ge(expd.sem, expd.at(pb, ph * TB + 1))
            S = psS[bank[h]]
            for t in range(TB):
                m = P * (t + 1) if causal else SEQ
                if wide:
                    i = nc.tensor.matmul(S[:, t, :], QT[:, par, h // HG, t * P:(t + 1) * P], KT[:, par, h, :], start=True, stop=True)
                    continue
                i = nc.tensor.matmul(S[:, t, 0:m], QS[0:KR, par, h, t * P:(t + 1) * P], KS[0:KR, par, h, 0:m],
                                     start=True, stop=not causal)
                if causal:
                    i = nc.tensor.matmul(S[:, t, m - P:m], consts["identb"][:], consts["mask"][:], start=False, stop=True)
            i.then_inc(scores.sem, 1)

        def row_max(dve, b, h):
            dve.wait_ge(scores.sem, scores.at(b, h))
            S = psS[bank[h]]
            if dist:
                Dh = D[:, h % RING, :]
                pb, ph = back(b, h, RING)
                dve.wait_ge(expd.sem, expd.at(pb, ph * TB + 1))
                for t in range(TB):
                    nc.vector.tensor_scalar(Dh[:, t * SEQ:(t + 1) * SEQ], S[:, t, :], 1e-12, None, ALU.max, ALU.min,
                                            accum_out=Dh[:, TB * SEQ + t:TB * SEQ + t + 1]).then_inc(clamped.sem, 1)
            elif causal:
                nc.vector.tensor_reduce(nmax[:, h % RING, 0:1], S[:, 0, 0:P], AX.X, ALU.max, negate=True)
                nc.vector.tensor_reduce(nmax[:, h % RING, 1:2], S[:, 1, :], AX.X, ALU.max, negate=True).then_inc(maxed.sem, 1)
            else:
                nc.vector.tensor_reduce(nmax[:, h % RING, :], S[:], AX.X, ALU.max, negate=True).then_inc(maxed.sem, 1)

        def take_logs(act, b, h):
            act.wait_ge(clamped.sem, clamped.at(b, h * TB + 1))
            nc.scalar.activation(D[:, h % RING, :], D[:, h % RING, :], ACT.Ln).then_inc(logged.sem, 1)

        def take_roots(act, b, h):
            act.wait_ge(logged.sem, logged.at(b, h))
            nc.scalar.activation(D[:, h % RING, :], D[:, h % RING, :], ACT.Exp, scale=0.5).then_inc(rooted.sem, 1)

        def exps(act, b, h):
            r = h % RING
            if dist:
                act.wait_ge(rooted.sem, rooted.at(b, h))
            else:
                act.wait_ge(maxed.sem, maxed.at(b, h))
            pb, ph = back(b, h, RING)
            act.wait_ge(turned.sem, turned.at(pb, ph))
            act.wait_ge(sums_inv.sem, sums_inv.at(pb, ph))
            for t in range(TB):
                m = P if causal and t == 0 else SEQ
                if dist:
                    src, bias, sc = D[:, r, t * SEQ:(t + 1) * SEQ], D[:, r, TB * SEQ + t:TB * SEQ + t + 1], -1.0
                else:
                    src, bias, sc = psS[bank[h]][:, t, 0:m], nmax[:, r, t:t + 1], 1.0
                nc.scalar.activation(prob[:, r, t, 0:m], src, ACT.Exp, bias=bias, scale=sc,
                                     accum_out=rsum[:, r, t:t + 1]).then_inc(expd.sem, 1)

        def invert_sums(dve, b, h):
            dve.wait_ge(expd.sem, expd.at(b, h * TB + 1))
            pb, ph = back(b, h, RING)
            dve.wait_ge(normed.sem, normed.at(pb, ph * TB + 1))
            nc.vector.reciprocal(rinv[:, h % RING, :], rsum[:, h % RING, :]).then_inc(sums_inv.sem, 1)

        def normalise(pool, b, h):
            r = h % RING
            pool.wait_ge(sums_inv.sem, sums_inv.at(b, h))
            pool.sem_inc(passed, 1)
            for t in range(TB):
                m = P if causal and t == 0 else SEQ
                nc.gpsimd.tensor_scalar(prob[:, r, t, 0:m], prob[:, r, t, 0:m], rinv[:, r, t:t + 1], 1.0,
                                        ALU.mult, ALU.mult).then_inc(normed.sem, 1)

        def turn(pe, b, h):
            pe.wait_ge(normed.sem, normed.at(b, h * TB + 1))
            pb, ph = back(b, h, 2)
            e = evac_by[ph]
            pe.wait_ge(turned_out[e].sem, turned_out[e].at(pb, per_e[e].index(ph)))
            T = psT[h % 2]
            for t in range(TB):
                for m in range(TB):
                    if causal and m > t:
                        continue
                    i = nc.tensor.transpose(T[:, m, t * P:(t + 1) * P], prob[:, h % RING, t, m * P:(m + 1) * P], consts["ident"][:])
            i.then_inc(turned.sem, 1)

        def take_turned(eng, e, b, h):
            eng.wait_ge(turned.sem, turned.at(b, h))
            pb, ph = back(b, h, RING)
            eng.wait_ge(weighed.sem, weighed.at(pb, ph))
            regions = [(slice(0, 2), slice(0, SEQ))]
            if causal:
                src, dst = (z.rearrange("p a b -> p (a b)") for z in (psT[h % 2][:], probT[:, h % RING, :, :]))
                pieces = [(dst[:, 0:SEQ], src[:, 0:SEQ]), (dst[:, SEQ + P:], src[:, SEQ + P:])]
            else:
                pieces = [(probT[:, h % RING, :, :], psT[h % 2][:])]
            for dst, src in pieces:
                i = nc.scalar.activation(dst, src, ACT.Copy) if e == "a" else nc.vector.tensor_copy(dst, src)
            i.then_inc(turned_out[e].sem, 1)

        def weigh(pe, b, par, h):
            e = evac_by[h]
            pe.wait_ge(turned_out[e].sem, turned_out[e].at(b, per_e[e].index(h)))
            grp, j = divmod(h, HG)
            if h == 0:
                v = vw_out if wide else v_ready
                pe.wait_ge(v.sem, v.at(b))
            if j == 0:
                pb, pg = (b, grp - 2) if grp >= 2 else (b - 1, grp - 2 + NG)
                pe.wait_ge(o_out.sem, o_out.at(pb, pg))
            for m in range(TB):
                n0 = P * m if causal else 0
                width = P // HG
                vh = V[:, par, m, h * HD:(h + 1) * HD] if wide else v32[:, par, m, h, :]
                i = nc.tensor.matmul(psO[grp % 2][width * j:width * (j + 1), n0:], vh, probT[:, h % RING, m, n0:],
                                     start=(m == 0), stop=(m == TB - 1))
            i.then_inc(weighed.sem, 1)

        def take_o(act, b, grp):
            act.wait_ge(weighed.sem, weighed.at(b, HG * grp + HG - 1))
            act.wait_ge(y_psum.sem, y_psum.at(b - 1))
            nc.scalar.activation(OT[:, grp, :], psO[grp % 2][:], ACT.Copy).then_inc(o_out.sem, 1)

        def project_out(pe, b, staged):
            pe.wait_ge(o_out.sem, o_out.at(b))
            if not wide:
                pe.wait_ge(v_ready.sem, v_ready.at(staged))
            pe.wait_ge(y_steps.sem, y_steps.at(b - 1, 0))
            for t in range(TB):
                for grp in range(NG):
                    i = nc.tensor.matmul(psY[:, t * P:(t + 1) * P], OT[:, grp, t * P:(t + 1) * P], wo[:, grp, :],
                                         start=(grp == 0), stop=(grp == NG - 1))
            i.then_inc(y_psum.sem, 1)

        def norm_stats(dve, b):
            dve.wait_ge(y_psum.sem, y_psum.at(b))
            dve.wait_ge(xb_ready.sem, xb_ready.at(b))
            dve.wait_ge(x_done.sem, x_done.at(b - 1))
            nc.vector.tensor_tensor(y[:], psY.rearrange("p (t c) -> p t c", t=TB), xb[:], ALU.add).then_inc(y_steps.sem, 1)
            dve.wait_ge(y_steps.sem, y_steps.at(b, 0))
            for t in range(TB):
                nc.vector.bn_stats(stats[:, t, :], y[:, t, :]).then_inc(y_steps.sem, 1)
            dve.wait_ge(y_steps.sem, y_steps.at(b, 2))
            dve.sem_inc(passed, 1)
            for t in range(TB):
                nc.vector.bn_aggr(mv[:, t, :], stats[:, t, :]).then_inc(y_steps.sem, 1)
            dve.wait_ge(y_steps.sem, y_steps.at(b, 4))
            nc.vector.tensor_scalar(veps[:], mv[:, :, 1], EPS, None, ALU.add).then_inc(y_steps.sem, 1)

        def root_var(pool, b):
            pool.wait_ge(y_steps.sem, y_steps.at(b, 5))
            last = z_steps.at(b - 1, 1) if wide else x_done.at(b - 1)
            pool.wait_ge(z_steps.sem if wide else x_done.sem, last)
            nc.gpsimd.tensor_tensor(rstd[:], veps[:], mhalf[:], ALU.pow).then_inc(rstd_ready.sem, 1)

        def write_x(dve, b):
            ready = rstd2_ready if wide else rstd_ready
            dve.wait_ge(ready.sem, ready.at(b))
            for t in range(TB):
                nc.vector.tensor_scalar(x_state[:, bass.ds(b * TB + t, 1), :], y[:, t:t + 1, :], mv[:, t, 0:1], rstd[:, t:t + 1],
                                        ALU.subtract, ALU.mult).then_inc(x_done.sem, 1)

        def inner_norm(dve, b):
            dve.wait_ge(rstd_ready.sem, rstd_ready.at(b))
            n = 0
            for t in range(TB):
                nc.vector.tensor_scalar(z[:, t, :], y[:, t, :], mv[:, t, 0:1], rstd[:, t:t + 1],
                                        ALU.subtract, ALU.mult).then_inc(z_steps.sem, 1)
            dve.wait_ge(z_steps.sem, z_steps.at(b, 1))
            nc.vector.tensor_tensor(y[:], z[:], gamma[:].unsqueeze(1).to_broadcast([P, TB, P]), ALU.mult).then_inc(a_scaled.sem, 1)
            dve.wait_ge(a_scaled.sem, a_scaled.at(b))
            nc.vector.tensor_tensor(y[:], y[:], xbeta[:], ALU.add).then_inc(z_steps.sem, 1)
            dve.wait_ge(z_steps.sem, z_steps.at(b, 2))
            for t in range(TB):
                nc.vector.bn_stats(stats[:, t, :], y[:, t, :]).then_inc(z_steps.sem, 1)
            dve.wait_ge(z_steps.sem, z_steps.at(b, 4))
            dve.sem_inc(passed, 1)
            for t in range(TB):
                nc.vector.bn_aggr(mv[:, t, :], stats[:, t, :]).then_inc(z_steps.sem, 1)
            dve.wait_ge(z_steps.sem, z_steps.at(b, 6))
            nc.vector.tensor_scalar(veps[:], mv[:, :, 1], EPS, None, ALU.add).then_inc(z_steps.sem, 1)

        def root_var2(pool, b):
            pool.wait_ge(z_steps.sem, z_steps.at(b, 7))
            nc.gpsimd.tensor_tensor(rstd[:], veps[:], mhalf[:], ALU.pow).then_inc(rstd2_ready.sem, 1)

        def run(eng, emit):
            emit(0, True, False)
            with eng.Fori(1, NB // BODY - 1) as i:
                emit(i * BODY, False, False)
            emit(NB - BODY, False, True)

        with nc.Block() as block:
            @block.sync
            def _(sp):
                if wide:
                    return
                for s in (stored, stacked):
                    s.open(sp)
                stack(sp, 0, 0)

                def emit(b0, first, last):
                    slots, head_at, misc_at, out_at = body(b0, first, last)
                    for s in range(slots):
                        if a := misc_at(s, SLOT_QK):
                            stack(sp, *a)
                run(sp, emit)

            @block.gpsimd
            def _(pool):
                for s in [xs_ready, xb_ready, normed, rstd_ready] + ([rstd2_ready] if wide else []) + ([squared] if dist else []):
                    s.open(pool)
                stage_x(pool, 0)
                if dist:
                    square_qk(pool, 0)

                def emit(b0, first, last):
                    slots, head_at, misc_at, out_at = body(b0, first, last)
                    for s in range(slots):
                        if a := misc_at(s, SLOT_XT):
                            stage_x(pool, a[0])
                        if dist and (a := misc_at(s, SLOT_QK + 1)):
                            square_qk(pool, a[0])
                        if a := head_at(s, LAG_N):
                            normalise(pool, a[0], a[2])
                        if a := out_at(s, -2):
                            add_out_bias(pool, a[0])
                        if a := out_at(s):
                            root_var(pool, a[0])
                        if wide and (a := out_at(s, LAG_W // 2)):
                            root_var2(pool, a[0])
                run(pool, emit)

            @block.tensor
            def _(pe):
                for s in [xT_psum, qk_psum, v_psum, scores, turned, weighed, y_psum] + ([qkw_psum, vw_psum] if wide else []) + ([n2_psum] if dist else []):
                    s.open(pe)
                turn_x(pe, 0)
                if wide:
                    for g in range(NG):
                        project_qk_wide(pe, 0, g)
                    for n in range(2 * TB):
                        project_v_wide(pe, 0, n)
                else:
                    project_qk(pe, 0)
                    if dist:
                        sum_squares(pe, 0)
                    project_v(pe, 0)

                def emit(b0, first, last):
                    slots, head_at, misc_at, out_at = body(b0, first, last)
                    for s in range(slots):
                        if a := head_at(s, 0):
                            score(pe, *a)
                        if a := head_at(s, LAG_T):
                            turn(pe, a[0], a[2])
                        if a := head_at(s, LAG_PV):
                            weigh(pe, *a)
                        if a := misc_at(s, SLOT_XT):
                            turn_x(pe, a[0])
                        if wide:
                            for g in range(NG):
                                if a := misc_at(s, SLOT_QK + g):
                                    project_qk_wide(pe, a[0], g)
                            for n in range(2 * TB):
                                if a := misc_at(s, SLOT_QK + NG + n):
                                    project_v_wide(pe, a[0], n)
                        elif a := misc_at(s, SLOT_QK):
                            project_qk(pe, a[0])
                        if dist and (a := misc_at(s, SLOT_QK + 1)):
                            sum_squares(pe, a[0])
                        if not wide and (a := misc_at(s, SLOT_V)):
                            project_v(pe, a[0])
                        if a := out_at(s):
                            project_out(pe, a[0], b0 + BODY - 1 if last else a[0] + 2)
                run(pe, emit)

            @block.scalar
            def _(act):
                for s in [xT_ready, expd, o_out, turned_out["a"]] + ([logged, rooted] if dist else []) + ([qk_out["a"]] if wide else []):
                    s.open(act)
                nc.scalar.preload_act_table_set("natural_log_exp_and_others" if dist else "exp_and_others")
                take_xT(act, 0)
                if wide:
                    for g in range(0, NG, 2):
                        take_qk_wide(act, "a", 0, 0, g)

                def emit(b0, first, last):
                    slots, head_at, misc_at, out_at = body(b0, first, last)
                    for s in range(slots):
                        if dist and (a := head_at(s, LAG_M)):
                            take_logs(act, a[0], a[2])
                        if dist and (a := head_at(s, LAG_R)):
                            take_roots(act, a[0], a[2])
                        if a := head_at(s, LAG_E):
                            exps(act, a[0], a[2])
                        if a := misc_at(s, SLOT_XT):
                            take_xT(act, a[0])
                        a = head_at(s, LAG_K)
                        if a and evac_by[a[2]] == "a":
                            take_turned(act, "a", a[0], a[2])
                        a = head_at(s, LAG_O)
                        if a and a[2] % HG == HG - 1:
                            take_o(act, a[0], a[2] // HG)
                        if wide:
                            for g in range(0, NG, 2):
                                if a := misc_at(s, SLOT_QK + g):
                                    take_qk_wide(act, "a", *a, g)
                run(act, emit)

            @block.vector
            def _(dve):
                for s in [qk_ready, v_ready, split, maxed, sums_inv, turned_out["v"], y_steps, x_done] + ([n2_split, clamped] if dist else []) + ([qk_out["v"], vw_out, z_steps, a_scaled] if wide else []):
                    s.open(dve)
                if wide:
                    for g in range(1, NG, 2):
                        take_qk_wide(dve, "v", 0, 0, g)
                    for n in range(2 * TB):
                        take_v_wide(dve, 0, 0, n)
                else:
                    take_qk(dve, 0)
                    for step in range(4):
                        split_qk(dve, 0, step)
                    if dist:
                        split_squares(dve, 0)
                    take_v(dve, 0, 0)

                def emit(b0, first, last):
                    slots, head_at, misc_at, out_at = body(b0, first, last)
                    for s in range(slots):
                        if a := head_at(s, LAG_M):
                            row_max(dve, a[0], a[2])
                        if a := head_at(s, LAG_N):
                            invert_sums(dve, a[0], a[2])
                        a = head_at(s, LAG_K)
                        if a and evac_by[a[2]] == "v":
                            take_turned(dve, "v", a[0], a[2])
                        if wide:
                            for g in range(1, NG, 2):
                                if a := misc_at(s, SLOT_QK + g):
                                    take_qk_wide(dve, "v", *a, g)
                            for n in range(2 * TB):
                                if a := misc_at(s, SLOT_QK + NG + n):
                                    take_v_wide(dve, *a, n)
                        elif a := misc_at(s, SLOT_QK):
                            take_qk(dve, a[0])
                        for step in range(0 if wide else 4):
                            if a := misc_at(s, SLOT_QK + 1 + step):
                                split_qk(dve, a[0], step)
                        if dist and (a := misc_at(s, SLOT_QK + 1)):
                            split_squares(dve, a[0])
                        if not wide and (a := misc_at(s, SLOT_V + 1)):
                            take_v(dve, *a)
                        if a := out_at(s):
                            norm_stats(dve, a[0])
                        if wide and (a := out_at(s, LAG_W // 2)):
                            inner_norm(dve, a[0])
                        if a := out_at(s, LAG_W):
                            write_x(dve, a[0])
                run(dve, emit)


def turn_all(nc, name, x_state, XT, consts):
    with ExitStack() as ctx:
        banks = [ctx.enter_context(nc.psum_tensor(f"{name}_xt{i}", [P, 4, P], F32)) for i in range(4)]
        turned, out = nc.alloc_semaphore(f"{name}_turned"), [nc.alloc_semaphore(f"{name}_out{e}") for e in "va"]
        with nc.Block() as block:
            @block.tensor
            def _(pe):
                for g in range(NT // 4):
                    if g >= 4:
                        pe.wait_ge(out[g % 2], (g - 4) // 2 + 1)
                    for t in range(4):
                        i = nc.tensor.transpose(banks[g % 4][:, t, :], x_state[:, 4 * g + t, :], consts["ident"][:])
                    i.then_inc(turned, 1)

            @block.vector
            def _(dve):
                for g in range(0, NT // 4, 2):
                    dve.wait_ge(turned, g + 1)
                    nc.vector.tensor_copy(XT[:, 4 * g * P:4 * (g + 1) * P], banks[g % 4][:].rearrange("p a b -> p (a b)")).then_inc(out[0], 1)

            @block.scalar
            def _(act):
                for g in range(1, NT // 4, 2):
                    act.wait_ge(turned, g + 1)
                    nc.scalar.activation(XT[:, 4 * g * P:4 * (g + 1) * P], banks[g % 4][:].rearrange("p a b -> p (a b)"), ACT.Copy).then_inc(out[1], 1)




def finish_layer(nc, name, x_state, acc):
    G = 4
    with ExitStack() as ctx:
        def sb(n, shape, dt=F32):
            return ctx.enter_context(nc.sbuf_tensor(f"{name}_{n}", shape, dt))

        y, stats, mv = sb("y", [P, NT, P]), sb("stats", [P, NT, 6]), sb("mv", [P, NT, 2])
        veps, rstd, mhalf = sb("veps", [P, NT]), sb("rstd", [P, NT]), sb("mhalf", [P, NT])
        added, stated, aggregated = (nc.alloc_semaphore(f"{name}_{n}") for n in ("added", "stated", "aggregated"))
        filled, rooted = nc.alloc_semaphore(f"{name}_filled"), nc.alloc_semaphore(f"{name}_rooted")
        var_ready = nc.alloc_semaphore(f"{name}_var_ready")
        with nc.Block() as block:
            @block.gpsimd
            def _(pool):
                nc.gpsimd.memset(mhalf[:], -0.5).then_inc(filled, 1)
                pool.wait_ge(filled, 1)
                for g in range(NT // G):
                    s = slice(g * G, (g + 1) * G)
                    pool.wait_ge(var_ready, g + 1)
                    nc.gpsimd.tensor_tensor(rstd[:, s], veps[:, s], mhalf[:, s], ALU.pow).then_inc(rooted, 1)

            @block.vector
            def _(dve):
                def write(g):
                    dve.wait_ge(rooted, g + 1)
                    for t in range(g * G, (g + 1) * G):
                        nc.vector.tensor_scalar(x_state[:, t, :], y[:, t, :], mv[:, t, 0:1], rstd[:, t:t + 1], ALU.subtract, ALU.mult)

                for g in range(NT // G):
                    s = slice(g * G, (g + 1) * G)
                    nc.vector.tensor_tensor(y[:, s, :], x_state[:, s, :], acc[:, s, :], ALU.add).then_inc(added, 1)
                    dve.wait_ge(added, g + 1)
                    for t in range(g * G, (g + 1) * G):
                        nc.vector.bn_stats(stats[:, t, :], y[:, t, :]).then_inc(stated, 1)
                    for t in range(g * G, (g + 1) * G):
                        dve.wait_ge(stated, t + 1)
                        nc.vector.bn_aggr(mv[:, t, :], stats[:, t, :]).then_inc(aggregated, 1)
                    dve.wait_ge(aggregated, (g + 1) * G)
                    nc.vector.tensor_scalar(veps[:, s], mv[:, s, 1], EPS, None, ALU.add).then_inc(var_ready, 1)
                    if g:
                        write(g - 1)
                write(NT // G - 1)


def route(nc, name, kind, XT, consts, w, coef, acc, cap=None):
    with ExitStack() as ctx:
        def sb(n, shape, dt=F32):
            return ctx.enter_context(nc.sbuf_tensor(f"{name}_{n}", shape, dt))

        def te(n, dt=F32):
            return sb(n, [P, NT, E], dt)

        def over_e(a):
            return a[:].unsqueeze(2).to_broadcast([P, NT, E])

        def over_t(a):
            return a[:].unsqueeze(1).to_broadcast([P, NT, E])

        def flat(a):
            return a[:].rearrange("p t e -> p (t e)")

        gate = sb("gate", [P, E])
        logit, d, ex, first, val, sel1, sel2 = (te(n) for n in ("logit", "d", "ex", "first", "val", "sel1", "sel2"))
        order = sb("order", [P, E])
        top, total, inv, p1, p2 = (sb(n, [P, NT]) for n in ("top", "total", "inv", "p1", "p2"))
        psL = ctx.enter_context(nc.psum_tensor(f"{name}_L", [P, NT, E], F32))
        psR = ctx.enter_context(nc.psum_tensor(f"{name}_R", [P, NT, E], F32))
        psN = ctx.enter_context(nc.psum_tensor(f"{name}_N", [P, NT, E], F32))
        psC = [ctx.enter_context(nc.psum_tensor(f"{name}_C{i}", [E + 1, 4, P], F32)) for i in range(2)]
        psB = [ctx.enter_context(nc.psum_tensor(f"{name}_B{i}", [P, 4, P], F32)) for i in range(2)]
        coefT, b2 = sb("coefT", [E + 1, NT, P]), sb("b2", [E + 1, P])
        loads = [(gate[:], w["gate"]), (order[:], consts["order"].partition_broadcast(P))]
        if kind != "mean2":
            loads += [(b2[:], w["b2"])]
        if kind == "cap2":
            pb, eb = sb("pb", [P, E]), sb("eb", [P, E])
            bits = sb("bits", [P, 31, E], I32)
            loads += [(pb[:], w["proj_b"].partition_broadcast(P)), (eb[:], w["expert_bias"].partition_broadcast(P)),
                      (bits[:], consts["bits"])]
        loaded, logits = nc.alloc_semaphore(f"{name}_loaded"), nc.alloc_semaphore(f"{name}_logits")
        chain, exps = nc.alloc_semaphore(f"{name}_chain"), nc.alloc_semaphore(f"{name}_exps")
        counted = nc.alloc_semaphore(f"{name}_counted")
        coefT_psum, coefT_out = nc.alloc_semaphore(f"{name}_coefT_psum"), nc.alloc_semaphore(f"{name}_coefT_out")
        b2_psum, b2_out = nc.alloc_semaphore(f"{name}_b2_psum"), nc.alloc_semaphore(f"{name}_b2_out")

        with nc.Block() as block:
            @block.sync
            def _(sp):
                for dst, src in loads:
                    sp.dma_start(dst, src).then_inc(loaded, 16)
                sp.wait_ge(loaded, 16 * len(loads))

            @block.tensor
            def _(pe):
                pe.wait_ge(loaded, 16 * len(loads))
                for t in range(NT):
                    i = nc.tensor.matmul(psL[:, t, :], XT[:, t * P:(t + 1) * P], gate[:], start=True, stop=True)
                i.then_inc(logits, 1)

            @block.scalar
            def _(act):
                act.wait_ge(chain, 3)
                nc.scalar.activation(flat(ex), flat(d), ACT.Exp, scale=-1.0 if kind == "cap2" else 1.0).then_inc(exps, 1)

            @block.vector
            def _(dve):
                n = [0]

                def link(i):
                    n[0] += 1
                    i.then_inc(chain, 1)
                    dve.wait_ge(chain, n[0])

                def pick(sel, of):
                    link(nc.vector.tensor_reduce(top[:], of[:], AX.X, ALU.max))
                    link(nc.vector.tensor_tensor(first[:], of[:], over_e(top), ALU.is_equal))
                    link(nc.vector.tensor_tensor(val[:], first[:], over_t(order), ALU.mult))
                    link(nc.vector.tensor_reduce(total[:], val[:], AX.X, ALU.max))
                    link(nc.vector.tensor_tensor(sel[:], val[:], over_e(total), ALU.is_equal))

                dve.wait_ge(loaded, 16 * len(loads))
                dve.wait_ge(logits, 1)
                if kind == "cap2":
                    link(nc.vector.tensor_copy(logit[:], psL[:]))
                    link(nc.vector.tensor_tensor(d[:], logit[:], over_t(pb), ALU.add))
                    link(nc.vector.tensor_copy(logit[:], d[:]))
                    dve.wait_ge(exps, 1)
                    link(nc.vector.tensor_scalar(ex[:], ex[:], 1.0, None, ALU.add))
                    link(nc.vector.reciprocal(d[:], ex[:]))
                    link(nc.vector.tensor_tensor(ex[:], d[:], over_t(eb), ALU.add))
                    link(nc.vector.tensor_scalar(ex[:], ex[:], 1e-12, None, ALU.max))
                else:
                    link(nc.vector.tensor_copy(logit[:], psL[:]))
                    link(nc.vector.tensor_reduce(top[:], logit[:], AX.X, ALU.max))
                    link(nc.vector.tensor_tensor(d[:], logit[:], over_e(top), ALU.subtract))
                    dve.wait_ge(exps, 1)
                link(nc.vector.tensor_reduce(total[:], ex[:], AX.X, ALU.add))
                link(nc.vector.reciprocal(inv[:], total[:]))
                link(nc.vector.tensor_tensor(ex[:], ex[:], over_e(inv), ALU.mult))
                pick(sel1, logit if kind != "cap2" else ex)
                if kind == "top1":
                    link(nc.vector.tensor_tensor(coef[:, :, 0:E], ex[:], sel1[:], ALU.mult))
                else:
                    link(nc.vector.tensor_tensor(d[:], ex[:], sel1[:], ALU.subtract))
                    link(nc.vector.tensor_scalar(val[:], sel1[:], -2.0, None, ALU.mult))
                    link(nc.vector.tensor_tensor(d[:], d[:], val[:], ALU.add))
                    pick(sel2, d)
                    link(nc.vector.tensor_tensor(sel1[:], sel1[:], sel2[:], ALU.add))
                    link(nc.vector.tensor_tensor(d[:], ex[:], sel1[:], ALU.mult))
                    link(nc.vector.tensor_reduce(p1[:], d[:], AX.X, ALU.add))
                    link(nc.vector.tensor_scalar(p1[:], p1[:], 1e-12, None, ALU.max))
                    link(nc.vector.reciprocal(inv[:], p1[:]))
                    link(nc.vector.tensor_tensor(val[:], d[:], over_e(inv), ALU.mult))

        if kind == "mean2":
            cnt, wsum, mean = (sb(n, [P, E]) for n in ("cnt", "wsum", "mean"))
            with nc.Block() as block:
                @block.tensor
                def _(pe):
                    nc.tensor.matmul(flat(psR), consts["ones"][:], flat(sel1), start=True, stop=True).then_inc(counted, 1)
                    nc.tensor.matmul(flat(psN), consts["ones"][:], flat(val), start=True, stop=True).then_inc(counted, 1)

                @block.vector
                def _(dve):
                    chain2, n = nc.alloc_semaphore(f"{name}_chain2"), [0]

                    def link(i):
                        n[0] += 1
                        i.then_inc(chain2, 1)
                        dve.wait_ge(chain2, n[0])

                    dve.wait_ge(counted, 2)
                    link(nc.vector.tensor_reduce(cnt[:], psR[:].rearrange("p t e -> p e t"), AX.X, ALU.add))
                    link(nc.vector.tensor_reduce(wsum[:], psN[:].rearrange("p t e -> p e t"), AX.X, ALU.add))
                    link(nc.vector.tensor_scalar(cnt[:], cnt[:], 1.0, None, ALU.max))
                    link(nc.vector.reciprocal(mean[:], cnt[:]))
                    link(nc.vector.tensor_tensor(mean[:], mean[:], wsum[:], ALU.mult))
                    link(nc.vector.tensor_tensor(coef[:, :, 0:E], sel1[:], over_t(mean), ALU.mult))
                    link(nc.vector.memset(acc[:], 0.0))
            return

        if kind == "cap2":
            cand, thr = sb("cand", [P, E], I32), sb("thr", [P, E], I32)
            step, cnt, need = sb("step", [P, E], I32), sb("cnt", [P, E]), sb("need", [P, E])
            reach = te("reach")
            reached, tallied = nc.alloc_semaphore(f"{name}_reached"), nc.alloc_semaphore(f"{name}_tallied")
            bis = nc.alloc_semaphore(f"{name}_bisect")
            PER = 5
            with nc.Block() as block:
                @block.tensor
                def _(pe):
                    with pe.Fori(0, 31) as i:
                        pe.wait_ge(reached, i + 1)
                        nc.tensor.matmul(flat(psN), consts["ones"][:], flat(reach), start=True, stop=True).then_inc(tallied, 1)

                @block.vector
                def _(dve):
                    nc.vector.memset(thr[:], 0).then_inc(bis, 1)
                    dve.wait_ge(bis, 1)
                    with dve.Fori(0, 31) as i:
                        nc.vector.tensor_tensor(cand[:], thr[:], bits[:, bass.ds(i, 1), :].rearrange("p a e -> p (a e)"), ALU.bitwise_or).then_inc(bis, 1)
                        dve.wait_ge(bis, i * PER + 2)
                        nc.vector.tensor_tensor(reach[:], val[:], over_t(cand.bitcast(F32)), ALU.is_ge).then_inc(reached, 1)
                        dve.wait_ge(tallied, i + 1)
                        nc.vector.tensor_reduce(cnt[:], psN[:].rearrange("p t e -> p e t"), AX.X, ALU.add).then_inc(bis, 1)
                        dve.wait_ge(bis, i * PER + 3)
                        nc.vector.tensor_scalar(need[:], cnt[:], float(cap), None, ALU.is_ge).then_inc(bis, 1)
                        dve.wait_ge(bis, i * PER + 4)
                        nc.vector.tensor_tensor(step[:], need[:], bits[:, bass.ds(i, 1), :].rearrange("p a e -> p (a e)"), ALU.mult).then_inc(bis, 1)
                        dve.wait_ge(bis, i * PER + 5)
                        nc.vector.tensor_tensor(thr[:], thr[:], step[:], ALU.bitwise_or).then_inc(bis, 1)
                        dve.wait_ge(bis, i * PER + 6)

            tallied2 = nc.alloc_semaphore(f"{name}_tallied2")
            above, chain3 = te("above"), nc.alloc_semaphore(f"{name}_chain3")
            with nc.Block() as block:
                @block.tensor
                def _(pe):
                    pe.wait_ge(chain3, 2)
                    nc.tensor.matmul(flat(psL), consts["ones"][:], flat(above), start=True, stop=True).then_inc(tallied2, 1)
                    nc.tensor.matmul(flat(psR), consts["below"][:], flat(reach), start=True, stop=True).then_inc(tallied2, 1)
                    nc.tensor.matmul(flat(psN), consts["ones"][:], flat(reach), start=True, stop=True).then_inc(tallied2, 1)

                @block.vector
                def _(dve):
                    n = [0]

                    def link(i):
                        n[0] += 1
                        i.then_inc(chain3, 1)
                        dve.wait_ge(chain3, n[0])

                    link(nc.vector.tensor_tensor(above[:], val[:], over_t(thr.bitcast(F32)), ALU.is_gt))
                    link(nc.vector.tensor_tensor(reach[:], val[:], over_t(thr.bitcast(F32)), ALU.is_equal))
                    dve.wait_ge(tallied2, 3)
                    link(nc.vector.tensor_reduce(cnt[:], psL[:].rearrange("p t e -> p e t"), AX.X, ALU.add))
                    link(nc.vector.tensor_scalar(need[:], cnt[:], -1.0, float(cap), ALU.mult, ALU.add))
                    link(nc.vector.tensor_copy(d[:], psN[:]))
                    for e in range(E):
                        link(nc.vector.tensor_tensor_scan(first[:, :, e], consts["ones"][:, 0:NT], d[:, :, e], 0.0, ALU.mult, ALU.add))
                    link(nc.vector.tensor_tensor(first[:], first[:], d[:], ALU.subtract))
                    link(nc.vector.tensor_tensor(first[:], first[:], psR[:], ALU.add))
                    link(nc.vector.tensor_tensor(first[:], first[:], over_t(need), ALU.is_lt))
                    link(nc.vector.tensor_tensor(reach[:], first[:], reach[:], ALU.mult))
                    link(nc.vector.tensor_tensor(above[:], above[:], reach[:], ALU.add))
                    link(nc.vector.tensor_tensor(coef[:, :, 0:E], above[:], val[:], ALU.mult))
                    link(nc.vector.memset(coef[:, :, E:E + 1], 1.0))
        else:
            chain4, counted4 = nc.alloc_semaphore(f"{name}_chain4"), nc.alloc_semaphore(f"{name}_counted4")
            with nc.Block() as block:
                @block.tensor
                def _(pe):
                    nc.tensor.matmul(flat(psR), consts["below"][:], flat(sel1), start=True, stop=True).then_inc(counted4, 1)
                    nc.tensor.matmul(flat(psN), consts["ones"][:], flat(sel1), start=True, stop=True).then_inc(counted4, 1)

                @block.vector
                def _(dve):
                    n = [0]

                    def link(i):
                        n[0] += 1
                        i.then_inc(chain4, 1)
                        dve.wait_ge(chain4, n[0])

                    dve.wait_ge(counted4, 2)
                    link(nc.vector.tensor_copy(d[:], psN[:]))
                    for e in range(E):
                        link(nc.vector.tensor_tensor_scan(first[:, :, e], consts["ones"][:, 0:NT], d[:, :, e], 0.0, ALU.mult, ALU.add))
                    link(nc.vector.tensor_tensor(first[:], first[:], d[:], ALU.subtract))
                    link(nc.vector.tensor_tensor(first[:], first[:], psR[:], ALU.add))
                    link(nc.vector.tensor_scalar(first[:], first[:], float(cap), None, ALU.is_lt))
                    link(nc.vector.tensor_tensor(coef[:, :, 0:E], coef[:, :, 0:E], first[:], ALU.mult))
                    link(nc.vector.memset(coef[:, :, E:E + 1], 1.0))

        with nc.Block() as block:
            @block.tensor
            def _(pe):
                def turn(g):
                    if g >= 2:
                        pe.wait_ge(coefT_out, g - 1)
                    for t in range(4):
                        i = nc.tensor.transpose(psC[g % 2][:, t, :], coef[:, 4 * g + t, :], consts["ident"][:])
                    i.then_inc(coefT_psum, 1)

                turn(0)
                for g in range(NT // 4):
                    if g + 1 < NT // 4:
                        turn(g + 1)
                    pe.wait_ge(coefT_out, g + 1)
                    if g >= 2:
                        pe.wait_ge(b2_out, g - 1)
                    for t in range(4):
                        i = nc.tensor.matmul(psB[g % 2][:, t, :], coefT[:, 4 * g + t, :], b2[:], start=True, stop=True)
                    i.then_inc(b2_psum, 1)

            @block.scalar
            def _(act):
                for g in range(NT // 4):
                    act.wait_ge(coefT_psum, g + 1)
                    nc.scalar.activation(coefT[:, 4 * g:4 * g + 4, :], psC[g % 2][:], ACT.Copy).then_inc(coefT_out, 1)

            @block.vector
            def _(dve):
                for g in range(NT // 4):
                    dve.wait_ge(b2_psum, g + 1)
                    nc.vector.tensor_copy(acc[:, 4 * g:4 * g + 4, :], psB[g % 2][:]).then_inc(b2_out, 1)


def experts(nc, name, XT, coef, acc, w, n_experts, F, func, gated=False, table=None):
    C = 512
    NC, TC, NF = NT * P // C, C // P, F // P
    with ExitStack() as ctx:
        def sb(n, shape, dt=F32):
            return ctx.enter_context(nc.sbuf_tensor(f"{name}_{n}", shape, dt))

        w1, w2 = sb("w1", [P, 2, F * (1 + gated)]), sb("w2", [P, 2, NF, P])
        hT = sb("hT", [P, 2, NF, C])
        b1 = None if gated else sb("b1", [P, 2, NF])
        g_sb = sb("g", [P, 2, C]) if gated else None
        NH = 2 if gated else 4
        psH = [[ctx.enter_context(nc.psum_tensor(f"{name}_H{i}{j}", [P, C], F32)) for j in range(1 + gated)] for i in range(NH)]
        psY = [ctx.enter_context(nc.psum_tensor(f"{name}_Y{i}", [P, TC, P], F32)) for i in range(2)]

        weights = [Signal(nc, f"{name}_weights{i}", 32 if gated else 48) for i in range(2)]
        h_psum = Signal(nc, f"{name}_h_psum", NF)
        g_out = Signal(nc, f"{name}_g_out", NF)
        h_out = Signal(nc, f"{name}_h_out", NF, NC + 2)
        y_psum, acc_done = Signal(nc, f"{name}_y_psum", 1, NC + 2), Signal(nc, f"{name}_acc_done", 1, NC + 2)

        def load(sp, e, par):
            sp.wait_ge(y_psum.sem, y_psum.at(e * NC - NC - 1))
            sp.dma_start(w1[:, par, :], w["w1"][bass.ds(e, 1), :, :].rearrange("a p f -> (a p) f")).then_inc(weights[par].sem, 16)
            sp.dma_start(w2[:, par, :, :], w["w2"][bass.ds(e, 1), :, :].rearrange("a p f -> (a p) f")).then_inc(weights[par].sem, 16)
            if not gated:
                sp.wait_ge(h_out.sem, h_out.at(e * NC - NC - 1))
                sp.dma_start(b1[:, par, :], w["b1"][bass.ds(e, 1), :, :].rearrange("a p f -> (a p) f")).then_inc(weights[par].sem, 16)

        def ring(f, parity):
            return (parity * NF + f) % NH

        def up(pe, pair_of, job, par, parity, c):
            pe.wait_ge(weights[par].sem, weights[par].at(pair_of))
            for f in range(NF):
                pe.wait_ge(h_out.sem, h_out.at(job, f - NH))
                for j in range(1 + gated):
                    i = nc.tensor.matmul(psH[ring(f, parity)][j][:], w1[:, par, j * F + f * P:j * F + (f + 1) * P],
                                         XT[:, bass.ds(c * C, C)], start=True, stop=True)
                i.then_inc(h_psum.sem, 1)

        def down(pe, job, par, parity):
            pe.wait_ge(acc_done.sem, acc_done.at(job - 2))
            for f in range(NF):
                pe.wait_ge(h_out.sem, h_out.at(job, f))
                for t in range(TC):
                    i = nc.tensor.matmul(psY[parity][:, t, :], hT[:, parity, f, t * P:(t + 1) * P], w2[:, par, f, :],
                                         start=(f == 0 and t == 0), stop=(f == NF - 1), skip_group_check=True)
            i.then_inc(y_psum.sem, 1)

        def bend(act, pair_of, job, par, parity):
            if not gated:
                act.wait_ge(weights[par].sem, weights[par].at(pair_of))
            for f in range(NF):
                act.wait_ge(h_psum.sem, h_psum.at(job, f))
                if f == 0 and not gated:
                    act.wait_ge(y_psum.sem, y_psum.at(job - 2))
                bank = psH[ring(f, parity)]
                if gated:
                    act.wait_ge(h_out.sem, h_out.at(job, f - 2))
                    nc.scalar.activation(g_sb[:, f % 2, :], bank[0][:], func).then_inc(g_out.sem, 1)
                else:
                    nc.scalar.activation(hT[:, parity, f, :], bank[0][:], func,
                                         bias=b1[:, par, f:f + 1]).then_inc(h_out.sem, 1)

        def multiply(dve, job, parity):
            dve.wait_ge(y_psum.sem, y_psum.at(job - 2))
            for f in range(NF):
                dve.wait_ge(g_out.sem, g_out.at(job, f))
                nc.vector.tensor_tensor(hT[:, parity, f, :], g_sb[:, f % 2, :], psH[ring(f, parity)][1][:], ALU.mult).then_inc(h_out.sem, 1)

        def add(dve, job, e, c, parity):
            dve.wait_ge(y_psum.sem, y_psum.at(job))
            dve.wait_ge(acc_done.sem, acc_done.at(job - NC))
            if coef is None:
                nc.vector.tensor_tensor(acc[:, bass.ds(c * TC, TC), :], psY[parity][:], acc[:, bass.ds(c * TC, TC), :], ALU.add).then_inc(acc_done.sem, 1)
                return
            for t in range(TC):
                at = acc[:, bass.ds(c * TC + t, 1), :]
                i = nc.vector.scalar_tensor_tensor(out=at, in0=psY[parity][:, t:t + 1, :], scalar=coef[:, bass.ds(c * TC + t, 1), bass.ds(e, 1)].rearrange("p a b -> p (a b)"),
                                                   in1=at, op0=ALU.mult, op1=ALU.add)
            i.then_inc(acc_done.sem, 1)

        def run(eng, job):
            def pair(pair_of, n):
                e0 = pair_of * 2
                for par in range(n):
                    e = e0 + par
                    with eng.Fori(0, NC // 2) as c2:
                        for parity in range(2):
                            c = c2 * 2 + parity
                            job(pair_of, e * NC + c, e, c, par, parity)
            if n_experts == 1:
                pair(0, 1)
            else:
                with eng.Fori(0, n_experts // 2) as e2:
                    pair(e2, 2)

        with nc.Block() as block:
            @block.sync
            def _(sp):
                for s in weights:
                    s.open(sp)
                if n_experts == 1:
                    load(sp, 0, 0)
                else:
                    with sp.Fori(0, n_experts // 2) as e2:
                        for par in range(2):
                            load(sp, e2 * 2 + par, par)

            @block.tensor
            def _(pe):
                for s in (h_psum, y_psum):
                    s.open(pe)

                def job(pair_of, j, e, c, par, parity):
                    up(pe, pair_of, j, par, parity, c)
                    down(pe, j, par, parity)
                run(pe, job)

            @block.scalar
            def _(act):
                (g_out if gated else h_out).open(act)
                nc.scalar.preload_act_table_set(table)
                run(act, lambda pair_of, j, e, c, par, parity: bend(act, pair_of, j, par, parity))

            @block.vector
            def _(dve):
                acc_done.open(dve)
                if gated:
                    h_out.open(dve)

                def job(pair_of, j, e, c, par, parity):
                    if gated:
                        multiply(dve, j, parity)
                    add(dve, j, e, c, parity)
                run(dve, job)


def sign_mlp(nc, name, XT, acc, w):
    C = 512
    NC, TC, NF = NT * P // C, C // P, 4
    with ExitStack() as ctx:
        def sb(n, shape, dt=F32):
            return ctx.enter_context(nc.sbuf_tensor(f"{name}_{n}", shape, dt))

        k0, k1, k2 = sb("k0", [P, 2, NF * P], U8), sb("k1", [P, NF, NF * P], U8), sb("k2", [P, NF, P], U8)
        w0a, w0b = sb("w0a", [P, NF * P]), sb("w0b", [P, NF * P])
        w0, w1, w2 = sb("w0", [P, NF * P]), sb("w1", [P, NF, NF * P]), sb("w2", [P, NF, P])
        scales = sb("scales", [P, 3])
        h1, h2 = sb("h1", [P, 2, NF, C]), sb("h2", [P, 2, NF, C])
        psH = [ctx.enter_context(nc.psum_tensor(f"{name}_H{i}", [P, C], F32)) for i in range(4)]
        psY = [ctx.enter_context(nc.psum_tensor(f"{name}_Y{i}", [P, TC, P], F32)) for i in range(2)]
        loaded, made = nc.alloc_semaphore(f"{name}_loaded"), nc.alloc_semaphore(f"{name}_made")
        loads = [(k0[:], w["k0"].rearrange("(a p) f -> p a f", p=P)), (k1[:], w["k1"].rearrange("(a p) f -> p a f", p=P)),
                 (k2[:], w["k2"].rearrange("(a p) f -> p a f", p=P))] + [(scales[:, i:i + 1], w[f"s{i}"].partition_broadcast(P)) for i in range(3)]
        with nc.Block() as block:
            @block.sync
            def _(sp):
                for dst, src in loads:
                    sp.dma_start(dst, src).then_inc(loaded, 16)
                sp.wait_ge(loaded, 16 * len(loads))

            @block.vector
            def _(dve):
                dve.wait_ge(loaded, 16 * len(loads))
                nc.vector.tensor_scalar(w0a[:], k0[:, 0, :], 2.0, None, ALU.mult).then_inc(made, 1)
                nc.vector.tensor_scalar(w0b[:], k0[:, 1, :], 2.0, None, ALU.mult).then_inc(made, 1)
                nc.vector.tensor_scalar(w1[:], k1[:], 2.0, -1.0, ALU.mult, ALU.add).then_inc(made, 1)
                nc.vector.tensor_scalar(w2[:], k2[:], 2.0, -1.0, ALU.mult, ALU.add).then_inc(made, 1)
                nc.vector.tensor_scalar(scales[:, 0:2], scales[:, 0:2], 2.0, None, ALU.mult).then_inc(made, 1)
                dve.wait_ge(made, 5)
                nc.vector.tensor_tensor(w0[:], w0a[:], w0b[:], ALU.subtract).then_inc(made, 1)

        h_psum, h_out = Signal(nc, f"{name}_h_psum", 2 * NF), Signal(nc, f"{name}_h_out", 2 * NF)
        y_psum, y_out = Signal(nc, f"{name}_y_psum", 1), Signal(nc, f"{name}_y_out", 1)
        with nc.Block() as block:
            @block.tensor
            def _(pe):
                for s in (h_psum, y_psum):
                    s.open(pe)
                with pe.Fori(0, NC // 2) as c2:
                    for parity in range(2):
                        c = c2 * 2 + parity
                        for f in range(NF):
                            pe.wait_ge(h_out.sem, h_out.at(c - 1, NF + f))
                            nc.tensor.matmul(psH[f][:], w0[:, f * P:(f + 1) * P], XT[:, bass.ds(c * C, C)], start=True, stop=True).then_inc(h_psum.sem, 1)
                        for g in range(NF):
                            for f in range(NF):
                                if g == 0:
                                    pe.wait_ge(h_out.sem, h_out.at(c, f))
                                i = nc.tensor.matmul(psH[g][:], w1[:, f, g * P:(g + 1) * P], h1[:, parity, f, :], start=(f == 0), stop=(f == NF - 1))
                            i.then_inc(h_psum.sem, 1)
                        pe.wait_ge(y_out.sem, y_out.at(c - 2))
                        for g in range(NF):
                            pe.wait_ge(h_out.sem, h_out.at(c, NF + g))
                            for t in range(TC):
                                i = nc.tensor.matmul(psY[parity][:, t, :], h2[:, parity, g, t * P:(t + 1) * P], w2[:, g, :],
                                                     start=(g == 0 and t == 0), stop=(g == NF - 1), skip_group_check=True)
                        i.then_inc(y_psum.sem, 1)

            @block.scalar
            def _(act):
                h_out.open(act)
                with act.Fori(0, NC // 2) as c2:
                    for parity in range(2):
                        c = c2 * 2 + parity
                        act.wait_ge(y_psum.sem, y_psum.at(c - 2))
                        for n in range(2 * NF):
                            layer, f = divmod(n, NF)
                            act.wait_ge(h_psum.sem, h_psum.at(c, n))
                            nc.scalar.activation((h1, h2)[layer][:, parity, f, :], psH[f][:], ACT.Relu,
                                                 scale=scales[:, layer:layer + 1]).then_inc(h_out.sem, 1)

            @block.vector
            def _(dve):
                y_out.open(dve)
                with dve.Fori(0, NC // 2) as c2:
                    for parity in range(2):
                        c = c2 * 2 + parity
                        dve.wait_ge(y_psum.sem, y_psum.at(c))
                        nc.vector.tensor_scalar(acc[:, bass.ds(c * TC, TC), :], psY[parity][:], scales[:, 2:3], None, ALU.mult).then_inc(y_out.sem, 1)




STEPS = ("attn0", "ffn0", "attn1", "ffn1", "attn2", "ffn2", "attn3", "ffn3")


def program(nc, d, steps=STEPS):
    with ExitStack() as ctx:
        def sb(n, shape, dt=F32):
            return ctx.enter_context(nc.sbuf_tensor(n, shape, dt))

        x_state = sb("x_state", [P, NT, P])
        names = ("ident", "ones", "below", "mask")
        consts = {n: sb(f"{n}_sb", [P, P]) for n in names}
        identb, maskb = sb("identb", [P, P], BF16), sb("maskb", [P, P], BF16)
        loaded, cast = nc.alloc_semaphore("consts_loaded"), nc.alloc_semaphore("consts_cast")
        with nc.Block() as block:
            @block.sync
            def _(sp):
                sp.dma_start(x_state[:], d["x"].rearrange("(t p) c -> p t c", p=P)).then_inc(loaded, 16)
                for n in names:
                    sp.dma_start(consts[n][:], d[n]).then_inc(loaded, 16)
                sp.wait_ge(loaded, 16 * (1 + len(names)))

            @block.vector
            def _(dve):
                dve.wait_ge(loaded, 16 * (1 + len(names)))
                nc.vector.tensor_copy(identb[:], consts["ident"][:]).then_inc(cast, 1)
                nc.vector.tensor_copy(maskb[:], consts["mask"][:]).then_inc(cast, 1)
        consts.update(identb=identb, mask=maskb, order=d["order"], bits=d["bits"])
        parts = nc.dram_tensor("qk_parts", [P, PARTS, 2 * SEQ], BF16).ap()
        lengths = nc.dram_tensor("qk_lengths", [H, PARTS, 2 * SEQ], BF16).ap()
        scratch = dict(parts=parts, n2=lengths)
        HD = P // H

        def weights(prefix):
            return {n[len(prefix):]: a for n, a in d.items() if n.startswith(prefix)}

        def ffn(layer):
            with ExitStack() as inner:
                def big(n, shape):
                    return inner.enter_context(nc.sbuf_tensor(f"L{layer}_{n}", shape, F32))

                XT, acc = big("XT", [P, NT * P]), big("acc", [P, NT, P])
                name, w = f"L{layer}", weights(f"f{layer}_")
                turn_all(nc, name, x_state, XT, consts)
                if layer == 2:
                    sign_mlp(nc, name + "m", XT, acc, w)
                else:
                    coef = big("coef", [P, NT, E + 1])
                    kind = {0: "top1", 1: "mean2", 3: "cap2"}[layer]
                    route(nc, name + "r", kind, XT, consts, w, coef, acc, cap=CAPACITY.get(layer))
                    if layer == 0:
                        experts(nc, name + "e", XT, coef, acc, w, E, 512, ACT.Relu, table="exp_and_others")
                    elif layer == 1:
                        experts(nc, name + "e", XT, coef, acc, w, E, 512, ACT.Silu, gated=True, table="silu_and_others")
                    else:
                        experts(nc, name + "e", XT, coef, acc, w, E, 256, ACT.Gelu, table="gelu_and_others")
                        experts(nc, name + "s", XT, None, acc, weights("f3s_"), 1, 512, ACT.Gelu, table="gelu_and_others")
                finish_layer(nc, name + "f", x_state, acc)

        for step in steps:
            layer = int(step[-1])
            free = list(nc.free_semaphores)
            if step.startswith("ffn"):
                ffn(layer)
            else:
                kind, scale = [("wide", None), ("dist", -2.0), ("plain", HD ** -0.5), ("causal", HD ** -0.5)][layer]
                attention(nc, f"A{layer}", kind, x_state, consts, weights(f"a{layer}_"), scratch, scale)
            left = set(nc.free_semaphores)
            nc.clear_and_free_semaphores([s for s in free if s not in left])
            nc.all_engine_barrier()

        stored = nc.alloc_semaphore("out_stored")
        with nc.Block() as block:
            @block.sync
            def _(sp):
                sp.dma_start(d["out"].rearrange("(t p) c -> p t c", p=P), x_state[:]).then_inc(stored, 16)
                sp.wait_ge(stored, 16)


def lay_out(v):
    import numpy as np

    v = {n: np.asarray(a) for n, a in v.items()}
    HD = P // H
    f32 = np.float32

    def put(*a):
        return np.ascontiguousarray(a[0])

    def columns(b):
        return b.reshape(-1, P).T

    out = {"x": v["L0_attn_x"].reshape(NT * P, P)}
    out["ident"] = np.eye(P, dtype=f32)
    out["ones"] = np.ones((P, P), f32)
    out["below"] = np.triu(np.ones((P, P), f32), 1)
    out["mask"] = np.triu(np.full((P, P), -1e9, f32), 1)
    out["order"] = np.arange(E, 0, -1).astype(f32)
    out["bits"] = np.ascontiguousarray(np.broadcast_to((1 << np.arange(30, -1, -1)).astype(np.int32)[None, :, None], (P, 31, E)))
    sums = np.zeros((P, 2, H), f32)
    for c in range(P):
        sums[c, 0, c // HD], sums[c, 1, c // HD] = 0.25, 1.0
    out["a1_hsum"] = sums

    def wo8(m):
        z = np.zeros((P, 4, P), f32)
        for h in range(H):
            z[32 * (h % 4):32 * (h % 4) + HD, h // 4, :] = m[HD * h:HD * (h + 1)]
        return z

    q, k = v["L0_attn_Wq"].T.reshape(P, 8, P), v["L0_attn_Wk"].T.reshape(P, 8, P)
    out["a0_wqk"] = np.stack([q, k], 1)
    out["a0_bqk"] = np.stack([columns(v["L0_attn_bq"]), columns(v["L0_attn_bk"])], 1)
    out["a0_wv"], out["a0_bv"] = v["L0_attn_Wv"].T, v["L0_attn_bv"]
    out["a0_wo"] = v["L0_attn_Wo"].T.reshape(8, P, P).transpose(1, 0, 2)
    out["a0_bo"] = v["L0_attn_bo"]
    out["a0_adaptive"] = columns(np.repeat(v["L0_attn_adaptive_scale"], 64))
    out["a0_gamma"], out["a0_beta"] = v["L0_attn_gamma"], v["L0_attn_beta"]
    out["a1_wqk"] = np.stack([v["L1_attn_wq"].T, v["L1_attn_wk"].T], 1)[:, :, None, :]
    out["a1_bqk"] = np.stack([v["L1_attn_bq"], v["L1_attn_bk"]], 1)[:, :, None]
    out["a1_wv"], out["a1_bv"] = v["L1_attn_wv"].T, v["L1_attn_bv"]
    out["a1_wo"], out["a1_bo"] = wo8(v["L1_attn_wo"].T), v["L1_attn_bo"]
    g_in, g_out = v["L2_attn_w_qkv"].shape[1:]
    blocks = np.zeros((P, 3 * P), f32)
    proj = np.zeros((P, P), f32)
    for g in range(P // g_in):
        blocks[g * g_in:(g + 1) * g_in, g * g_out:(g + 1) * g_out] = v["L2_attn_w_qkv"][g]
        proj[g * g_in:(g + 1) * g_in, g * g_in:(g + 1) * g_in] = v["L2_attn_w_proj"][g]
    out["a2_wqk"] = blocks[:, 0:2 * P].reshape(P, 2, 1, P)
    out["a2_wv"], out["a2_wo"], out["a2_bo"] = blocks[:, 2 * P:], wo8(proj), v["L2_attn_b_proj"]
    w, b = v["L3_attn_w_attn"].T, v["L3_attn_b_attn"]
    out["a3_wqk"], out["a3_bqk"] = w[:, 0:2 * P].reshape(P, 2, 1, P), columns(b[0:2 * P])[:, :, None]
    out["a3_wv"], out["a3_bv"] = w[:, 2 * P:], b[2 * P:]
    out["a3_wo"], out["a3_bo"] = wo8(v["L3_attn_w_proj"].T), v["L3_attn_b_proj"]

    def down(w2):
        return w2.reshape(w2.shape[0], -1, P, P).transpose(0, 2, 1, 3).reshape(w2.shape[0], P, -1)

    def bias(b1):
        return b1.reshape(b1.shape[0], -1, P).transpose(0, 2, 1)

    out["f0_gate"] = v["L0_ffn_gate_w"].T
    out["f0_w1"], out["f0_b1"] = v["L0_ffn_w1"], bias(v["L0_ffn_b1"])
    out["f0_w2"] = down(v["L0_ffn_w2"])
    out["f0_b2"] = np.concatenate([v["L0_ffn_b2"], np.zeros((1, P), f32)], 0)
    out["f1_gate"] = v["L1_ffn_router_w"].T
    out["f1_w1"] = np.concatenate([v["L1_ffn_gate_w"].transpose(0, 2, 1), v["L1_ffn_up_w"].transpose(0, 2, 1)], 2)
    out["f1_w2"] = down(v["L1_ffn_down_w"].transpose(0, 2, 1))
    for n in ("k0", "k1", "k2"):
        out[f"f2_{n}"] = v[f"L2_ffn_{n}"]
    for n in ("s0", "s1", "s2"):
        out[f"f2_{n}"] = v[f"L2_ffn_{n}"].reshape(1)
    out["f3_gate"], out["f3_proj_b"], out["f3_expert_bias"] = v["L3_ffn_proj_w"].T, v["L3_ffn_proj_b"], v["L3_ffn_expert_bias"]
    out["f3_w1"], out["f3_b1"] = v["L3_ffn_fc1_w"].transpose(0, 2, 1), bias(v["L3_ffn_fc1_b"])
    out["f3_w2"] = down(v["L3_ffn_fc2_w"].transpose(0, 2, 1))
    out["f3_b2"] = np.concatenate([v["L3_ffn_fc2_b"], v["L3_ffn_sh2_b"][None]], 0)
    out["f3s_w1"], out["f3s_b1"] = v["L3_ffn_sh1_w"].T[None], bias(v["L3_ffn_sh1_b"][None])
    out["f3s_w2"] = down(v["L3_ffn_sh2_w"].T[None])
    return {n: np.ascontiguousarray(a) for n, a in out.items()}


def kernel(**inputs):
    import concourse.bacc as bacc
    from concourse.bass_utils import run_bass_kernel_spmd

    nc = bacc.Bacc("TRN2", target_bir_lowering=False, num_devices=1)
    arrays = lay_out(inputs)
    d = {n: nc.dram_tensor(n, a.shape, mybir.dt.from_np(a.dtype), kind="ExternalInput").ap() for n, a in arrays.items()}
    d["out"] = nc.dram_tensor("out", (NT * P, P), F32, kind="ExternalOutput").ap()
    program(nc, d)
    r = run_bass_kernel_spmd(nc, [arrays], core_ids=[0])
    return r.results[0]["out"].reshape(NB, SEQ, P)
```

```python
from contextlib import ExitStack
import concourse.bass as bass
from concourse import mybir

F32 = mybir.dt.float32
BF16 = mybir.dt.bfloat16
U8 = mybir.dt.uint8
I32 = mybir.dt.int32
ALU = mybir.AluOpType
ACT = mybir.ActivationFunctionType
AX = mybir.AxisListType
P = 128
H = 16
NB, SEQ = 16, 256
TB = SEQ // P
NT = NB * TB
PARTS = 3
EPS = 1e-5
E = 8
AHEAD = 3
CAPACITY = {0: -(-5 * NT * P // (4 * E)), 3: -(-5 * (-(-NT * P * 2 // E)) // 4)}


class Signal:

    def __init__(self, nc, name, per, ahead=AHEAD):
        self.sem, self.per, self.ahead = nc.alloc_semaphore(name), per, ahead

    def open(self, engine):
        engine.sem_inc(self.sem, self.ahead * self.per)

    def at(self, batch, k=None):
        return (batch + self.ahead) * self.per + (self.per if k is None else k + 1)


SIX = [1, 4, 7, 10, 12, 15]
PLANS = {
    "wide": dict(ring=4, lags=(0, 0, 0, 1, 3, 3, 5, 6, 8, 4), slots=(0, 1, 4), by_scalar=SIX),
    "dist": dict(ring=8, lags=(0, 1, 2, 4, 6, 6, 9, 9, 12, 1), slots=(0, 3, 9), by_scalar=[]),
    "plain": dict(ring=8, lags=(0, 0, 0, 3, 5, 5, 7, 8, 11, 2), slots=(0, 2, 8), by_scalar=SIX),
    "causal": dict(ring=8, lags=(0, 0, 0, 3, 5, 5, 7, 8, 11, 2), slots=(0, 2, 8), by_scalar=SIX),
}
BODY = 2


def attention(nc, name, kind, x_state, consts, w, scratch=None, scale=None):
    dist, causal = kind == "dist", kind == "causal"
    wide = kind == "wide"
    HD = 64 if wide else P // H
    NG = H * HD // P if wide else 4
    HG = H // NG
    CROSS = PARTS * PARTS * HD
    KR = CROSS + (2 * PARTS if dist else 0)
    plan = PLANS[kind]
    RING = plan["ring"]
    LAG_M, LAG_R, LAG_E, LAG_N, LAG_T, LAG_K, LAG_PV, LAG_O, LAG_OUT, LAG_W = plan["lags"]
    SLOT_XT, SLOT_QK, SLOT_V = plan["slots"]
    per_e = {"v": [h for h in range(H) if h not in plan["by_scalar"]], "a": plan["by_scalar"]}
    bank = [h % 2 for h in range(H)] if wide else [h % 3 for h in range(H - 1)] + [1]
    bank_last = {h: next(d for d in range(1, H) if bank[(h - d) % H] == bank[h]) for h in range(H)}
    evac_by = {h: e for e in per_e for h in per_e[e]}

    with ExitStack() as ctx:
        def sb(n, shape, dt=F32):
            return ctx.enter_context(nc.sbuf_tensor(f"{name}_{n}", shape, dt))

        def ps(n, shape, dt=F32):
            return ctx.enter_context(nc.psum_tensor(f"{name}_{n}", shape, dt))

        def sig(n, per):
            return Signal(nc, f"{name}_{n}", per)

        NQ = NG if wide else 1
        wqk, wv, wo = sb("wqk", [P, 2, NQ, P]), sb("wv", [P, NQ * P]), sb("wo", [P, NG, P])
        bqk = sb("bqk", [P, 2, NQ])
        bv, bo = sb("bv", [P, NQ * P]), sb("bo", [P, P])
        xs, xb, xT = sb("xs", [P, TB, P]), sb("xb", [P, TB, P]), sb("xT", [P, SEQ])
        if wide:
            QT, KT = sb("QT", [P, 2, NG, SEQ]), sb("KT", [P, 2, H, SEQ])
            V = sb("V", [P, 2, TB, H * HD])
            hscale, bqs = sb("hscale", [P, NG]), sb("bqs", [P, NG])
            gamma, beta = sb("gamma", [P, P]), sb("beta", [P, P])
            xbeta, z = sb("xbeta", [P, TB, P]), sb("z", [P, TB, P])
        else:
            qk, rest = sb("qk", [P, 2 * SEQ]), sb("rest", [P, 2 * SEQ])
            parts = sb("parts", [P, PARTS, 2 * SEQ], BF16)
            QS, KS = sb("QS", [P, 2, H, SEQ], BF16), sb("KS", [P, 2, H, SEQ], BF16)
            v32 = sb("v32", [P, 2, TB, H, 32])
        prob, probT = sb("prob", [P, RING, TB, SEQ]), sb("probT", [P, RING, TB, SEQ])
        nmax, rsum, rinv = sb("nmax", [P, RING, TB]), sb("rsum", [P, RING, TB]), sb("rinv", [P, RING, TB])
        OT = sb("OT", [P, NG, SEQ])
        y, stats, mv = sb("y", [P, TB, P]), sb("stats", [P, TB, 6]), sb("mv", [P, TB, 2])
        veps, rstd, mhalf = sb("veps", [P, TB]), sb("rstd", [P, TB]), sb("mhalf", [P, TB])
        if dist:
            D = sb("D", [P, RING, TB * SEQ + TB])
            sq, hsum = sb("sq", [P, 2 * SEQ]), sb("hsum", [P, 2, H])
            n2, n2r = sb("n2", [H, 2 * SEQ]), sb("n2r", [H, 2 * SEQ])
            n2p = sb("n2p", [H, PARTS, 2 * SEQ], BF16)
        psS = [ps(f"S{i}", [P, TB, SEQ]) for i in range(max(bank) + 1)]
        psT = [ps(f"T{i}", [P, TB, SEQ]) for i in range(2)]
        psO, psM = [ps(f"O{i}", [P, SEQ]) for i in range(2)], ps("M", [P, 2, SEQ])
        psY = ps("Y", [P, SEQ])[:] if wide else psM[:, 1, :]

        n_stack = 2 * PARTS * PARTS + (2 if dist else 0)
        loaded = nc.alloc_semaphore(f"{name}_loaded")
        zeroed, filled = nc.alloc_semaphore(f"{name}_zeroed"), nc.alloc_semaphore(f"{name}_filled")
        passed = nc.alloc_semaphore(f"{name}_passed")
        xb_ready = sig("xb_ready", 1 + wide)
        xs_ready, xT_psum, xT_ready = sig("xs_ready", 1), sig("xT_psum", 1), sig("xT_ready", 1)
        qk_psum, qk_ready, v_psum, v_ready = sig("qk_psum", 1), sig("qk_ready", 2), sig("v_psum", 1), sig("v_ready", 1)
        split, stored, stacked = sig("split", 4), sig("stored", 16 * (2 if dist else 1)), sig("stacked", 16 * n_stack)
        scores, maxed, expd, sums_inv, normed = sig("scores", H), sig("maxed", H), sig("expd", H * TB), sig("sums_inv", H), sig("normed", H * TB)
        turned = sig("turned", H)
        turned_out = {e: sig(f"turned_{e}", max(len(per_e[e]), 1)) for e in per_e}
        weighed, o_out = sig("weighed", H), sig("o_out", NG)
        y_psum, y_steps, rstd_ready, x_done = sig("y_psum", 1), sig("y_steps", 6), sig("rstd_ready", 1), sig("x_done", TB)
        if wide:
            vw_psum, vw_out = sig("vw_psum", 2 * TB), sig("vw_out", 2 * TB)
            qk_out = {"a": sig("qk_out_a", NG // 2), "v": sig("qk_out_v", NG // 2)}
            qkw_psum = sig("qkw_psum", NG)
            z_steps, a_scaled = sig("z_steps", 8), sig("a_scaled", 1)
            rstd2_ready = sig("rstd2_ready", 1)
        if dist:
            squared, n2_psum, n2_split, logged, rooted = sig("squared", 1), sig("n2_psum", 1), sig("n2_split", 5), sig("logged", H), sig("rooted", H)
            clamped = sig("clamped", H * TB)

        with nc.Block() as block:
            loads = [(wqk[:], w["wqk"]), (wv[:], w["wv"]), (wo[:], w["wo"]), (bo[:], w["bo"].partition_broadcast(P))]
            if "bqk" in w:
                loads += [(bqk[:], w["bqk"]), (bv[:], w["bv"].partition_broadcast(P))]
            if dist:
                loads += [(hsum[:], w["hsum"])]
            if wide:
                loads += [(hscale[:], w["adaptive"]), (gamma[:], w["gamma"].partition_broadcast(P)),
                          (beta[:], w["beta"].partition_broadcast(P))]

            @block.sync
            def _(sp):
                for dst, src in loads:
                    sp.dma_start(dst, src).then_inc(loaded, 16)
                sp.wait_ge(loaded, 16 * len(loads))

            @block.gpsimd
            def _(pool):
                nc.gpsimd.memset(KT[:] if wide else v32[:], 0.0).then_inc(zeroed, 1)
                nc.gpsimd.memset(mhalf[:], -0.5).then_inc(zeroed, 1)
                if "bqk" not in w:
                    nc.gpsimd.memset(bqk[:], 0.0).then_inc(zeroed, 1)
                    nc.gpsimd.memset(bv[:], 0.0).then_inc(zeroed, 1)

            @block.vector
            def _(dve):
                if wide:
                    dve.wait_ge(loaded, 16 * len(loads))
                    nc.vector.tensor_scalar(hscale[:], hscale[:], float(HD) ** -0.5, None, ALU.mult).then_inc(filled, 1)
                    dve.wait_ge(filled, 1)
                    nc.vector.tensor_tensor(bqs[:], bqk[:, 0, :], hscale[:], ALU.mult).then_inc(filled, 1)
                if dist:
                    nc.vector.memset(QS[:], 1.0).then_inc(filled, 1)
                    nc.vector.memset(KS[:], 1.0).then_inc(filled, 1)

        def body(b0, first, last):
            slots = H * BODY + (LAG_OUT + LAG_W if last else 0)

            def head_at(s, lag):
                s -= lag
                if s >= H * BODY or (first and s < 0):
                    return None
                bl, h = divmod(s, H)
                return b0 + bl, bl % 2, h

            def misc_at(s, slot):
                bl, j = divmod(s, H)
                if j == slot and bl < BODY and not (last and bl == BODY - 1):
                    return b0 + bl + 1, (bl + 1) % 2
                return None

            def out_at(s, lag=0):
                s -= lag + LAG_OUT
                if (s + 1) % H == 0 and s < H * BODY and not (first and s < 0):
                    bl = (s + 1) // H - 1
                    return b0 + bl, bl % 2
                return None

            return slots, head_at, misc_at, out_at

        def back(b, h, d):
            return (b, h - d) if h >= d else (b - 1, h - d + H)

        def stage_x(pool, b):
            pool.wait_ge(xT_psum.sem, xT_psum.at(b - 1))
            nc.gpsimd.tensor_copy(xs[:], x_state[:, bass.ds(b * TB, TB), :]).then_inc(xs_ready.sem, 1)

        def add_out_bias(pool, b):
            pool.wait_ge(y_steps.sem, y_steps.at(b - 1, 0))
            if wide:
                pool.wait_ge(z_steps.sem, z_steps.at(b - 1, 2))
            pool.sem_inc(passed, 1)
            nc.gpsimd.tensor_tensor(xb[:], x_state[:, bass.ds(b * TB, TB), :],
                                    bo[:].unsqueeze(1).to_broadcast([P, TB, P]), ALU.add).then_inc(xb_ready.sem, 1)
            if wide:
                nc.gpsimd.tensor_tensor(xbeta[:], x_state[:, bass.ds(b * TB, TB), :],
                                        beta[:].unsqueeze(1).to_broadcast([P, TB, P]), ALU.add).then_inc(xb_ready.sem, 1)

        def turn_x(pe, b):
            pe.wait_ge(xs_ready.sem, xs_ready.at(b, 0))
            if wide:
                pe.wait_ge(vw_out.sem, vw_out.at(b - 1))
            else:
                pe.wait_ge(v_ready.sem, v_ready.at(b - 1))
                pe.wait_ge(y_steps.sem, y_steps.at(b - 3, 0))
            for t in range(TB):
                i = nc.tensor.transpose(psM[:, 0, t * P:(t + 1) * P], xs[:, t, :], consts["ident"][:])
            i.then_inc(xT_psum.sem, 1)

        def take_xT(act, b):
            act.wait_ge(xT_psum.sem, xT_psum.at(b))
            v = vw_psum if wide else v_psum
            act.wait_ge(v.sem, v.at(b - 1))
            nc.scalar.activation(xT[:], psM[:, 0, :], ACT.Copy).then_inc(xT_ready.sem, 1)

        def project_qk(pe, b):
            pe.wait_ge(xT_ready.sem, xT_ready.at(b))
            for j in range(2):
                i = nc.tensor.matmul(psM[:, j, :], wqk[:, j, 0, :], xT[:], start=True, stop=True)
            i.then_inc(qk_psum.sem, 1)

        def take_qk(dve, b):
            dve.wait_ge(qk_psum.sem, qk_psum.at(b))
            dve.wait_ge(split.sem, split.at(b - 1))
            if dist:
                dve.wait_ge(squared.sem, squared.at(b - 1))
            nc.vector.tensor_scalar(qk[:, 0:SEQ], psM[:, 0, :], bqk[:, 0, :], scale, ALU.add, ALU.mult).then_inc(qk_ready.sem, 1)
            nc.vector.tensor_scalar(qk[:, SEQ:], psM[:, 1, :], bqk[:, 1, :], None, ALU.add).then_inc(qk_ready.sem, 1)

        def split_qk(dve, b, step):
            if step == 0:
                dve.wait_ge(qk_ready.sem, qk_ready.at(b))
                dve.wait_ge(stored.sem, stored.at(b - 1))
                nc.vector.tensor_copy(parts[:, 0, :], qk[:]).then_inc(split.sem, 1)
                return
            dve.wait_ge(split.sem, split.at(b, step - 1))
            if step == 1:
                nc.vector.tensor_tensor(rest[:], qk[:], parts[:, 0, :], ALU.subtract).then_inc(split.sem, 1)
            elif step == 2:
                nc.vector.tensor_copy(parts[:, 1, :], rest[:]).then_inc(split.sem, 1)
            else:
                nc.vector.tensor_tensor(parts[:, 2, :], rest[:], parts[:, 1, :], ALU.subtract).then_inc(split.sem, 1)

        def square_qk(pool, b):
            pool.wait_ge(qk_ready.sem, qk_ready.at(b))
            pool.wait_ge(n2_psum.sem, n2_psum.at(b - 1))
            nc.gpsimd.tensor_tensor(sq[:], qk[:], qk[:], ALU.mult).then_inc(squared.sem, 1)

        def sum_squares(pe, b):
            pe.wait_ge(squared.sem, squared.at(b))
            pe.wait_ge(qk_ready.sem, qk_ready.at(b))
            for j in range(2):
                i = nc.tensor.matmul(psM[0:H, j, :], hsum[:, j, :], sq[:, j * SEQ:(j + 1) * SEQ], start=True, stop=True)
            i.then_inc(n2_psum.sem, 1)

        def split_squares(dve, b):
            dve.wait_ge(n2_psum.sem, n2_psum.at(b))
            dve.wait_ge(stored.sem, stored.at(b - 1))
            nc.vector.tensor_copy(n2[:], psM[0:H, :, :].rearrange("p a b -> p (a b)")).then_inc(n2_split.sem, 1)
            dve.wait_ge(n2_split.sem, n2_split.at(b, 0))
            nc.vector.tensor_copy(n2p[:, 0, :], n2[:]).then_inc(n2_split.sem, 1)
            dve.wait_ge(n2_split.sem, n2_split.at(b, 1))
            nc.vector.tensor_tensor(n2r[:], n2[:], n2p[:, 0, :], ALU.subtract).then_inc(n2_split.sem, 1)
            dve.wait_ge(n2_split.sem, n2_split.at(b, 2))
            nc.vector.tensor_copy(n2p[:, 1, :], n2r[:]).then_inc(n2_split.sem, 1)
            dve.wait_ge(n2_split.sem, n2_split.at(b, 3))
            nc.vector.tensor_tensor(n2p[:, 2, :], n2r[:], n2p[:, 1, :], ALU.subtract).then_inc(n2_split.sem, 1)

        def project_v(pe, b):
            if dist:
                pe.wait_ge(n2_split.sem, n2_split.at(b, 0))
            pe.wait_ge(qk_ready.sem, qk_ready.at(b))
            for t in range(TB):
                i = nc.tensor.matmul(psM[:, 0, t * P:(t + 1) * P], xT[:, t * P:(t + 1) * P], wv[:], start=True, stop=True)
            i.then_inc(v_psum.sem, 1)

        def take_v(dve, b, par):
            dve.wait_ge(v_psum.sem, v_psum.at(b))
            dve.wait_ge(weighed.sem, weighed.at(b - 2))
            src = psM[:, 0, :].rearrange("p (t c) -> p t c", t=TB)
            for t in range(TB):
                i = nc.vector.tensor_tensor(v32[:, par, t, :, 0:HD], src[:, t, :].rearrange("p (h c) -> p h c", h=H),
                                            bv[:].rearrange("p (h c) -> p h c", h=H), ALU.add)
            i.then_inc(v_ready.sem, 1)

        def stack(sp, b, par):
            sp.wait_ge(split.sem, split.at(b))
            sp.wait_ge(stacked.sem, stacked.at(b - 1))
            sp.dma_start(scratch["parts"], parts[:]).then_inc(stored.sem, 16)
            if dist:
                sp.wait_ge(n2_split.sem, n2_split.at(b))
                sp.dma_start(scratch["n2"], n2p[:]).then_inc(stored.sem, 16)
            sp.wait_ge(stored.sem, stored.at(b))
            sp.wait_ge(scores.sem, scores.at(b - 2))
            src = scratch["parts"].rearrange("(h c) a n -> a c h n", h=H)
            for a in range(PARTS):
                for a2 in range(PARTS):
                    rows = slice((a * PARTS + a2) * HD, (a * PARTS + a2 + 1) * HD)
                    sp.dma_start(QS[rows, par, :, :], src[a, :, :, 0:SEQ]).then_inc(stacked.sem, 16)
                    sp.dma_start(KS[rows, par, :, :], src[a2, :, :, SEQ:]).then_inc(stacked.sem, 16)
            if dist:
                n2v = scratch["n2"].rearrange("h a n -> a h n")
                sp.dma_start(QS[CROSS:CROSS + PARTS, par, :, :], n2v[:, :, 0:SEQ]).then_inc(stacked.sem, 16)
                sp.dma_start(KS[CROSS + PARTS:KR, par, :, :], n2v[:, :, SEQ:]).then_inc(stacked.sem, 16)

        def project_qk_wide(pe, b, g):
            if g == 0:
                pe.wait_ge(xT_ready.sem, xT_ready.at(b))
            else:
                e = "av"[(g - 1) % 2]
                pe.wait_ge(qk_out[e].sem, qk_out[e].at(b, (g - 1) // 2))
            for j in range(2):
                i = nc.tensor.matmul(psM[:, j, :], wqk[:, j, g, :], xT[:], start=True, stop=True)
            i.then_inc(qkw_psum.sem, 1)

        def take_qk_wide(eng, e, b, par, g):
            eng.wait_ge(qkw_psum.sem, qkw_psum.at(b, g))
            if g < 2:
                eng.wait_ge(scores.sem, scores.at(b - 2))
            halves = [(slice(HD * j, HD * (j + 1)), HG * g + j) for j in range(HG)]
            if e == "a":
                nc.scalar.activation(QT[:, par, g, :], psM[:, 0, :], ACT.Identity, bias=bqs[:, g:g + 1], scale=hscale[:, g:g + 1])
                for rows, h in halves:
                    i = nc.scalar.activation(KT[rows, par, h, :], psM[rows, 1, :], ACT.Identity, bias=bqk[rows, 1, g:g + 1])
            else:
                nc.vector.tensor_scalar(QT[:, par, g, :], psM[:, 0, :], hscale[:, g:g + 1], bqs[:, g:g + 1], ALU.mult, ALU.add)
                for rows, h in halves:
                    i = nc.vector.tensor_scalar(KT[rows, par, h, :], psM[rows, 1, :], bqk[rows, 1, g:g + 1], None, ALU.add)
            i.then_inc(qk_out[e].sem, 1)

        def project_v_wide(pe, b, n):
            t, half = divmod(n, 2)
            if n == 0:
                pe.wait_ge(qk_out["v"].sem, qk_out["v"].at(b))
            else:
                pe.wait_ge(vw_out.sem, vw_out.at(b, n - 1))
            nc.tensor.matmul(psM[:].rearrange("p a b -> p (a b)"), xT[:, t * P:(t + 1) * P], wv[:, 512 * half:512 * (half + 1)],
                             start=True, stop=True).then_inc(vw_psum.sem, 1)

        def take_v_wide(dve, b, par, n):
            t, half = divmod(n, 2)
            dve.wait_ge(vw_psum.sem, vw_psum.at(b, n))
            if n == 0:
                dve.wait_ge(weighed.sem, weighed.at(b - 2))
            cols = slice(512 * half, 512 * (half + 1))
            nc.vector.tensor_tensor(V[:, par, t, cols], psM[:].rearrange("p a b -> p (a b)"), bv[:, cols], ALU.add).then_inc(vw_out.sem, 1)

        def score(pe, b, par, h):
            if h == 0 and not wide:
                pe.wait_ge(stacked.sem, stacked.at(b))
            if wide and h == 0:
                for o in qk_out.values():
                    pe.wait_ge(o.sem, o.at(b))
            pb, ph = back(b, h, bank_last[h])
            if dist:
                pe.wait_ge(clamped.sem, clamped.at(pb, ph * TB + 1))
            else:
                pe.wait_ge(expd.sem, expd.at(pb, ph * TB + 1))
            S = psS[bank[h]]
            for t in range(TB):
                m = P * (t + 1) if causal else SEQ
                if wide:
                    i = nc.tensor.matmul(S[:, t, :], QT[:, par, h // HG, t * P:(t + 1) * P], KT[:, par, h, :], start=True, stop=True)
                    continue
                i = nc.tensor.matmul(S[:, t, 0:m], QS[0:KR, par, h, t * P:(t + 1) * P], KS[0:KR, par, h, 0:m],
                                     start=True, stop=not causal)
                if causal:
                    i = nc.tensor.matmul(S[:, t, m - P:m], consts["identb"][:], consts["mask"][:], start=False, stop=True)
            i.then_inc(scores.sem, 1)

        def row_max(dve, b, h):
            dve.wait_ge(scores.sem, scores.at(b, h))
            S = psS[bank[h]]
            if dist:
                Dh = D[:, h % RING, :]
                pb, ph = back(b, h, RING)
                dve.wait_ge(expd.sem, expd.at(pb, ph * TB + 1))
                for t in range(TB):
                    nc.vector.tensor_scalar(Dh[:, t * SEQ:(t + 1) * SEQ], S[:, t, :], 1e-12, None, ALU.max, ALU.min,
                                            accum_out=Dh[:, TB * SEQ + t:TB * SEQ + t + 1]).then_inc(clamped.sem, 1)
            elif causal:
                nc.vector.tensor_reduce(nmax[:, h % RING, 0:1], S[:, 0, 0:P], AX.X, ALU.max, negate=True)
                nc.vector.tensor_reduce(nmax[:, h % RING, 1:2], S[:, 1, :], AX.X, ALU.max, negate=True).then_inc(maxed.sem, 1)
            else:
                nc.vector.tensor_reduce(nmax[:, h % RING, :], S[:], AX.X, ALU.max, negate=True).then_inc(maxed.sem, 1)

        def take_logs(act, b, h):
            act.wait_ge(clamped.sem, clamped.at(b, h * TB + 1))
            nc.scalar.activation(D[:, h % RING, :], D[:, h % RING, :], ACT.Ln).then_inc(logged.sem, 1)

        def take_roots(act, b, h):
            act.wait_ge(logged.sem, logged.at(b, h))
            nc.scalar.activation(D[:, h % RING, :], D[:, h % RING, :], ACT.Exp, scale=0.5).then_inc(rooted.sem, 1)

        def exps(act, b, h):
            r = h % RING
            if dist:
                act.wait_ge(rooted.sem, rooted.at(b, h))
            else:
                act.wait_ge(maxed.sem, maxed.at(b, h))
            pb, ph = back(b, h, RING)
            act.wait_ge(turned.sem, turned.at(pb, ph))
            act.wait_ge(sums_inv.sem, sums_inv.at(pb, ph))
            for t in range(TB):
                m = P if causal and t == 0 else SEQ
                if dist:
                    src, bias, sc = D[:, r, t * SEQ:(t + 1) * SEQ], D[:, r, TB * SEQ + t:TB * SEQ + t + 1], -1.0
                else:
                    src, bias, sc = psS[bank[h]][:, t, 0:m], nmax[:, r, t:t + 1], 1.0
                nc.scalar.activation(prob[:, r, t, 0:m], src, ACT.Exp, bias=bias, scale=sc,
                                     accum_out=rsum[:, r, t:t + 1]).then_inc(expd.sem, 1)

        def invert_sums(dve, b, h):
            dve.wait_ge(expd.sem, expd.at(b, h * TB + 1))
            pb, ph = back(b, h, RING)
            dve.wait_ge(normed.sem, normed.at(pb, ph * TB + 1))
            nc.vector.reciprocal(rinv[:, h % RING, :], rsum[:, h % RING, :]).then_inc(sums_inv.sem, 1)

        def normalise(pool, b, h):
            r = h % RING
            pool.wait_ge(sums_inv.sem, sums_inv.at(b, h))
            pool.sem_inc(passed, 1)
            for t in range(TB):
                m = P if causal and t == 0 else SEQ
                nc.gpsimd.tensor_scalar(prob[:, r, t, 0:m], prob[:, r, t, 0:m], rinv[:, r, t:t + 1], 1.0,
                                        ALU.mult, ALU.mult).then_inc(normed.sem, 1)

        def turn(pe, b, h):
            pe.wait_ge(normed.sem, normed.at(b, h * TB + 1))
            pb, ph = back(b, h, 2)
            e = evac_by[ph]
            pe.wait_ge(turned_out[e].sem, turned_out[e].at(pb, per_e[e].index(ph)))
            T = psT[h % 2]
            for t in range(TB):
                for m in range(TB):
                    if causal and m > t:
                        continue
                    i = nc.tensor.transpose(T[:, m, t * P:(t + 1) * P], prob[:, h % RING, t, m * P:(m + 1) * P], consts["ident"][:])
            i.then_inc(turned.sem, 1)

        def take_turned(eng, e, b, h):
            eng.wait_ge(turned.sem, turned.at(b, h))
            pb, ph = back(b, h, RING)
            eng.wait_ge(weighed.sem, weighed.at(pb, ph))
            if causal:
                src, dst = (z.rearrange("p a b -> p (a b)") for z in (psT[h % 2][:], probT[:, h % RING, :, :]))
                pieces = [(dst[:, 0:SEQ], src[:, 0:SEQ]), (dst[:, SEQ + P:], src[:, SEQ + P:])]
            else:
                pieces = [(probT[:, h % RING, :, :], psT[h % 2][:])]
            for dst, src in pieces:
                i = nc.scalar.activation(dst, src, ACT.Copy) if e == "a" else nc.vector.tensor_copy(dst, src)
            i.then_inc(turned_out[e].sem, 1)

        def weigh(pe, b, par, h):
            e = evac_by[h]
            pe.wait_ge(turned_out[e].sem, turned_out[e].at(b, per_e[e].index(h)))
            grp, j = divmod(h, HG)
            if h == 0:
                v = vw_out if wide else v_ready
                pe.wait_ge(v.sem, v.at(b))
            if j == 0:
                pb, pg = (b, grp - 2) if grp >= 2 else (b - 1, grp - 2 + NG)
                pe.wait_ge(o_out.sem, o_out.at(pb, pg))
            for m in range(TB):
                n0 = P * m if causal else 0
                width = P // HG
                vh = V[:, par, m, h * HD:(h + 1) * HD] if wide else v32[:, par, m, h, :]
                i = nc.tensor.matmul(psO[grp % 2][width * j:width * (j + 1), n0:], vh, probT[:, h % RING, m, n0:],
                                     start=(m == 0), stop=(m == TB - 1))
            i.then_inc(weighed.sem, 1)

        def take_o(act, b, grp):
            act.wait_ge(weighed.sem, weighed.at(b, HG * grp + HG - 1))
            act.wait_ge(y_psum.sem, y_psum.at(b - 1))
            nc.scalar.activation(OT[:, grp, :], psO[grp % 2][:], ACT.Copy).then_inc(o_out.sem, 1)

        def project_out(pe, b, staged):
            pe.wait_ge(o_out.sem, o_out.at(b))
            if not wide:
                pe.wait_ge(v_ready.sem, v_ready.at(staged))
            pe.wait_ge(y_steps.sem, y_steps.at(b - 1, 0))
            for t in range(TB):
                for grp in range(NG):
                    i = nc.tensor.matmul(psY[:, t * P:(t + 1) * P], OT[:, grp, t * P:(t + 1) * P], wo[:, grp, :],
                                         start=(grp == 0), stop=(grp == NG - 1))
            i.then_inc(y_psum.sem, 1)

        def norm_stats(dve, b):
            dve.wait_ge(y_psum.sem, y_psum.at(b))
            dve.wait_ge(xb_ready.sem, xb_ready.at(b))
            dve.wait_ge(x_done.sem, x_done.at(b - 1))
            nc.vector.tensor_tensor(y[:], psY.rearrange("p (t c) -> p t c", t=TB), xb[:], ALU.add).then_inc(y_steps.sem, 1)
            dve.wait_ge(y_steps.sem, y_steps.at(b, 0))
            for t in range(TB):
                nc.vector.bn_stats(stats[:, t, :], y[:, t, :]).then_inc(y_steps.sem, 1)
            dve.wait_ge(y_steps.sem, y_steps.at(b, 2))
            dve.sem_inc(passed, 1)
            for t in range(TB):
                nc.vector.bn_aggr(mv[:, t, :], stats[:, t, :]).then_inc(y_steps.sem, 1)
            dve.wait_ge(y_steps.sem, y_steps.at(b, 4))
            nc.vector.tensor_scalar(veps[:], mv[:, :, 1], EPS, None, ALU.add).then_inc(y_steps.sem, 1)

        def root_var(pool, b):
            pool.wait_ge(y_steps.sem, y_steps.at(b, 5))
            last = z_steps.at(b - 1, 1) if wide else x_done.at(b - 1)
            pool.wait_ge(z_steps.sem if wide else x_done.sem, last)
            nc.gpsimd.tensor_tensor(rstd[:], veps[:], mhalf[:], ALU.pow).then_inc(rstd_ready.sem, 1)

        def write_x(dve, b):
            ready = rstd2_ready if wide else rstd_ready
            dve.wait_ge(ready.sem, ready.at(b))
            for t in range(TB):
                nc.vector.tensor_scalar(x_state[:, bass.ds(b * TB + t, 1), :], y[:, t:t + 1, :], mv[:, t, 0:1], rstd[:, t:t + 1],
                                        ALU.subtract, ALU.mult).then_inc(x_done.sem, 1)

        def inner_norm(dve, b):
            dve.wait_ge(rstd_ready.sem, rstd_ready.at(b))
            for t in range(TB):
                nc.vector.tensor_scalar(z[:, t, :], y[:, t, :], mv[:, t, 0:1], rstd[:, t:t + 1],
                                        ALU.subtract, ALU.mult).then_inc(z_steps.sem, 1)
            dve.wait_ge(z_steps.sem, z_steps.at(b, 1))
            nc.vector.tensor_tensor(y[:], z[:], gamma[:].unsqueeze(1).to_broadcast([P, TB, P]), ALU.mult).then_inc(a_scaled.sem, 1)
            dve.wait_ge(a_scaled.sem, a_scaled.at(b))
            nc.vector.tensor_tensor(y[:], y[:], xbeta[:], ALU.add).then_inc(z_steps.sem, 1)
            dve.wait_ge(z_steps.sem, z_steps.at(b, 2))
            for t in range(TB):
                nc.vector.bn_stats(stats[:, t, :], y[:, t, :]).then_inc(z_steps.sem, 1)
            dve.wait_ge(z_steps.sem, z_steps.at(b, 4))
            dve.sem_inc(passed, 1)
            for t in range(TB):
                nc.vector.bn_aggr(mv[:, t, :], stats[:, t, :]).then_inc(z_steps.sem, 1)
            dve.wait_ge(z_steps.sem, z_steps.at(b, 6))
            nc.vector.tensor_scalar(veps[:], mv[:, :, 1], EPS, None, ALU.add).then_inc(z_steps.sem, 1)

        def root_var2(pool, b):
            pool.wait_ge(z_steps.sem, z_steps.at(b, 7))
            nc.gpsimd.tensor_tensor(rstd[:], veps[:], mhalf[:], ALU.pow).then_inc(rstd2_ready.sem, 1)

        def run(eng, emit):
            emit(0, True, False)
            with eng.Fori(1, NB // BODY - 1) as i:
                emit(i * BODY, False, False)
            emit(NB - BODY, False, True)

        with nc.Block() as block:
            @block.sync
            def _(sp):
                if wide:
                    return
                for s in (stored, stacked):
                    s.open(sp)
                stack(sp, 0, 0)

                def emit(b0, first, last):
                    slots, head_at, misc_at, out_at = body(b0, first, last)
                    for s in range(slots):
                        if a := misc_at(s, SLOT_QK):
                            stack(sp, *a)
                run(sp, emit)

            @block.gpsimd
            def _(pool):
                for s in [xs_ready, xb_ready, normed, rstd_ready] + ([rstd2_ready] if wide else []) + ([squared] if dist else []):
                    s.open(pool)
                stage_x(pool, 0)
                if dist:
                    square_qk(pool, 0)

                def emit(b0, first, last):
                    slots, head_at, misc_at, out_at = body(b0, first, last)
                    for s in range(slots):
                        if a := misc_at(s, SLOT_XT):
                            stage_x(pool, a[0])
                        if dist and (a := misc_at(s, SLOT_QK + 1)):
                            square_qk(pool, a[0])
                        if a := head_at(s, LAG_N):
                            normalise(pool, a[0], a[2])
                        if a := out_at(s, -2):
                            add_out_bias(pool, a[0])
                        if a := out_at(s):
                            root_var(pool, a[0])
                        if wide and (a := out_at(s, LAG_W // 2)):
                            root_var2(pool, a[0])
                run(pool, emit)

            @block.tensor
            def _(pe):
                for s in [xT_psum, qk_psum, v_psum, scores, turned, weighed, y_psum] + ([qkw_psum, vw_psum] if wide else []) + ([n2_psum] if dist else []):
                    s.open(pe)
                turn_x(pe, 0)
                if wide:
                    for g in range(NG):
                        project_qk_wide(pe, 0, g)
                    for n in range(2 * TB):
                        project_v_wide(pe, 0, n)
                else:
                    project_qk(pe, 0)
                    if dist:
                        sum_squares(pe, 0)
                    project_v(pe, 0)

                def emit(b0, first, last):
                    slots, head_at, misc_at, out_at = body(b0, first, last)
                    for s in range(slots):
                        if a := head_at(s, 0):
                            score(pe, *a)
                        if a := head_at(s, LAG_T):
                            turn(pe, a[0], a[2])
                        if a := head_at(s, LAG_PV):
                            weigh(pe, *a)
                        if a := misc_at(s, SLOT_XT):
                            turn_x(pe, a[0])
                        if wide:
                            for g in range(NG):
                                if a := misc_at(s, SLOT_QK + g):
                                    project_qk_wide(pe, a[0], g)
                            for n in range(2 * TB):
                                if a := misc_at(s, SLOT_QK + NG + n):
                                    project_v_wide(pe, a[0], n)
                        elif a := misc_at(s, SLOT_QK):
                            project_qk(pe, a[0])
                        if dist and (a := misc_at(s, SLOT_QK + 1)):
                            sum_squares(pe, a[0])
                        if not wide and (a := misc_at(s, SLOT_V)):
                            project_v(pe, a[0])
                        if a := out_at(s):
                            project_out(pe, a[0], b0 + BODY - 1 if last else a[0] + 2)
                run(pe, emit)

            @block.scalar
            def _(act):
                for s in [xT_ready, expd, o_out, turned_out["a"]] + ([logged, rooted] if dist else []) + ([qk_out["a"]] if wide else []):
                    s.open(act)
                nc.scalar.preload_act_table_set("natural_log_exp_and_others" if dist else "exp_and_others")
                take_xT(act, 0)
                if wide:
                    for g in range(0, NG, 2):
                        take_qk_wide(act, "a", 0, 0, g)

                def emit(b0, first, last):
                    slots, head_at, misc_at, out_at = body(b0, first, last)
                    for s in range(slots):
                        if dist and (a := head_at(s, LAG_M)):
                            take_logs(act, a[0], a[2])
                        if dist and (a := head_at(s, LAG_R)):
                            take_roots(act, a[0], a[2])
                        if a := head_at(s, LAG_E):
                            exps(act, a[0], a[2])
                        if a := misc_at(s, SLOT_XT):
                            take_xT(act, a[0])
                        a = head_at(s, LAG_K)
                        if a and evac_by[a[2]] == "a":
                            take_turned(act, "a", a[0], a[2])
                        a = head_at(s, LAG_O)
                        if a and a[2] % HG == HG - 1:
                            take_o(act, a[0], a[2] // HG)
                        if wide:
                            for g in range(0, NG, 2):
                                if a := misc_at(s, SLOT_QK + g):
                                    take_qk_wide(act, "a", *a, g)
                run(act, emit)

            @block.vector
            def _(dve):
                for s in [qk_ready, v_ready, split, maxed, sums_inv, turned_out["v"], y_steps, x_done] + ([n2_split, clamped] if dist else []) + ([qk_out["v"], vw_out, z_steps, a_scaled] if wide else []):
                    s.open(dve)
                if wide:
                    for g in range(1, NG, 2):
                        take_qk_wide(dve, "v", 0, 0, g)
                    for n in range(2 * TB):
                        take_v_wide(dve, 0, 0, n)
                else:
                    take_qk(dve, 0)
                    for step in range(4):
                        split_qk(dve, 0, step)
                    if dist:
                        split_squares(dve, 0)
                    take_v(dve, 0, 0)

                def emit(b0, first, last):
                    slots, head_at, misc_at, out_at = body(b0, first, last)
                    for s in range(slots):
                        if a := head_at(s, LAG_M):
                            row_max(dve, a[0], a[2])
                        if a := head_at(s, LAG_N):
                            invert_sums(dve, a[0], a[2])
                        a = head_at(s, LAG_K)
                        if a and evac_by[a[2]] == "v":
                            take_turned(dve, "v", a[0], a[2])
                        if wide:
                            for g in range(1, NG, 2):
                                if a := misc_at(s, SLOT_QK + g):
                                    take_qk_wide(dve, "v", *a, g)
                            for n in range(2 * TB):
                                if a := misc_at(s, SLOT_QK + NG + n):
                                    take_v_wide(dve, *a, n)
                        elif a := misc_at(s, SLOT_QK):
                            take_qk(dve, a[0])
                        for step in range(0 if wide else 4):
                            if a := misc_at(s, SLOT_QK + 1 + step):
                                split_qk(dve, a[0], step)
                        if dist and (a := misc_at(s, SLOT_QK + 1)):
                            split_squares(dve, a[0])
                        if not wide and (a := misc_at(s, SLOT_V + 1)):
                            take_v(dve, *a)
                        if a := out_at(s):
                            norm_stats(dve, a[0])
                        if wide and (a := out_at(s, LAG_W // 2)):
                            inner_norm(dve, a[0])
                        if a := out_at(s, LAG_W):
                            write_x(dve, a[0])
                run(dve, emit)


def turn_all(nc, name, x_state, XT, consts):
    with ExitStack() as ctx:
        banks = [ctx.enter_context(nc.psum_tensor(f"{name}_xt{i}", [P, 4, P], F32)) for i in range(4)]
        turned, out = nc.alloc_semaphore(f"{name}_turned"), [nc.alloc_semaphore(f"{name}_out{e}") for e in "va"]
        with nc.Block() as block:
            @block.tensor
            def _(pe):
                for g in range(NT // 4):
                    if g >= 4:
                        pe.wait_ge(out[g % 2], (g - 4) // 2 + 1)
                    for t in range(4):
                        i = nc.tensor.transpose(banks[g % 4][:, t, :], x_state[:, 4 * g + t, :], consts["ident"][:])
                    i.then_inc(turned, 1)

            @block.vector
            def _(dve):
                for g in range(0, NT // 4, 2):
                    dve.wait_ge(turned, g + 1)
                    nc.vector.tensor_copy(XT[:, 4 * g * P:4 * (g + 1) * P], banks[g % 4][:].rearrange("p a b -> p (a b)")).then_inc(out[0], 1)

            @block.scalar
            def _(act):
                for g in range(1, NT // 4, 2):
                    act.wait_ge(turned, g + 1)
                    nc.scalar.activation(XT[:, 4 * g * P:4 * (g + 1) * P], banks[g % 4][:].rearrange("p a b -> p (a b)"), ACT.Copy).then_inc(out[1], 1)




def finish_layer(nc, name, x_state, acc, fetch=None):
    G = 4
    with ExitStack() as ctx:
        def sb(n, shape, dt=F32):
            return ctx.enter_context(nc.sbuf_tensor(f"{name}_{n}", shape, dt))

        y, stats, mv = sb("y", [P, NT, P]), sb("stats", [P, NT, 6]), sb("mv", [P, NT, 2])
        shift = sb("shift", [P, NT])
        veps, rstd, mhalf = sb("veps", [P, NT]), sb("rstd", [P, NT]), sb("mhalf", [P, NT])
        added, stated, aggregated = (nc.alloc_semaphore(f"{name}_{n}") for n in ("added", "stated", "aggregated"))
        filled, rooted = nc.alloc_semaphore(f"{name}_filled"), nc.alloc_semaphore(f"{name}_rooted")
        var_ready, shift_ready = nc.alloc_semaphore(f"{name}_var_ready"), nc.alloc_semaphore(f"{name}_shift_ready")
        K = fetch["row"].shape[1] if fetch else 0
        rows = sb("rows", [P, K, NT, P]) if fetch else None
        fetched = [nc.alloc_semaphore(f"{name}_fetched{g}") for g in range(NT // G if fetch else 0)]
        weighted = nc.alloc_semaphore(f"{name}_weighted")
        with nc.Block() as block:
            @block.gpsimd
            def _(pool):
                def root(g):
                    s = slice(g * G, (g + 1) * G)
                    pool.wait_ge(var_ready, g + 1)
                    nc.gpsimd.tensor_tensor(rstd[:, s], veps[:, s], mhalf[:, s], ALU.pow).then_inc(rooted, 1)

                nc.gpsimd.memset(mhalf[:], -0.5).then_inc(filled, 1)
                pool.wait_ge(filled, 1)
                for g in range(NT // G):
                    for t in range(g * G, (g + 1) * G if fetch else g * G):
                        for k in range(K):
                            pool.indirect_dma_start(rows[:, k, t, :], None, fetch["results"],
                                                    bass.IndirectOffsetOnAxis(ap=fetch["row"][:, k, t:t + 1], axis=0)).then_inc(fetched[g], 16)
                    if g:
                        root(g - 1)
                root(NT // G - 1)

            @block.scalar
            def _(act):
                for g in range(NT // G):
                    act.wait_ge(shift_ready, g + 1)
                    for t in range(g * G, (g + 1) * G):
                        nc.scalar.activation(x_state[:, t, :], y[:, t, :], ACT.Identity, bias=shift[:, t:t + 1], scale=rstd[:, t:t + 1])

            @block.vector
            def _(dve):
                def write(g):
                    s = slice(g * G, (g + 1) * G)
                    dve.wait_ge(rooted, g + 1)
                    nc.vector.scalar_tensor_tensor(out=shift[:, s], in0=mv[:, s, 0], scalar=-1.0, in1=rstd[:, s], op0=ALU.mult, op1=ALU.mult).then_inc(shift_ready, 1)

                for g in range(NT // G):
                    s = slice(g * G, (g + 1) * G)
                    if fetch:
                        dve.wait_ge(fetched[g], 16 * K * G)
                    for k in range(K):
                        for t in range(g * G, (g + 1) * G):
                            nc.vector.scalar_tensor_tensor(out=acc[:, t, :], in0=rows[:, k, t, :], scalar=fetch["weight"][:, k, t:t + 1],
                                                           in1=acc[:, t, :], op0=ALU.mult, op1=ALU.add).then_inc(weighted, 1)
                        dve.wait_ge(weighted, (g * K + k + 1) * G)
                    nc.vector.tensor_tensor(y[:, s, :], x_state[:, s, :], acc[:, s, :], ALU.add).then_inc(added, 1)
                    dve.wait_ge(added, g + 1)
                    for t in range(g * G, (g + 1) * G):
                        nc.vector.bn_stats(stats[:, t, :], y[:, t, :]).then_inc(stated, 1)
                    for t in range(g * G, (g + 1) * G):
                        dve.wait_ge(stated, t + 1)
                        nc.vector.bn_aggr(mv[:, t, :], stats[:, t, :]).then_inc(aggregated, 1)
                    dve.wait_ge(aggregated, (g + 1) * G)
                    nc.vector.tensor_scalar(veps[:, s], mv[:, s, 1], EPS, None, ALU.add).then_inc(var_ready, 1)
                    if g:
                        write(g - 1)
                write(NT // G - 1)


def route(nc, name, kind, XT, consts, w, coef, acc, cap=None, places=None):
    with ExitStack() as ctx:
        def sb(n, shape, dt=F32):
            return ctx.enter_context(nc.sbuf_tensor(f"{name}_{n}", shape, dt))

        def te(n, dt=F32):
            return sb(n, [P, NT, E], dt)

        def over_e(a):
            return a[:].unsqueeze(2).to_broadcast([P, NT, E])

        def over_t(a):
            return a[:].unsqueeze(1).to_broadcast([P, NT, E])

        def flat(a):
            return a[:].rearrange("p t e -> p (t e)")

        gate = sb("gate", [P, E])
        logit, d, ex, first, val, sel1, sel2 = (te(n) for n in ("logit", "d", "ex", "first", "val", "sel1", "sel2"))
        order = sb("order", [P, E])
        top, total, inv, p1, p2 = (sb(n, [P, NT]) for n in ("top", "total", "inv", "p1", "p2"))
        psL = ctx.enter_context(nc.psum_tensor(f"{name}_L", [P, NT, E], F32))
        psR = ctx.enter_context(nc.psum_tensor(f"{name}_R", [P, NT, E], F32))
        psN = ctx.enter_context(nc.psum_tensor(f"{name}_N", [P, NT, E], F32))
        psC = [ctx.enter_context(nc.psum_tensor(f"{name}_C{i}", [E + 1, 4, P], F32)) for i in range(2)]
        psB = [ctx.enter_context(nc.psum_tensor(f"{name}_B{i}", [P, 4, P], F32)) for i in range(2)]
        coefT, b2 = sb("coefT", [E + 1, NT, P]), sb("b2", [E + 1, P])
        loads = [(gate[:], w["gate"]), (order[:], consts["order"].partition_broadcast(P))]
        if kind != "mean2":
            loads += [(b2[:], w["b2"])]
        if kind == "top1":
            token = sb("token", [P, NT])
            loads += [(token[:], consts["token"])]
        if kind == "cap2":
            pb, eb = sb("pb", [P, E]), sb("eb", [P, E])
            bits = sb("bits", [P, 31, E], I32)
            loads += [(pb[:], w["proj_b"].partition_broadcast(P)), (eb[:], w["expert_bias"].partition_broadcast(P)),
                      (bits[:], consts["bits"])]
        loaded, logits = nc.alloc_semaphore(f"{name}_loaded"), nc.alloc_semaphore(f"{name}_logits")
        chain, exps = nc.alloc_semaphore(f"{name}_chain"), nc.alloc_semaphore(f"{name}_exps")
        counted = nc.alloc_semaphore(f"{name}_counted")
        coefT_psum, coefT_out = nc.alloc_semaphore(f"{name}_coefT_psum"), nc.alloc_semaphore(f"{name}_coefT_out")
        b2_psum, b2_out = nc.alloc_semaphore(f"{name}_b2_psum"), nc.alloc_semaphore(f"{name}_b2_out")

        with nc.Block() as block:
            @block.sync
            def _(sp):
                for dst, src in loads:
                    sp.dma_start(dst, src).then_inc(loaded, 16)
                sp.wait_ge(loaded, 16 * len(loads))

            @block.tensor
            def _(pe):
                pe.wait_ge(loaded, 16 * len(loads))
                for t in range(NT):
                    i = nc.tensor.matmul(psL[:, t, :], XT[:, t * P:(t + 1) * P], gate[:], start=True, stop=True)
                i.then_inc(logits, 1)

            @block.scalar
            def _(act):
                act.wait_ge(chain, 3)
                nc.scalar.activation(flat(ex), flat(d), ACT.Exp, scale=-1.0 if kind == "cap2" else 1.0).then_inc(exps, 1)

            @block.vector
            def _(dve):
                n = [0]

                def link(i):
                    n[0] += 1
                    i.then_inc(chain, 1)
                    dve.wait_ge(chain, n[0])

                def pick(sel, of):
                    link(nc.vector.tensor_reduce(top[:], of[:], AX.X, ALU.max))
                    link(nc.vector.tensor_tensor(first[:], of[:], over_e(top), ALU.is_equal))
                    link(nc.vector.tensor_tensor(val[:], first[:], over_t(order), ALU.mult))
                    link(nc.vector.tensor_reduce(total[:], val[:], AX.X, ALU.max))
                    link(nc.vector.tensor_tensor(sel[:], val[:], over_e(total), ALU.is_equal))

                dve.wait_ge(loaded, 16 * len(loads))
                dve.wait_ge(logits, 1)
                if kind == "cap2":
                    link(nc.vector.tensor_copy(logit[:], psL[:]))
                    link(nc.vector.tensor_tensor(d[:], logit[:], over_t(pb), ALU.add))
                    link(nc.vector.tensor_copy(logit[:], d[:]))
                    dve.wait_ge(exps, 1)
                    link(nc.vector.tensor_scalar(ex[:], ex[:], 1.0, None, ALU.add))
                    link(nc.vector.reciprocal(d[:], ex[:]))
                    link(nc.vector.tensor_tensor(ex[:], d[:], over_t(eb), ALU.add))
                    link(nc.vector.tensor_scalar(ex[:], ex[:], 1e-12, None, ALU.max))
                else:
                    link(nc.vector.tensor_copy(logit[:], psL[:]))
                    link(nc.vector.tensor_reduce(top[:], logit[:], AX.X, ALU.max))
                    link(nc.vector.tensor_tensor(d[:], logit[:], over_e(top), ALU.subtract))
                    dve.wait_ge(exps, 1)
                link(nc.vector.tensor_reduce(total[:], ex[:], AX.X, ALU.add))
                link(nc.vector.reciprocal(inv[:], total[:]))
                link(nc.vector.tensor_tensor(ex[:], ex[:], over_e(inv), ALU.mult))
                pick(sel1, logit if kind != "cap2" else ex)
                if kind == "top1":
                    link(nc.vector.tensor_tensor(coef[:, :, 0:E], ex[:], sel1[:], ALU.mult))
                else:
                    link(nc.vector.tensor_tensor(d[:], ex[:], sel1[:], ALU.subtract))
                    link(nc.vector.tensor_scalar(val[:], sel1[:], -2.0, None, ALU.mult))
                    link(nc.vector.tensor_tensor(d[:], d[:], val[:], ALU.add))
                    pick(sel2, d)
                    link(nc.vector.tensor_tensor(sel1[:], sel1[:], sel2[:], ALU.add))
                    link(nc.vector.tensor_tensor(d[:], ex[:], sel1[:], ALU.mult))
                    link(nc.vector.tensor_reduce(p1[:], d[:], AX.X, ALU.add))
                    link(nc.vector.tensor_scalar(p1[:], p1[:], 1e-12, None, ALU.max))
                    link(nc.vector.reciprocal(inv[:], p1[:]))
                    link(nc.vector.tensor_tensor(val[:], d[:], over_e(inv), ALU.mult))

        if kind == "mean2":
            cnt, wsum, mean, tiles, ends = (sb(n, [P, E]) for n in ("cnt", "wsum", "mean", "tiles", "ends"))
            numbers = sb("numbers", [P, P])
            more, past = sb("more", [P, E, NT]), sb("past", [P, ROUTED_TILES, E])
            tile_of = sb("tile_of", [P, ROUTED_TILES])
            numbered = nc.alloc_semaphore(f"{name}_numbered")
            with nc.Block() as block:
                @block.sync
                def _(sp):
                    sp.dma_start(numbers[:], consts["numbers"].partition_broadcast(P)).then_inc(numbered, 16)

                @block.tensor
                def _(pe):
                    nc.tensor.matmul(flat(psR), consts["ones"][:], flat(sel1), start=True, stop=True).then_inc(counted, 1)
                    nc.tensor.matmul(flat(psN), consts["ones"][:], flat(val), start=True, stop=True).then_inc(counted, 1)
                    nc.tensor.matmul(flat(psL), consts["below"][:], flat(sel1), start=True, stop=True).then_inc(counted, 1)

                @block.vector
                def _(dve):
                    chain2, n = nc.alloc_semaphore(f"{name}_chain2"), [0]

                    def link(i):
                        n[0] += 1
                        i.then_inc(chain2, 1)
                        dve.wait_ge(chain2, n[0])

                    nc.vector.memset(acc[:], 0.0)
                    dve.wait_ge(counted, 3)
                    link(nc.vector.tensor_reduce(cnt[:], psR[:].rearrange("p t e -> p e t"), AX.X, ALU.add))
                    link(nc.vector.tensor_reduce(wsum[:], psN[:].rearrange("p t e -> p e t"), AX.X, ALU.add))
                    dve.wait_ge(numbered, 16)
                    link(nc.vector.tensor_scalar(tile_of[:, 0:NT], numbers[:, 0:NT], float(P), None, ALU.mult))
                    link(nc.vector.tensor_tensor(more[:], cnt[:].unsqueeze(2).to_broadcast([P, E, NT]),
                                                 tile_of[:, 0:NT].unsqueeze(1).to_broadcast([P, E, NT]), ALU.is_gt))
                    link(nc.vector.tensor_reduce(tiles[:], more[:], AX.X, ALU.add))
                    link(nc.vector.tensor_tensor_scan(ends[:], consts["ones"][:, 0:E], tiles[:], 0.0, ALU.mult, ALU.add))
                    link(nc.vector.tensor_tensor(past[:], numbers[:, 0:ROUTED_TILES].unsqueeze(2).to_broadcast([P, ROUTED_TILES, E]),
                                                 ends[:].unsqueeze(1).to_broadcast([P, ROUTED_TILES, E]), ALU.is_ge))
                    link(nc.vector.tensor_reduce(tile_of[:], past[:], AX.X, ALU.add))
                    link(nc.vector.tensor_scalar(places["expert"][:], tile_of[:], float(E - 1), None, ALU.min))
                    link(nc.vector.tensor_tensor(ends[:], ends[:], tiles[:], ALU.subtract))
                    link(nc.vector.tensor_scalar(ends[:], ends[:], float(P), None, ALU.mult))
                    link(nc.vector.tensor_copy(d[:], psR[:]))
                    for e in range(E):
                        link(nc.vector.tensor_tensor_scan(first[:, :, e], consts["ones"][:, 0:NT], d[:, :, e], 0.0, ALU.mult, ALU.add))
                    link(nc.vector.tensor_tensor(first[:], first[:], d[:], ALU.subtract))
                    link(nc.vector.tensor_tensor(first[:], first[:], psL[:], ALU.add))
                    link(nc.vector.tensor_tensor(first[:], first[:], over_t(ends), ALU.add))
                    link(nc.vector.tensor_scalar(cnt[:], cnt[:], 1.0, None, ALU.max))
                    link(nc.vector.reciprocal(mean[:], cnt[:]))
                    link(nc.vector.tensor_tensor(mean[:], mean[:], wsum[:], ALU.mult))
                    link(nc.vector.tensor_tensor(sel1[:], sel1[:], sel2[:], ALU.subtract))
                    for k, sel in enumerate((sel1, sel2)):
                        link(nc.vector.tensor_tensor(d[:], first[:], sel[:], ALU.mult))
                        link(nc.vector.tensor_reduce(top[:], d[:], AX.X, ALU.add))
                        link(nc.vector.tensor_copy(places["row"][:, k, :], top[:]))
                        link(nc.vector.tensor_tensor(d[:], sel[:], over_t(mean), ALU.mult))
                        link(nc.vector.tensor_reduce(places["weight"][:, k, :], d[:], AX.X, ALU.add))
            return

        if kind == "cap2":
            cand, thr = sb("cand", [P, E], I32), sb("thr", [P, E], I32)
            step, own, cnt, need = sb("step", [P, E], I32), sb("own", [P, E]), sb("cnt", [P, E]), sb("need", [P, E])
            reach = te("reach")
            reached, tallied = nc.alloc_semaphore(f"{name}_reached"), nc.alloc_semaphore(f"{name}_tallied")
            bis = nc.alloc_semaphore(f"{name}_bisect")
            PER = 4
            with nc.Block() as block:
                @block.tensor
                def _(pe):
                    with pe.Fori(0, 31) as i:
                        pe.wait_ge(reached, i + 1)
                        nc.tensor.matmul(psN[:, 0, :], consts["ones"][:], own[:], start=True, stop=True).then_inc(tallied, 1)

                @block.vector
                def _(dve):
                    nc.vector.memset(thr[:], 0).then_inc(bis, 1)
                    dve.wait_ge(bis, 1)
                    with dve.Fori(0, 31) as i:
                        nc.vector.tensor_tensor(cand[:], thr[:], bits[:, bass.ds(i, 1), :].rearrange("p a e -> p (a e)"), ALU.bitwise_or).then_inc(bis, 1)
                        dve.wait_ge(bis, i * PER + 2)
                        nc.vector.tensor_tensor(reach[:], val[:], over_t(cand.bitcast(F32)), ALU.is_ge).then_inc(bis, 1)
                        dve.wait_ge(bis, i * PER + 3)
                        nc.vector.tensor_reduce(own[:], reach[:].rearrange("p t e -> p e t"), AX.X, ALU.add).then_inc(reached, 1)
                        dve.wait_ge(tallied, i + 1)
                        nc.vector.scalar_tensor_tensor(out=step[:], in0=psN[:, 0, :], scalar=float(cap), in1=bits[:, bass.ds(i, 1), :].rearrange("p a e -> p (a e)"),
                                                       op0=ALU.is_ge, op1=ALU.mult).then_inc(bis, 1)
                        dve.wait_ge(bis, i * PER + 4)
                        nc.vector.tensor_tensor(thr[:], thr[:], step[:], ALU.bitwise_or).then_inc(bis, 1)
                        dve.wait_ge(bis, i * PER + 5)

            tallied2 = nc.alloc_semaphore(f"{name}_tallied2")
            above, chain3 = te("above"), nc.alloc_semaphore(f"{name}_chain3")
            with nc.Block() as block:
                @block.tensor
                def _(pe):
                    pe.wait_ge(chain3, 2)
                    nc.tensor.matmul(flat(psL), consts["ones"][:], flat(above), start=True, stop=True).then_inc(tallied2, 1)
                    nc.tensor.matmul(flat(psR), consts["below"][:], flat(reach), start=True, stop=True).then_inc(tallied2, 1)
                    nc.tensor.matmul(flat(psN), consts["ones"][:], flat(reach), start=True, stop=True).then_inc(tallied2, 1)

                @block.vector
                def _(dve):
                    n = [0]

                    def link(i):
                        n[0] += 1
                        i.then_inc(chain3, 1)
                        dve.wait_ge(chain3, n[0])

                    link(nc.vector.tensor_tensor(above[:], val[:], over_t(thr.bitcast(F32)), ALU.is_gt))
                    link(nc.vector.tensor_tensor(reach[:], val[:], over_t(thr.bitcast(F32)), ALU.is_equal))
                    dve.wait_ge(tallied2, 3)
                    link(nc.vector.tensor_reduce(cnt[:], psL[:].rearrange("p t e -> p e t"), AX.X, ALU.add))
                    link(nc.vector.tensor_scalar(need[:], cnt[:], -1.0, float(cap), ALU.mult, ALU.add))
                    link(nc.vector.tensor_copy(d[:], psN[:]))
                    for e in range(E):
                        link(nc.vector.tensor_tensor_scan(first[:, :, e], consts["ones"][:, 0:NT], d[:, :, e], 0.0, ALU.mult, ALU.add))
                    link(nc.vector.tensor_tensor(first[:], first[:], d[:], ALU.subtract))
                    link(nc.vector.tensor_tensor(first[:], first[:], psR[:], ALU.add))
                    link(nc.vector.tensor_tensor(first[:], first[:], over_t(need), ALU.is_lt))
                    link(nc.vector.tensor_tensor(reach[:], first[:], reach[:], ALU.mult))
                    link(nc.vector.tensor_tensor(above[:], above[:], reach[:], ALU.add))
                    link(nc.vector.tensor_tensor(coef[:, :, 0:E], above[:], val[:], ALU.mult))
                    link(nc.vector.memset(coef[:, :, E:E + 1], 1.0))
        else:
            chain4, counted4 = nc.alloc_semaphore(f"{name}_chain4"), nc.alloc_semaphore(f"{name}_counted4")
            with nc.Block() as block:
                @block.tensor
                def _(pe):
                    nc.tensor.matmul(flat(psR), consts["below"][:], flat(sel1), start=True, stop=True).then_inc(counted4, 1)
                    nc.tensor.matmul(flat(psN), consts["ones"][:], flat(sel1), start=True, stop=True).then_inc(counted4, 1)

                @block.vector
                def _(dve):
                    n = [0]

                    def link(i):
                        n[0] += 1
                        i.then_inc(chain4, 1)
                        dve.wait_ge(chain4, n[0])

                    dve.wait_ge(counted4, 2)
                    link(nc.vector.tensor_copy(d[:], psN[:]))
                    for e in range(E):
                        link(nc.vector.tensor_tensor_scan(first[:, :, e], consts["ones"][:, 0:NT], d[:, :, e], 0.0, ALU.mult, ALU.add))
                    link(nc.vector.tensor_tensor(first[:], first[:], d[:], ALU.subtract))
                    link(nc.vector.tensor_tensor(first[:], first[:], psR[:], ALU.add))
                    link(nc.vector.tensor_scalar(d[:], over_t(order), -float(cap), float(cap * E), ALU.mult, ALU.add))
                    link(nc.vector.tensor_tensor(d[:], d[:], first[:], ALU.add))
                    link(nc.vector.tensor_tensor(d[:], d[:], sel1[:], ALU.mult))
                    link(nc.vector.tensor_reduce(top[:], d[:], AX.X, ALU.add))
                    link(nc.vector.tensor_scalar(first[:], first[:], float(cap), None, ALU.is_lt))
                    link(nc.vector.tensor_tensor(d[:], sel1[:], first[:], ALU.mult))
                    link(nc.vector.tensor_reduce(inv[:], d[:], AX.X, ALU.add))
                    link(nc.vector.tensor_scalar(top[:], top[:], -float(cap * E), None, ALU.add))
                    link(nc.vector.tensor_tensor(total[:], top[:], inv[:], ALU.mult))
                    link(nc.vector.tensor_scalar(places["row"][:, 0, :], total[:], float(cap * E), None, ALU.add))
                    link(nc.vector.tensor_scalar(p1[:], inv[:], -1.0, 1.0, ALU.mult, ALU.add))
                    link(nc.vector.tensor_tensor(p1[:], p1[:], token[:], ALU.mult))
                    link(nc.vector.tensor_tensor(p1[:], p1[:], total[:], ALU.add))
                    link(nc.vector.tensor_scalar(places["send"][:], p1[:], float(cap * E), None, ALU.add))
                    link(nc.vector.tensor_tensor(coef[:, :, 0:E], coef[:, :, 0:E], first[:], ALU.mult))
                    link(nc.vector.tensor_reduce(places["weight"][:, 0, :], coef[:, :, 0:E], AX.X, ALU.add))
                    link(nc.vector.memset(coef[:, :, E:E + 1], 1.0))

        with nc.Block() as block:
            @block.tensor
            def _(pe):
                def turn(g):
                    if g >= 2:
                        pe.wait_ge(coefT_out, g - 1)
                    for t in range(4):
                        i = nc.tensor.transpose(psC[g % 2][:, t, :], coef[:, 4 * g + t, :], consts["ident"][:])
                    i.then_inc(coefT_psum, 1)

                turn(0)
                for g in range(NT // 4):
                    if g + 1 < NT // 4:
                        turn(g + 1)
                    pe.wait_ge(coefT_out, g + 1)
                    if g >= 2:
                        pe.wait_ge(b2_out, g - 1)
                    for t in range(4):
                        i = nc.tensor.matmul(psB[g % 2][:, t, :], coefT[:, 4 * g + t, :], b2[:], start=True, stop=True)
                    i.then_inc(b2_psum, 1)

            @block.scalar
            def _(act):
                for g in range(NT // 4):
                    act.wait_ge(coefT_psum, g + 1)
                    nc.scalar.activation(coefT[:, 4 * g:4 * g + 4, :], psC[g % 2][:], ACT.Copy).then_inc(coefT_out, 1)

            @block.vector
            def _(dve):
                for g in range(NT // 4):
                    dve.wait_ge(b2_psum, g + 1)
                    nc.vector.tensor_copy(acc[:, 4 * g:4 * g + 4, :], psB[g % 2][:]).then_inc(b2_out, 1)


ROUTED_TILES = 2 * NT + E


def routed_experts(nc, name, x_state, ident, places, w, table):
    F = w["w1"].shape[2] // 2
    NF, PAIRS = F // P, ROUTED_TILES // 2
    CLEAR = 8
    with ExitStack() as ctx:
        def sb(n, shape, dt=F32):
            return ctx.enter_context(nc.sbuf_tensor(f"{name}_{n}", shape, dt))

        def ps(n, shape):
            return ctx.enter_context(nc.psum_tensor(f"{name}_{n}", shape, F32))

        def sig(n, per):
            return Signal(nc, f"{name}_{n}", per)

        sent, results = (nc.dram_tensor(f"{name}_{n}", [ROUTED_TILES * P, P], F32).ap() for n in ("sent", "results"))
        by_pair = [a.rearrange("(q k p) c -> q p k c", k=2, p=P) for a in (sent, results)]
        zeros, w13, w2 = sb("zeros", [P, CLEAR, P]), sb("w13", [P, E, 2 * F]), sb("w2", [P, E, NF, P])
        xe, xT, ye = sb("xe", [P, 2, 2, P]), sb("xT", [P, 2, 2 * P]), sb("ye", [P, 2, 2, P])
        g, h, hT = sb("g", [P, 2, F]), sb("h", [P, 2, F]), sb("hT", [P, 2, 2, NF, P])
        psX, psY = ps("X", [P, 2, P]), ps("Y", [P, 2, P])
        psG, psU, psT = ([ps(f"{n}{k}", [P, F]) for k in range(2)] for n in "GUT")

        zeroed, cleared, sent_all, loaded = (nc.alloc_semaphore(f"{name}_{n}") for n in ("zeroed", "cleared", "sent_all", "loaded"))
        x_loaded, stored = [sig(f"x_loaded{i}", 16) for i in range(2)], [sig(f"stored{i}", 16) for i in range(2)]
        x_psum, xT_out, gu_psum, silu_out, h_out = sig("x_psum", 1), sig("xT_out", 1), sig("gu_psum", 2), sig("silu_out", 2), sig("h_out", 2)
        t_psum, hT_out, y_psum, y_out = sig("t_psum", 2), sig("hT_out", 2), sig("y_psum", 1), sig("y_out", 1)

        def load_x(sp, q, par):
            sp.wait_ge(x_psum.sem, x_psum.at(q - 2))
            sp.dma_start(xe[:, par, :, :], by_pair[0][bass.ds(q, 1), :, :, :].rearrange("a p k c -> (a p) k c")).then_inc(x_loaded[par].sem, 16)

        def store_y(sp, q, par):
            sp.wait_ge(y_out.sem, y_out.at(q))
            sp.dma_start(by_pair[1][bass.ds(q, 1), :, :, :].rearrange("a p k c -> (a p) k c"), ye[:, par, :, :]).then_inc(stored[par].sem, 16)

        def run(eng, job):
            job(0, 0, 0, True, False)
            job(1, 0, 1, False, False)
            with eng.Fori(1, PAIRS // 2 - 1) as q2:
                for par in range(2):
                    job(q2 * 2 + par, q2, par, False, False)
            job(PAIRS - 2, PAIRS // 2 - 1, 0, False, False)
            job(PAIRS - 1, PAIRS // 2 - 1, 1, False, True)

        def loop_of(q2, par, shift):
            return (par + shift) % 2, q2 + (par + shift) // 2

        with nc.Block() as block:
            @block.sync
            def _(sp):
                for s in x_loaded + stored:
                    s.open(sp)
                sp.wait_ge(zeroed, 1)
                for n in range(ROUTED_TILES // CLEAR):
                    sp.dma_start(sent[n * CLEAR * P:(n + 1) * CLEAR * P, :].rearrange("(p j) c -> p j c", p=P), zeros[:]).then_inc(cleared, 16)
                for e in range(E):
                    sp.dma_start(w13[:, e, :], w["w1"][e]).then_inc(loaded, 16)
                    sp.dma_start(w2[:, e, :, :], w["w2"][e]).then_inc(loaded, 16)
                sp.wait_ge(sent_all, 16 * 2 * NT)
                for par in range(2):
                    load_x(sp, par, par)
                with sp.Fori(0, PAIRS // 2 - 1) as q2:
                    for par in range(2):
                        q = q2 * 2 + par
                        load_x(sp, q + 2, par)
                        store_y(sp, q, par)
                for par in range(2):
                    store_y(sp, PAIRS - 2 + par, par)

            @block.gpsimd
            def _(pool):
                nc.gpsimd.memset(zeros[:], 0.0).then_inc(zeroed, 1)
                pool.wait_ge(cleared, 16 * (ROUTED_TILES // CLEAR))
                for t in range(NT):
                    for k in range(2):
                        pool.indirect_dma_start(sent, bass.IndirectOffsetOnAxis(ap=places["row"][:, k, t:t + 1], axis=0),
                                                x_state[:, t, :], None).then_inc(sent_all, 16)
                for s in stored:
                    pool.wait_ge(s.sem, s.at(PAIRS // 2 - 1))

            @block.tensor
            def _(pe):
                for s in (x_psum, gu_psum, t_psum, y_psum):
                    s.open(pe)
                pe.wait_ge(loaded, 16 * 2 * E)

                def turn_x(q, q2, par):
                    pe.wait_ge(x_loaded[par].sem, x_loaded[par].at(q2))
                    pe.wait_ge(xT_out.sem, xT_out.at(q - 1))
                    for k in range(2):
                        i = nc.tensor.transpose(psX[:, k, :], xe[:, par, k, :], ident[:])
                    i.then_inc(x_psum.sem, 1)

                def experts_of(q):
                    return [pe.value_load(places["expert"][0:1, bass.ds(q * 2 + k, 1)], min_val=0, max_val=E - 1) for k in range(2)]

                def down(q, par):
                    expert = experts_of(q)
                    pe.wait_ge(y_out.sem, y_out.at(q - 1))
                    pe.wait_ge(hT_out.sem, hT_out.at(q))
                    for k in range(2):
                        for f in range(NF):
                            i = nc.tensor.matmul(psY[:, k, :], hT[:, par, k, f, :], w2[:, bass.ds(expert[k], 1), f, :].rearrange("p a c -> p (a c)"),
                                                 start=(f == 0 and k == 0), stop=(f == NF - 1), skip_group_check=True)
                    i.then_inc(y_psum.sem, 1)

                def job(q, q2, par, first, last):
                    expert = experts_of(q)
                    if first:
                        turn_x(q, q2, par)
                    pe.wait_ge(xT_out.sem, xT_out.at(q))
                    for k in range(2):
                        pe.wait_ge(h_out.sem, h_out.at(q - 1, k))
                        for n, bank in enumerate((psG[k], psU[k])):
                            i = nc.tensor.matmul(bank[:], xT[:, par, k * P:(k + 1) * P],
                                                 w13[:, bass.ds(expert[k], 1), n * F:(n + 1) * F].rearrange("p a f -> p (a f)"), start=True, stop=True)
                        i.then_inc(gu_psum.sem, 1)
                    if not first:
                        down(q - 1, 1 - par)
                    if not last:
                        after_par, after_q2 = loop_of(q2, par, 1)
                        turn_x(q + 1, after_q2, after_par)
                    for k in range(2):
                        pe.wait_ge(h_out.sem, h_out.at(q, k))
                        pe.wait_ge(hT_out.sem, hT_out.at(q - 1, k))
                        for f in range(NF):
                            i = nc.tensor.transpose(psT[k][:, f * P:(f + 1) * P], h[:, k, f * P:(f + 1) * P], ident[:])
                        i.then_inc(t_psum.sem, 1)
                    if last:
                        down(q, par)
                run(pe, job)

            @block.scalar
            def _(act):
                for s in (silu_out, hT_out):
                    s.open(act)
                nc.scalar.preload_act_table_set(table)

                def job(q, q2, par, first, last):
                    for k in range(2):
                        act.wait_ge(gu_psum.sem, gu_psum.at(q, k))
                        act.wait_ge(h_out.sem, h_out.at(q - 1, k))
                        nc.scalar.activation(g[:, k, :], psG[k][:], ACT.Silu).then_inc(silu_out.sem, 1)
                    for k in range(2):
                        act.wait_ge(t_psum.sem, t_psum.at(q, k))
                        act.wait_ge(y_psum.sem, y_psum.at(q - 2))
                        nc.scalar.activation(hT[:, par, k, :, :].rearrange("p f c -> p (f c)"), psT[k][:], ACT.Copy).then_inc(hT_out.sem, 1)
                run(act, job)

            @block.vector
            def _(dve):
                for s in (xT_out, h_out, y_out):
                    s.open(dve)

                def take_xT(q, par):
                    dve.wait_ge(x_psum.sem, x_psum.at(q))
                    dve.wait_ge(gu_psum.sem, gu_psum.at(q - 2))
                    nc.vector.tensor_copy(xT[:, par, :], psX[:].rearrange("p a b -> p (a b)")).then_inc(xT_out.sem, 1)

                def take_y(q, q2, par):
                    dve.wait_ge(y_psum.sem, y_psum.at(q))
                    dve.wait_ge(stored[par].sem, stored[par].at(q2 - 1))
                    nc.vector.tensor_copy(ye[:, par, :, :], psY[:]).then_inc(y_out.sem, 1)

                def job(q, q2, par, first, last):
                    if first:
                        take_xT(q, par)
                    for k in range(2):
                        dve.wait_ge(silu_out.sem, silu_out.at(q, k))
                        dve.wait_ge(t_psum.sem, t_psum.at(q - 1, k))
                        nc.vector.tensor_tensor(h[:, k, :], g[:, k, :], psU[k][:], ALU.mult).then_inc(h_out.sem, 1)
                    if not first:
                        before_par, before_q2 = loop_of(q2, par, -1)
                        take_y(q - 1, before_q2, before_par)
                    if not last:
                        take_xT(q + 1, 1 - par)
                    if last:
                        take_y(q, q2, par)
                run(dve, job)
    return results


def capped_experts(nc, name, x_state, ident, places, w, cap, func, table):
    J, F = cap // P, w["w1"].shape[2]
    NF = F // P
    cuts = [(0, -(-J // 2)), (-(-J // 2), J)]
    with ExitStack() as ctx:
        def sb(n, shape, dt=F32):
            return ctx.enter_context(nc.sbuf_tensor(f"{name}_{n}", shape, dt))

        def sig(n, per):
            return Signal(nc, f"{name}_{n}", per)

        sent = nc.dram_tensor(f"{name}_sent", [E * cap + NT * P, P], F32).ap()
        results = nc.dram_tensor(f"{name}_results", [E * cap + 1, P], F32).ap()
        by_expert = [a[0:E * cap, :].rearrange("(e j p) c -> e p j c", j=J, p=P) for a in (sent, results)]
        zeros = sb("zeros", [P, E * J, P])
        xe, ye, xT = sb("xe", [P, 2, J, P]), sb("ye", [P, 2, J, P]), sb("xT", [P, 2, J * P])
        w1, w2, b1 = sb("w1", [P, 2, F]), sb("w2", [P, 2, NF, P]), sb("b1", [P, 2, NF])
        hT = sb("hT", [P, 2, NF, cuts[0][1] * P])
        psX = [ctx.enter_context(nc.psum_tensor(f"{name}_X{i}", [P, 4, P], F32)) for i in range(2)]
        psH = [ctx.enter_context(nc.psum_tensor(f"{name}_H{i}", [P, 4 * P], F32)) for i in range(NF)]
        psY = [ctx.enter_context(nc.psum_tensor(f"{name}_Y{i}", [P, 4, P], F32)) for i in range(2)]

        zeroed, cleared, sent_all = (nc.alloc_semaphore(f"{name}_{n}") for n in ("zeroed", "cleared", "sent_all"))
        weights = [sig(f"weights{i}", 48) for i in range(2)]
        x_loaded, stored = [sig(f"x_loaded{i}", 16) for i in range(2)], [sig(f"stored{i}", 16) for i in range(2)]
        x_psum, xT_out = sig("x_psum", 2), sig("xT_out", 2)
        h_psum, h_out = sig("h_psum", 2 * NF), sig("h_out", 2 * NF)
        y_psum, y_out = sig("y_psum", 2), sig("y_out", 2)

        def load_weights(sp, e, par):
            sp.wait_ge(y_psum.sem, y_psum.at(e - 2))
            sp.wait_ge(h_out.sem, h_out.at(e - 2))
            for dst, src in ((w1[:, par, :], w["w1"]), (w2[:, par, :, :], w["w2"])):
                sp.dma_start(dst, src[bass.ds(e, 1), :, :].rearrange("a p f -> (a p) f")).then_inc(weights[par].sem, 16)
            sp.dma_start(b1[:, par, :], w["b1"][bass.ds(e, 1), :, :].rearrange("a p f -> (a p) f")).then_inc(weights[par].sem, 16)

        def load_x(sp, e, par):
            sp.wait_ge(x_psum.sem, x_psum.at(e - 2))
            sp.dma_start(xe[:, par, :, :], by_expert[0][bass.ds(e, 1), :, :, :].rearrange("a p j c -> (a p) j c")).then_inc(x_loaded[par].sem, 16)

        def store_y(sp, e, par):
            sp.wait_ge(y_out.sem, y_out.at(e))
            sp.dma_start(by_expert[1][bass.ds(e, 1), :, :, :].rearrange("a p j c -> (a p) j c"), ye[:, par, :, :]).then_inc(stored[par].sem, 16)

        def run(eng, job):
            with eng.Fori(0, E // 2) as e2:
                for par in range(2):
                    job(e2 * 2 + par, e2, par)

        with nc.Block() as block:
            @block.sync
            def _(sp):
                for s in weights + x_loaded + stored:
                    s.open(sp)
                sp.wait_ge(zeroed, 1)
                sp.dma_start(sent[0:E * cap, :].rearrange("(p j) c -> p j c", p=P), zeros[:]).then_inc(cleared, 16)
                sp.dma_start(results[E * cap:, :], zeros[0:1, 0, :]).then_inc(cleared, 16)
                for par in range(2):
                    load_weights(sp, par, par)
                sp.wait_ge(sent_all, 16 * NT)
                for par in range(2):
                    load_x(sp, par, par)
                with sp.Fori(0, E // 2 - 1) as e2:
                    for par in range(2):
                        e = e2 * 2 + par
                        store_y(sp, e, par)
                        load_weights(sp, e + 2, par)
                        load_x(sp, e + 2, par)
                for par in range(2):
                    store_y(sp, E - 2 + par, par)

            @block.gpsimd
            def _(pool):
                nc.gpsimd.memset(zeros[:], 0.0).then_inc(zeroed, 1)
                pool.wait_ge(cleared, 32)
                for t in range(NT):
                    pool.indirect_dma_start(sent, bass.IndirectOffsetOnAxis(ap=places["send"][:, t:t + 1], axis=0),
                                            x_state[:, t, :], None).then_inc(sent_all, 16)
                for s in stored:
                    pool.wait_ge(s.sem, s.at(E // 2 - 1))

            @block.tensor
            def _(pe):
                for s in (x_psum, h_psum, y_psum):
                    s.open(pe)

                def job(e, pair_of, par):
                    pe.wait_ge(x_loaded[par].sem, x_loaded[par].at(pair_of))
                    for c, (j0, j1) in enumerate(cuts):
                        pe.wait_ge(xT_out.sem, xT_out.at(e - 1, c))
                        for j in range(j0, j1):
                            i = nc.tensor.transpose(psX[c][:, j - j0, :], xe[:, par, j, :], ident[:])
                        i.then_inc(x_psum.sem, 1)
                    pe.wait_ge(weights[par].sem, weights[par].at(pair_of))
                    for c, (j0, j1) in enumerate(cuts):
                        pe.wait_ge(xT_out.sem, xT_out.at(e, c))
                        for f in range(NF):
                            before = h_out.at(e, f) if c else h_out.at(e - 1, NF + f)
                            pe.wait_ge(h_out.sem, before)
                            nc.tensor.matmul(psH[f][:, 0:(j1 - j0) * P], w1[:, par, f * P:(f + 1) * P], xT[:, par, j0 * P:j1 * P],
                                             start=True, stop=True).then_inc(h_psum.sem, 1)
                    for c, (j0, j1) in enumerate(cuts):
                        pe.wait_ge(y_out.sem, y_out.at(e - 1, c))
                        for f in range(NF):
                            pe.wait_ge(h_out.sem, h_out.at(e, c * NF + f))
                            for j in range(j1 - j0):
                                i = nc.tensor.matmul(psY[c][:, j, :], hT[:, c, f, j * P:(j + 1) * P], w2[:, par, f, :],
                                                     start=(f == 0 and j == 0), stop=(f == NF - 1), skip_group_check=True)
                        i.then_inc(y_psum.sem, 1)
                run(pe, job)

            @block.scalar
            def _(act):
                h_out.open(act)
                nc.scalar.preload_act_table_set(table)

                def job(e, pair_of, par):
                    act.wait_ge(weights[par].sem, weights[par].at(pair_of))
                    for c, (j0, j1) in enumerate(cuts):
                        act.wait_ge(y_psum.sem, y_psum.at(e - 1, c))
                        for f in range(NF):
                            act.wait_ge(h_psum.sem, h_psum.at(e, c * NF + f))
                            nc.scalar.activation(hT[:, c, f, 0:(j1 - j0) * P], psH[f][:, 0:(j1 - j0) * P], func,
                                                 bias=b1[:, par, f:f + 1]).then_inc(h_out.sem, 1)
                run(act, job)

            @block.vector
            def _(dve):
                for s in (xT_out, y_out):
                    s.open(dve)

                def job(e, pair_of, par):
                    for c, (j0, j1) in enumerate(cuts):
                        dve.wait_ge(x_psum.sem, x_psum.at(e, c))
                        dve.wait_ge(h_psum.sem, h_psum.at(e - 2))
                        nc.vector.tensor_copy(xT[:, par, j0 * P:j1 * P], psX[c][:, 0:j1 - j0, :].rearrange("p a b -> p (a b)")).then_inc(xT_out.sem, 1)
                    for c, (j0, j1) in enumerate(cuts):
                        dve.wait_ge(y_psum.sem, y_psum.at(e, c))
                        dve.wait_ge(stored[par].sem, stored[par].at(pair_of - 1))
                        nc.vector.tensor_copy(ye[:, par, j0:j1, :], psY[c][:, 0:j1 - j0, :]).then_inc(y_out.sem, 1)
                run(dve, job)
    return results


def dense_experts(nc, name, XT, coef, acc, w, n_experts, F, func, table):
    C = 512
    NC, TC, NF = NT * P // C, C // P, F // P
    with ExitStack() as ctx:
        def sb(n, shape, dt=F32):
            return ctx.enter_context(nc.sbuf_tensor(f"{name}_{n}", shape, dt))

        w1, w2 = sb("w1", [P, 2, F]), sb("w2", [P, 2, NF, P])
        hT = sb("hT", [P, 2, NF, C])
        b1 = sb("b1", [P, 2, NF])
        NH = 4
        psH = [ctx.enter_context(nc.psum_tensor(f"{name}_H{i}", [P, C], F32)) for i in range(NH)]
        psY = [ctx.enter_context(nc.psum_tensor(f"{name}_Y{i}", [P, TC, P], F32)) for i in range(2)]

        weights = [Signal(nc, f"{name}_weights{i}", 48) for i in range(2)]
        h_psum = Signal(nc, f"{name}_h_psum", NF)
        h_out = Signal(nc, f"{name}_h_out", NF, NC + 2)
        y_psum, acc_done = Signal(nc, f"{name}_y_psum", 1, NC + 2), Signal(nc, f"{name}_acc_done", 1, NC + 2)

        def load(sp, e, par):
            sp.wait_ge(y_psum.sem, y_psum.at(e * NC - NC - 1))
            sp.dma_start(w1[:, par, :], w["w1"][bass.ds(e, 1), :, :].rearrange("a p f -> (a p) f")).then_inc(weights[par].sem, 16)
            sp.dma_start(w2[:, par, :, :], w["w2"][bass.ds(e, 1), :, :].rearrange("a p f -> (a p) f")).then_inc(weights[par].sem, 16)
            sp.wait_ge(h_out.sem, h_out.at(e * NC - NC - 1))
            sp.dma_start(b1[:, par, :], w["b1"][bass.ds(e, 1), :, :].rearrange("a p f -> (a p) f")).then_inc(weights[par].sem, 16)

        def ring(f, parity):
            return (parity * NF + f) % NH

        def up(pe, pair_of, job, par, parity, c):
            pe.wait_ge(weights[par].sem, weights[par].at(pair_of))
            for f in range(NF):
                pe.wait_ge(h_out.sem, h_out.at(job, f - NH))
                nc.tensor.matmul(psH[ring(f, parity)][:], w1[:, par, f * P:(f + 1) * P],
                                 XT[:, bass.ds(c * C, C)], start=True, stop=True).then_inc(h_psum.sem, 1)

        def down(pe, job, par, parity):
            pe.wait_ge(acc_done.sem, acc_done.at(job - 2))
            for f in range(NF):
                pe.wait_ge(h_out.sem, h_out.at(job, f))
                for t in range(TC):
                    i = nc.tensor.matmul(psY[parity][:, t, :], hT[:, parity, f, t * P:(t + 1) * P], w2[:, par, f, :],
                                         start=(f == 0 and t == 0), stop=(f == NF - 1), skip_group_check=True)
            i.then_inc(y_psum.sem, 1)

        def bend(act, pair_of, job, par, parity):
            act.wait_ge(weights[par].sem, weights[par].at(pair_of))
            for f in range(NF):
                act.wait_ge(h_psum.sem, h_psum.at(job, f))
                if f == 0:
                    act.wait_ge(y_psum.sem, y_psum.at(job - 2))
                nc.scalar.activation(hT[:, parity, f, :], psH[ring(f, parity)][:], func,
                                     bias=b1[:, par, f:f + 1]).then_inc(h_out.sem, 1)

        def add(dve, job, e, c, parity):
            dve.wait_ge(y_psum.sem, y_psum.at(job))
            dve.wait_ge(acc_done.sem, acc_done.at(job - NC))
            if coef is None:
                nc.vector.tensor_tensor(acc[:, bass.ds(c * TC, TC), :], psY[parity][:], acc[:, bass.ds(c * TC, TC), :], ALU.add).then_inc(acc_done.sem, 1)
                return
            for t in range(TC):
                at = acc[:, bass.ds(c * TC + t, 1), :]
                i = nc.vector.scalar_tensor_tensor(out=at, in0=psY[parity][:, t:t + 1, :], scalar=coef[:, bass.ds(c * TC + t, 1), bass.ds(e, 1)].rearrange("p a b -> p (a b)"),
                                                   in1=at, op0=ALU.mult, op1=ALU.add)
            i.then_inc(acc_done.sem, 1)

        def run(eng, job):
            def pair(pair_of, n):
                e0 = pair_of * 2
                for par in range(n):
                    e = e0 + par
                    with eng.Fori(0, NC // 2) as c2:
                        for parity in range(2):
                            c = c2 * 2 + parity
                            job(pair_of, e * NC + c, e, c, par, parity)
            if n_experts == 1:
                pair(0, 1)
            else:
                with eng.Fori(0, n_experts // 2) as e2:
                    pair(e2, 2)

        with nc.Block() as block:
            @block.sync
            def _(sp):
                for s in weights:
                    s.open(sp)
                if n_experts == 1:
                    load(sp, 0, 0)
                else:
                    with sp.Fori(0, n_experts // 2) as e2:
                        for par in range(2):
                            load(sp, e2 * 2 + par, par)

            @block.tensor
            def _(pe):
                for s in (h_psum, y_psum):
                    s.open(pe)

                def job(pair_of, j, e, c, par, parity):
                    up(pe, pair_of, j, par, parity, c)
                    down(pe, j, par, parity)
                run(pe, job)

            @block.scalar
            def _(act):
                h_out.open(act)
                nc.scalar.preload_act_table_set(table)
                run(act, lambda pair_of, j, e, c, par, parity: bend(act, pair_of, j, par, parity))

            @block.vector
            def _(dve):
                acc_done.open(dve)
                run(dve, lambda pair_of, j, e, c, par, parity: add(dve, j, e, c, parity))


def sign_mlp(nc, name, XT, acc, w):
    C = 512
    NC, TC, NF = NT * P // C, C // P, 4
    with ExitStack() as ctx:
        def sb(n, shape, dt=F32):
            return ctx.enter_context(nc.sbuf_tensor(f"{name}_{n}", shape, dt))

        k0, k1, k2 = sb("k0", [P, 2, NF * P], U8), sb("k1", [P, NF, NF * P], U8), sb("k2", [P, NF, P], U8)
        w0a, w0b = sb("w0a", [P, NF * P]), sb("w0b", [P, NF * P])
        w0, w1, w2 = sb("w0", [P, NF * P]), sb("w1", [P, NF, NF * P]), sb("w2", [P, NF, P])
        scales = sb("scales", [P, 3])
        h1, h2 = sb("h1", [P, 2, NF, C]), sb("h2", [P, 2, NF, C])
        psH = [ctx.enter_context(nc.psum_tensor(f"{name}_H{i}", [P, C], F32)) for i in range(4)]
        psY = [ctx.enter_context(nc.psum_tensor(f"{name}_Y{i}", [P, TC, P], F32)) for i in range(2)]
        loaded, made = nc.alloc_semaphore(f"{name}_loaded"), nc.alloc_semaphore(f"{name}_made")
        loads = [(k0[:], w["k0"].rearrange("(a p) f -> p a f", p=P)), (k1[:], w["k1"].rearrange("(a p) f -> p a f", p=P)),
                 (k2[:], w["k2"].rearrange("(a p) f -> p a f", p=P))] + [(scales[:, i:i + 1], w[f"s{i}"].partition_broadcast(P)) for i in range(3)]
        with nc.Block() as block:
            @block.sync
            def _(sp):
                for dst, src in loads:
                    sp.dma_start(dst, src).then_inc(loaded, 16)
                sp.wait_ge(loaded, 16 * len(loads))

            @block.vector
            def _(dve):
                dve.wait_ge(loaded, 16 * len(loads))
                nc.vector.tensor_scalar(w0a[:], k0[:, 0, :], 2.0, None, ALU.mult).then_inc(made, 1)
                nc.vector.tensor_scalar(w0b[:], k0[:, 1, :], 2.0, None, ALU.mult).then_inc(made, 1)
                nc.vector.tensor_scalar(w1[:], k1[:], 2.0, -1.0, ALU.mult, ALU.add).then_inc(made, 1)
                nc.vector.tensor_scalar(w2[:], k2[:], 2.0, -1.0, ALU.mult, ALU.add).then_inc(made, 1)
                nc.vector.tensor_scalar(scales[:, 0:2], scales[:, 0:2], 2.0, None, ALU.mult).then_inc(made, 1)
                dve.wait_ge(made, 5)
                nc.vector.tensor_tensor(w0[:], w0a[:], w0b[:], ALU.subtract).then_inc(made, 1)

        h_psum, h_out = Signal(nc, f"{name}_h_psum", 2 * NF), Signal(nc, f"{name}_h_out", 2 * NF)
        y_psum, y_out = Signal(nc, f"{name}_y_psum", 1), Signal(nc, f"{name}_y_out", 1)
        with nc.Block() as block:
            @block.tensor
            def _(pe):
                for s in (h_psum, y_psum):
                    s.open(pe)
                with pe.Fori(0, NC // 2) as c2:
                    for parity in range(2):
                        c = c2 * 2 + parity
                        for f in range(NF):
                            pe.wait_ge(h_out.sem, h_out.at(c - 1, NF + f))
                            nc.tensor.matmul(psH[f][:], w0[:, f * P:(f + 1) * P], XT[:, bass.ds(c * C, C)], start=True, stop=True).then_inc(h_psum.sem, 1)
                        for g in range(NF):
                            for f in range(NF):
                                if g == 0:
                                    pe.wait_ge(h_out.sem, h_out.at(c, f))
                                i = nc.tensor.matmul(psH[g][:], w1[:, f, g * P:(g + 1) * P], h1[:, parity, f, :], start=(f == 0), stop=(f == NF - 1))
                            i.then_inc(h_psum.sem, 1)
                        pe.wait_ge(y_out.sem, y_out.at(c - 2))
                        for g in range(NF):
                            pe.wait_ge(h_out.sem, h_out.at(c, NF + g))
                            for t in range(TC):
                                i = nc.tensor.matmul(psY[parity][:, t, :], h2[:, parity, g, t * P:(t + 1) * P], w2[:, g, :],
                                                     start=(g == 0 and t == 0), stop=(g == NF - 1), skip_group_check=True)
                        i.then_inc(y_psum.sem, 1)

            @block.scalar
            def _(act):
                h_out.open(act)
                with act.Fori(0, NC // 2) as c2:
                    for parity in range(2):
                        c = c2 * 2 + parity
                        act.wait_ge(y_psum.sem, y_psum.at(c - 2))
                        for n in range(2 * NF):
                            layer, f = divmod(n, NF)
                            act.wait_ge(h_psum.sem, h_psum.at(c, n))
                            nc.scalar.activation((h1, h2)[layer][:, parity, f, :], psH[f][:], ACT.Relu,
                                                 scale=scales[:, layer:layer + 1]).then_inc(h_out.sem, 1)

            @block.vector
            def _(dve):
                y_out.open(dve)
                with dve.Fori(0, NC // 2) as c2:
                    for parity in range(2):
                        c = c2 * 2 + parity
                        dve.wait_ge(y_psum.sem, y_psum.at(c))
                        nc.vector.tensor_scalar(acc[:, bass.ds(c * TC, TC), :], psY[parity][:], scales[:, 2:3], None, ALU.mult).then_inc(y_out.sem, 1)




STEPS = ("attn0", "ffn0", "attn1", "ffn1", "attn2", "ffn2", "attn3", "ffn3")


def program(nc, d, steps=STEPS):
    with ExitStack() as ctx:
        def sb(n, shape, dt=F32):
            return ctx.enter_context(nc.sbuf_tensor(n, shape, dt))

        x_state = sb("x_state", [P, NT, P])
        names = ("ident", "ones", "below", "mask")
        consts = {n: sb(f"{n}_sb", [P, P]) for n in names}
        identb, maskb = sb("identb", [P, P], BF16), sb("maskb", [P, P], BF16)
        loaded, cast = nc.alloc_semaphore("consts_loaded"), nc.alloc_semaphore("consts_cast")
        with nc.Block() as block:
            @block.sync
            def _(sp):
                sp.dma_start(x_state[:], d["x"].rearrange("(t p) c -> p t c", p=P)).then_inc(loaded, 16)
                for n in names:
                    sp.dma_start(consts[n][:], d[n]).then_inc(loaded, 16)
                sp.wait_ge(loaded, 16 * (1 + len(names)))

            @block.vector
            def _(dve):
                dve.wait_ge(loaded, 16 * (1 + len(names)))
                nc.vector.tensor_copy(identb[:], consts["ident"][:]).then_inc(cast, 1)
                nc.vector.tensor_copy(maskb[:], consts["mask"][:]).then_inc(cast, 1)
        consts.update(identb=identb, mask=maskb, order=d["order"], bits=d["bits"], token=d["token"], numbers=d["numbers"])
        parts = nc.dram_tensor("qk_parts", [P, PARTS, 2 * SEQ], BF16).ap()
        lengths = nc.dram_tensor("qk_lengths", [H, PARTS, 2 * SEQ], BF16).ap()
        scratch = dict(parts=parts, n2=lengths)
        HD = P // H

        def weights(prefix):
            return {n[len(prefix):]: a for n, a in d.items() if n.startswith(prefix)}

        def ffn(layer):
            with ExitStack() as inner:
                def big(n, shape, dt=F32):
                    return inner.enter_context(nc.sbuf_tensor(f"L{layer}_{n}", shape, dt))

                XT, acc = big("XT", [P, NT * P]), big("acc", [P, NT, P])
                name, w = f"L{layer}", weights(f"f{layer}_")
                turn_all(nc, name, x_state, XT, consts)
                if layer == 2:
                    sign_mlp(nc, name + "m", XT, acc, w)
                else:
                    coef = big("coef", [P, NT, E + 1])
                    kind = {0: "top1", 1: "mean2", 3: "cap2"}[layer]
                    if layer == 0:
                        places = dict(weight=big("weight", [P, 1, NT]), send=big("send", [P, NT], I32), row=big("row", [P, 1, NT], I32))
                    elif layer == 1:
                        places = dict(weight=big("weight", [P, 2, NT]), row=big("row", [P, 2, NT], I32), expert=big("expert", [P, ROUTED_TILES], I32))
                    else:
                        places = None
                    route(nc, name + "r", kind, XT, consts, w, coef, acc, cap=CAPACITY.get(layer), places=places)
                    if layer == 0:
                        results = capped_experts(nc, name + "e", x_state, consts["ident"], places, w, CAPACITY[0], ACT.Relu, "exp_and_others")
                    elif layer == 1:
                        results = routed_experts(nc, name + "e", x_state, consts["ident"], places, w, "silu_and_others")
                    else:
                        dense_experts(nc, name + "e", XT, coef, acc, w, E, 256, ACT.Gelu, "gelu_and_others")
                        dense_experts(nc, name + "s", XT, None, acc, weights("f3s_"), 1, 512, ACT.Gelu, "gelu_and_others")
                fetch = dict(results=results, row=places["row"], weight=places["weight"]) if layer in (0, 1) else None
                finish_layer(nc, name + "f", x_state, acc, fetch)

        for step in steps:
            layer = int(step[-1])
            free = list(nc.free_semaphores)
            if step.startswith("ffn"):
                ffn(layer)
            else:
                kind, scale = [("wide", None), ("dist", -2.0), ("plain", HD ** -0.5), ("causal", HD ** -0.5)][layer]
                attention(nc, f"A{layer}", kind, x_state, consts, weights(f"a{layer}_"), scratch, scale)
            left = set(nc.free_semaphores)
            nc.clear_and_free_semaphores([s for s in free if s not in left])
            nc.all_engine_barrier()

        stored = nc.alloc_semaphore("out_stored")
        with nc.Block() as block:
            @block.sync
            def _(sp):
                sp.dma_start(d["out"].rearrange("(t p) c -> p t c", p=P), x_state[:]).then_inc(stored, 16)
                sp.wait_ge(stored, 16)


def lay_out(v):
    import numpy as np

    v = {n: np.asarray(a) for n, a in v.items()}
    HD = P // H
    f32 = np.float32

    def put(*a):
        return np.ascontiguousarray(a[0])

    def columns(b):
        return b.reshape(-1, P).T

    out = {"x": v["L0_attn_x"].reshape(NT * P, P)}
    out["ident"] = np.eye(P, dtype=f32)
    out["ones"] = np.ones((P, P), f32)
    out["below"] = np.triu(np.ones((P, P), f32), 1)
    out["mask"] = np.triu(np.full((P, P), -1e9, f32), 1)
    out["order"] = np.arange(E, 0, -1).astype(f32)
    out["bits"] = np.ascontiguousarray(np.broadcast_to((1 << np.arange(30, -1, -1)).astype(np.int32)[None, :, None], (P, 31, E)))
    out["numbers"] = np.arange(P).astype(f32)
    out["token"] = np.arange(NT * P).reshape(NT, P).T.astype(f32)
    sums = np.zeros((P, 2, H), f32)
    for c in range(P):
        sums[c, 0, c // HD], sums[c, 1, c // HD] = 0.25, 1.0
    out["a1_hsum"] = sums

    def wo8(m):
        z = np.zeros((P, 4, P), f32)
        for h in range(H):
            z[32 * (h % 4):32 * (h % 4) + HD, h // 4, :] = m[HD * h:HD * (h + 1)]
        return z

    q, k = v["L0_attn_Wq"].T.reshape(P, 8, P), v["L0_attn_Wk"].T.reshape(P, 8, P)
    out["a0_wqk"] = np.stack([q, k], 1)
    out["a0_bqk"] = np.stack([columns(v["L0_attn_bq"]), columns(v["L0_attn_bk"])], 1)
    out["a0_wv"], out["a0_bv"] = v["L0_attn_Wv"].T, v["L0_attn_bv"]
    out["a0_wo"] = v["L0_attn_Wo"].T.reshape(8, P, P).transpose(1, 0, 2)
    out["a0_bo"] = v["L0_attn_bo"]
    out["a0_adaptive"] = columns(np.repeat(v["L0_attn_adaptive_scale"], 64))
    out["a0_gamma"], out["a0_beta"] = v["L0_attn_gamma"], v["L0_attn_beta"]
    out["a1_wqk"] = np.stack([v["L1_attn_wq"].T, v["L1_attn_wk"].T], 1)[:, :, None, :]
    out["a1_bqk"] = np.stack([v["L1_attn_bq"], v["L1_attn_bk"]], 1)[:, :, None]
    out["a1_wv"], out["a1_bv"] = v["L1_attn_wv"].T, v["L1_attn_bv"]
    out["a1_wo"], out["a1_bo"] = wo8(v["L1_attn_wo"].T), v["L1_attn_bo"]
    g_in, g_out = v["L2_attn_w_qkv"].shape[1:]
    blocks = np.zeros((P, 3 * P), f32)
    proj = np.zeros((P, P), f32)
    for g in range(P // g_in):
        blocks[g * g_in:(g + 1) * g_in, g * g_out:(g + 1) * g_out] = v["L2_attn_w_qkv"][g]
        proj[g * g_in:(g + 1) * g_in, g * g_in:(g + 1) * g_in] = v["L2_attn_w_proj"][g]
    out["a2_wqk"] = blocks[:, 0:2 * P].reshape(P, 2, 1, P)
    out["a2_wv"], out["a2_wo"], out["a2_bo"] = blocks[:, 2 * P:], wo8(proj), v["L2_attn_b_proj"]
    w, b = v["L3_attn_w_attn"].T, v["L3_attn_b_attn"]
    out["a3_wqk"], out["a3_bqk"] = w[:, 0:2 * P].reshape(P, 2, 1, P), columns(b[0:2 * P])[:, :, None]
    out["a3_wv"], out["a3_bv"] = w[:, 2 * P:], b[2 * P:]
    out["a3_wo"], out["a3_bo"] = wo8(v["L3_attn_w_proj"].T), v["L3_attn_b_proj"]

    def down(w2):
        return w2.reshape(w2.shape[0], -1, P, P).transpose(0, 2, 1, 3).reshape(w2.shape[0], P, -1)

    def bias(b1):
        return b1.reshape(b1.shape[0], -1, P).transpose(0, 2, 1)

    out["f0_gate"] = v["L0_ffn_gate_w"].T
    out["f0_w1"], out["f0_b1"] = v["L0_ffn_w1"], bias(v["L0_ffn_b1"])
    out["f0_w2"] = down(v["L0_ffn_w2"])
    out["f0_b2"] = np.concatenate([v["L0_ffn_b2"], np.zeros((1, P), f32)], 0)
    out["f1_gate"] = v["L1_ffn_router_w"].T
    out["f1_w1"] = np.concatenate([v["L1_ffn_gate_w"].transpose(0, 2, 1), v["L1_ffn_up_w"].transpose(0, 2, 1)], 2)
    out["f1_w2"] = down(v["L1_ffn_down_w"].transpose(0, 2, 1))
    for n in ("k0", "k1", "k2"):
        out[f"f2_{n}"] = v[f"L2_ffn_{n}"]
    for n in ("s0", "s1", "s2"):
        out[f"f2_{n}"] = v[f"L2_ffn_{n}"].reshape(1)
    out["f3_gate"], out["f3_proj_b"], out["f3_expert_bias"] = v["L3_ffn_proj_w"].T, v["L3_ffn_proj_b"], v["L3_ffn_expert_bias"]
    out["f3_w1"], out["f3_b1"] = v["L3_ffn_fc1_w"].transpose(0, 2, 1), bias(v["L3_ffn_fc1_b"])
    out["f3_w2"] = down(v["L3_ffn_fc2_w"].transpose(0, 2, 1))
    out["f3_b2"] = np.concatenate([v["L3_ffn_fc2_b"], v["L3_ffn_sh2_b"][None]], 0)
    out["f3s_w1"], out["f3s_b1"] = v["L3_ffn_sh1_w"].T[None], bias(v["L3_ffn_sh1_b"][None])
    out["f3s_w2"] = down(v["L3_ffn_sh2_w"].T[None])
    return {n: np.ascontiguousarray(a) for n, a in out.items()}


def kernel(**inputs):
    import concourse.bacc as bacc
    from concourse.bass_utils import run_bass_kernel_spmd

    nc = bacc.Bacc("TRN2", target_bir_lowering=False, num_devices=1)
    arrays = lay_out(inputs)
    d = {n: nc.dram_tensor(n, a.shape, mybir.dt.from_np(a.dtype), kind="ExternalInput").ap() for n, a in arrays.items()}
    d["out"] = nc.dram_tensor("out", (NT * P, P), F32, kind="ExternalOutput").ap()
    program(nc, d)
    r = run_bass_kernel_spmd(nc, [arrays], core_ids=[0])
    return r.results[0]["out"].reshape(NB, SEQ, P)
```
